# Optimizing a Trainium2 kernel written in Bass

```python
import numpy as np
import jax
import jax.numpy as jnp

def _softmax(x, axis=-1):
    return jax.nn.softmax(x, axis=axis)

def _gelu(x):
    return jax.nn.gelu(x, approximate=True)

def _silu(x):
    return jax.nn.silu(x)

def _sigmoid(x):
    return jax.nn.sigmoid(x)

def _layernorm(x, axis=-1, eps=1e-05):
    m = jnp.mean(x, axis=axis, keepdims=True)
    v = jnp.var(x, axis=axis, keepdims=True)
    return (x - m) / jnp.sqrt(v + eps)

def _scatter_add(tgt, idx, src, axis=0):
    return tgt.at[idx].add(src)

def _segment_sum(src, seg, n):
    return jax.ops.segment_sum(src, seg, n)
kernel_name = 'mk_flamingo_gated_d1_seqx_r8_5f47f2'

def setup_inputs(seed: int=0):
    np.random.seed(seed)
    _w = jnp.asarray

    def _rec_inputs():
        import jax
        import jax.numpy as jnp
        _rk = jax.random.key(seed)
        x = 7.22e-05 + 1 * jax.random.normal(jax.random.fold_in(_rk, 1), (16, 128, 256), jnp.float32)
        _lenS = 128 - jax.random.randint(jax.random.fold_in(_rk, 7), (16,), 0, max(1, 128 // 4) + 1, jnp.int32)
        _lenS2 = 128 - jax.random.randint(jax.random.fold_in(_rk, 8), (16,), 0, max(1, 128 // 4) + 1, jnp.int32)
        _ctx_1024P = jax.random.normal(jax.random.fold_in(_rk, 11), (16, 16, 128), jnp.float32)
        _ctx_1024c = jax.random.dirichlet(jax.random.fold_in(_rk, 511), 0.3 * jnp.ones((16,), jnp.float32), (16, 128))
        _ctx_1024t = jnp.einsum('bsk,bkd->bsd', _ctx_1024c, _ctx_1024P)
        _ctx_1024t = _ctx_1024t * jax.lax.rsqrt(jnp.mean(jnp.square(_ctx_1024t)) + 1e-12) * 0.953939
        ctx_1024 = -1.39393e-06 + 0.999914 * (_ctx_1024t + 0.3 * jax.random.normal(jax.random.fold_in(_rk, 611), (16, 128, 128), jnp.float32))
        fside_BxSx2_0 = jax.random.uniform(jax.random.fold_in(_rk, 12), (16, 128, 2), jnp.float32, 0.0, 0.999707)
        _g = jax.random.normal(jax.random.fold_in(_rk, 9001), (2, 1), jnp.float32)
        _g = jnp.sign(_g) * jnp.maximum(jnp.abs(_g), 1.0) + (_g == 0) * 1.0
        g_xattn = _g[0]
        g_ffn = _g[1]
        return (x, ctx_1024, fside_BxSx2_0, g_xattn, g_ffn)
    x, ctx_1024, fside_BxSx2_0, g_xattn, g_ffn = _rec_inputs()

    def _L0_xattn_setup():
        import jax, jax.numpy as jnp
        import numpy as np
        DIM = 256
        CTX_DIM = 128
        N_HEADS = 32
        HEAD_DIM = DIM // N_HEADS
        POS_DIM = 2
        B, N, CTXN = (2, 256, 256)
        ROPE_BASE = 10000.0

        def apply_axial_rope(x, pos):
            b, n, h, d = x.shape
            p = pos.shape[-1]
            dpa = d // p
            half = dpa // 2
            freqs = ROPE_BASE ** (-jnp.arange(half, dtype=x.dtype) / half)
            ang = pos[..., :, None] * freqs
            cos = jnp.cos(ang)[:, :, None, :, :]
            sin = jnp.sin(ang)[:, :, None, :, :]
            xr = x.reshape(b, n, h, p, half, 2)
            x1, x2 = (xr[..., 0], xr[..., 1])
            out = jnp.stack([x1 * cos - x2 * sin, x1 * sin + x2 * cos], axis=-1)
            return out.reshape(b, n, h, d)
        key = jax.random.key(seed)
        ks = jax.random.split(key, 8)
        x = jax.random.normal(ks[0], (B, N, DIM), jnp.float32)
        ctx = jax.random.normal(ks[1], (B, CTXN, CTX_DIM), jnp.float32)
        pos_map = jax.random.uniform(ks[2], (B, N, POS_DIM), jnp.float32)
        ctx_pos_map = jax.random.uniform(ks[3], (B, CTXN, POS_DIM), jnp.float32)
        Wq = jax.random.normal(ks[4], (DIM, DIM), jnp.float32) / np.sqrt(DIM)
        Wkv = jax.random.normal(ks[5], (CTX_DIM, 2 * DIM), jnp.float32) / np.sqrt(CTX_DIM)
        Wout = jax.random.normal(ks[6], (DIM, DIM), jnp.float32) / np.sqrt(DIM)
        bout = jnp.zeros((DIM,), jnp.float32)
        return {'x': x, 'ctx': ctx, 'pos_map': pos_map, 'ctx_pos_map': ctx_pos_map, 'Wq': Wq, 'Wkv': Wkv, 'Wout': Wout, 'bout': bout}
    _L0_xattn_all = _L0_xattn_setup()
    _L0_xattn_in = {k: v for k, v in _L0_xattn_all.items() if k in ('Wq', 'Wkv', 'Wout', 'bout')}
    del _L0_xattn_all

    def _L0_ffn_setup():
        import jax, jax.numpy as jnp
        import numpy as np
        import math
        GOLDEN_CENTER = 1.0 / math.e
        GOLDEN_LOWER = 0.5 - math.log(4.0 / 3.0)
        GOLDEN_UPPER = 0.5
        B, T, D = (4, 128, 256)
        E = 8
        F = 1024 // (E // 2)
        R = 64
        NL = 2

        def _router_weights(x, Wr, temperature):
            logits = jnp.einsum('btd,de->bte', x, Wr)
            inhibition = jax.nn.sigmoid(logits / temperature)
            in_zone = (inhibition >= GOLDEN_LOWER) & (inhibition <= GOLDEN_UPPER)
            distance = jnp.abs(inhibition - GOLDEN_CENTER)
            w = jnp.exp(-distance / 0.1) * in_zone.astype(x.dtype)
            wsum = w.sum(axis=-1, keepdims=True)
            no_expert = wsum < 1e-08
            fb = jnp.exp(-distance / 0.3)
            _, top2 = jax.lax.top_k(fb, 2)
            fb_mask = jax.nn.one_hot(top2, E, dtype=x.dtype).sum(axis=-2)
            fb_w = fb * fb_mask
            fb_w = fb_w / jnp.clip(fb_w.sum(axis=-1, keepdims=True), 1e-08)
            w = jnp.where(no_expert, fb_w, w)
            return w / jnp.clip(w.sum(axis=-1, keepdims=True), 1e-08)
        key = jax.random.key(seed)
        ks = jax.random.split(key, 13)
        s = 0.02
        x = jax.random.normal(ks[0], (B, T, D), dtype=jnp.float32)
        Wg = jax.random.normal(ks[1], (E, D, F), dtype=jnp.float32) * s
        Wu = jax.random.normal(ks[2], (E, D, F), dtype=jnp.float32) * s
        Wd = jax.random.normal(ks[3], (E, F, D), dtype=jnp.float32) * s
        Ga = jax.random.normal(ks[4], (NL, D, R), dtype=jnp.float32) * s
        Gb = jax.random.normal(ks[5], (NL, R, F), dtype=jnp.float32) * s
        Ua = jax.random.normal(ks[6], (NL, D, R), dtype=jnp.float32) * s
        Ub = jax.random.normal(ks[7], (NL, R, F), dtype=jnp.float32) * s
        Da = jax.random.normal(ks[8], (NL, F, R), dtype=jnp.float32) * s
        Db = jax.random.normal(ks[9], (NL, R, D), dtype=jnp.float32) * s
        Wr = jax.random.normal(ks[10], (D, E), dtype=jnp.float32) * s
        temperature = jnp.ones((1,), dtype=jnp.float32)
        return {'x': x, 'Wg': Wg, 'Wu': Wu, 'Wd': Wd, 'Ga': Ga, 'Gb': Gb, 'Ua': Ua, 'Ub': Ub, 'Da': Da, 'Db': Db, 'Wr': Wr, 'temperature': temperature}
    _L0_ffn_all = _L0_ffn_setup()
    _L0_ffn_in = {k: v for k, v in _L0_ffn_all.items() if k in ('Wg', 'Wu', 'Wd', 'Ga', 'Gb', 'Ua', 'Ub', 'Da', 'Db', 'Wr', 'temperature')}
    del _L0_ffn_all
    return {'x': x, 'ctx_1024': ctx_1024, 'fside_BxSx2_0': fside_BxSx2_0, 'g_xattn': g_xattn, 'g_ffn': g_ffn, 'L0_xattn_Wq': _L0_xattn_in['Wq'], 'L0_xattn_Wkv': _L0_xattn_in['Wkv'], 'L0_xattn_Wout': _L0_xattn_in['Wout'], 'L0_xattn_bout': _L0_xattn_in['bout'], 'L0_ffn_Wg': _L0_ffn_in['Wg'], 'L0_ffn_Wu': _L0_ffn_in['Wu'], 'L0_ffn_Wd': _L0_ffn_in['Wd'], 'L0_ffn_Ga': _L0_ffn_in['Ga'], 'L0_ffn_Gb': _L0_ffn_in['Gb'], 'L0_ffn_Ua': _L0_ffn_in['Ua'], 'L0_ffn_Ub': _L0_ffn_in['Ub'], 'L0_ffn_Da': _L0_ffn_in['Da'], 'L0_ffn_Db': _L0_ffn_in['Db'], 'L0_ffn_Wr': _L0_ffn_in['Wr'], 'L0_ffn_temperature': _L0_ffn_in['temperature']}

def reference(x, ctx_1024, fside_BxSx2_0, g_xattn, g_ffn, L0_xattn_Wq, L0_xattn_Wkv, L0_xattn_Wout, L0_xattn_bout, L0_ffn_Wg, L0_ffn_Wu, L0_ffn_Wd, L0_ffn_Ga, L0_ffn_Gb, L0_ffn_Ua, L0_ffn_Ub, L0_ffn_Da, L0_ffn_Db, L0_ffn_Wr, L0_ffn_temperature):
    import jax
    import jax.numpy as jnp

    def _L0_xattn_ref(x, ctx, pos_map, ctx_pos_map, Wq, Wkv, Wout, bout):
        import jax, jax.numpy as jnp
        import numpy as np
        DIM = 256
        CTX_DIM = 128
        N_HEADS = 32
        HEAD_DIM = DIM // N_HEADS
        POS_DIM = 2
        B, N, CTXN = (2, 256, 256)
        ROPE_BASE = 10000.0

        def apply_axial_rope(x, pos):
            b, n, h, d = x.shape
            p = pos.shape[-1]
            dpa = d // p
            half = dpa // 2
            freqs = ROPE_BASE ** (-jnp.arange(half, dtype=x.dtype) / half)
            ang = pos[..., :, None] * freqs
            cos = jnp.cos(ang)[:, :, None, :, :]
            sin = jnp.sin(ang)[:, :, None, :, :]
            xr = x.reshape(b, n, h, p, half, 2)
            x1, x2 = (xr[..., 0], xr[..., 1])
            out = jnp.stack([x1 * cos - x2 * sin, x1 * sin + x2 * cos], axis=-1)
            return out.reshape(b, n, h, d)
        b, n, _ = x.shape
        ctx_n = ctx.shape[1]
        q = (x @ Wq).reshape(b, n, N_HEADS, HEAD_DIM)
        k, v = jnp.split(ctx @ Wkv, 2, axis=-1)
        k = k.reshape(b, ctx_n, N_HEADS, HEAD_DIM)
        v = v.reshape(b, ctx_n, N_HEADS, HEAD_DIM)
        q = apply_axial_rope(q, pos_map)
        k = apply_axial_rope(k, ctx_pos_map)
        scale = 1.0 / np.sqrt(HEAD_DIM).astype(np.float32)
        logits = jnp.einsum('bqhd,bkhd->bhqk', q, k) * scale
        w = jax.nn.softmax(logits, axis=-1)
        attn = jnp.einsum('bhqk,bkhd->bqhd', w, v)
        attn = attn.reshape(b, n, N_HEADS * HEAD_DIM)
        return attn @ Wout + bout

    def _L0_ffn_ref(x, Wg, Wu, Wd, Ga, Gb, Ua, Ub, Da, Db, Wr, temperature):
        import jax, jax.numpy as jnp
        import numpy as np
        import math
        GOLDEN_CENTER = 1.0 / math.e
        GOLDEN_LOWER = 0.5 - math.log(4.0 / 3.0)
        GOLDEN_UPPER = 0.5
        B, T, D = (4, 128, 256)
        E = 8
        F = 1024 // (E // 2)
        R = 64
        NL = 2

        def _router_weights(x, Wr, temperature):
            logits = jnp.einsum('btd,de->bte', x, Wr)
            inhibition = jax.nn.sigmoid(logits / temperature)
            in_zone = (inhibition >= GOLDEN_LOWER) & (inhibition <= GOLDEN_UPPER)
            distance = jnp.abs(inhibition - GOLDEN_CENTER)
            w = jnp.exp(-distance / 0.1) * in_zone.astype(x.dtype)
            wsum = w.sum(axis=-1, keepdims=True)
            no_expert = wsum < 1e-08
            fb = jnp.exp(-distance / 0.3)
            _, top2 = jax.lax.top_k(fb, 2)
            fb_mask = jax.nn.one_hot(top2, E, dtype=x.dtype).sum(axis=-2)
            fb_w = fb * fb_mask
            fb_w = fb_w / jnp.clip(fb_w.sum(axis=-1, keepdims=True), 1e-08)
            w = jnp.where(no_expert, fb_w, w)
            return w / jnp.clip(w.sum(axis=-1, keepdims=True), 1e-08)
        weights = _router_weights(x, Wr, temperature)
        gate = jnp.einsum('btd,edf->ebtf', x, Wg)
        up = jnp.einsum('btd,edf->ebtf', x, Wu)
        gate = gate.at[:NL].add(jnp.einsum('btd,edr,erf->ebtf', x, Ga, Gb))
        up = up.at[:NL].add(jnp.einsum('btd,edr,erf->ebtf', x, Ua, Ub))
        mid = jax.nn.silu(gate) * up
        out = jnp.einsum('ebtf,efd->ebtd', mid, Wd)
        out = out.at[:NL].add(jnp.einsum('ebtf,efr,erd->ebtd', mid[:NL], Da, Db))
        return jnp.einsum('bte,ebtd->btd', weights, out)
    x = x + jnp.tanh(g_xattn[0]) * _L0_xattn_ref(_layernorm(x, axis=-1), ctx_1024, fside_BxSx2_0, fside_BxSx2_0, L0_xattn_Wq, L0_xattn_Wkv, L0_xattn_Wout, L0_xattn_bout)
    x = x + jnp.tanh(g_ffn[0]) * _L0_ffn_ref(_layernorm(x, axis=-1), L0_ffn_Wg, L0_ffn_Wu, L0_ffn_Wd, L0_ffn_Ga, L0_ffn_Gb, L0_ffn_Ua, L0_ffn_Ub, L0_ffn_Da, L0_ffn_Db, L0_ffn_Wr, L0_ffn_temperature)
    return x

_drawn_inputs = setup_inputs


def setup_inputs(seed=0):
    import zlib

    import numpy as np

    out = dict(_drawn_inputs(seed))
    spreads = {'L0_xattn_bout': (0.0, 0.1)}
    factors = {'L0_ffn_Wg': 7.096,
     'L0_ffn_Wu': 7.002,
     'L0_ffn_Wd': 6.991,
     'L0_ffn_Ga': 8.0,
     'L0_ffn_Gb': 8.0,
     'L0_ffn_Ua': 8.0,
     'L0_ffn_Ub': 8.0,
     'L0_ffn_Da': 8.0,
     'L0_ffn_Db': 8.0,
     'L0_ffn_Wr': 8.0}
    for name, (base, spread) in spreads.items():
        noise = np.random.default_rng([zlib.crc32(name.encode()), seed]).standard_normal(out[name].shape)
        drawn = base * np.exp(spread * noise) if base else spread * noise
        out[name] = jnp.asarray(drawn.astype(out[name].dtype))
    for name, factor in factors.items():
        out[name] = (out[name] * factor).astype(out[name].dtype)
    return out
```

```python
import math
from contextlib import ExitStack

import concourse.bass as bass
from concourse import mybir

F32 = mybir.dt.float32
F32R = mybir.dt.float32r
F16 = mybir.dt.float16
I32 = mybir.dt.int32
ALU = mybir.AluOpType
ACT = mybir.ActivationFunctionType
AX_X = mybir.AxisListType.X

P = 128


def has(b, back):
    return not isinstance(b, int) or b >= back


def flamingo_kernel(nc, x, ctxT, pos, g_xattn, g_ffn, Wq, Wkv, Wout, bout, Wexp, GaT, Gb, UaT, Ub, DaT, Db,
                    Wr, temperature, ident, ident16, lower_tri, out):
    B, T, D = x.shape
    DK = D // P
    HEADS, HD = 32, 8
    QUAD = 4
    GROUPS = HEADS // QUAD
    ROWS = P // QUAD
    UNITS = 4
    UH = HEADS // UNITS
    NE, WCOLS = Wexp.shape[0], Wexp.shape[2]
    F = WCOLS // (3 * DK)
    FK = F // P
    NL, R = GaT.shape[0], GaT.shape[1]
    TG = 4
    NG = B // TG
    GT = TG * P
    SCALE = 1.0 / math.sqrt(HD)
    EPS = 1e-5
    TWO_PI = 2.0 * math.pi
    PI2_HI = 6.28125
    PI2_LO = TWO_PI - PI2_HI
    ROUND = 1.5 * 2.0 ** 23
    FREQ = [1.0, 10000.0 ** -0.5]
    LOWER, UPPER, CENTER = 0.5 - math.log(4.0 / 3.0), 0.5, 1.0 / math.e
    assert T == P and D == HEADS * HD and WCOLS == 6 * 256 and NL == 2 and B % 4 == 0

    ctx = ExitStack()
    with ctx:
        def sb(name, shape, dt=F32):
            return ctx.enter_context(nc.sbuf_tensor(name, shape, dt))

        def sem(name):
            return ctx.enter_context(nc.semaphore(name))

        X = sb("X", [P, B, D])
        H2H = sb("H2H", [P, DK, B * P], F32R)
        H2L = sb("H2L", [P, DK, B * P], F32R)
        WH = sb("WH", [P, 2, WCOLS], F32R)
        WL = sb("WL", [P, 2, WCOLS], F32R)
        WS = sb("WS", [P, 2, WCOLS])
        LG = sb("LG", [P, B, NE])
        WT = sb("WT", [P, B, NE])
        ID = sb("ID", [P, P])
        ID16 = sb("ID16", [P, P], F16)
        TRI = sb("TRI", [P, NE, NE])
        GATE = sb("GATE", [P, 2])
        TG2 = sb("TG2", [P, 2])
        TEMP = sb("TEMP", [P, 1])
        HIT = sb("HIT", [P, 2])
        BOUT = sb("BOUT", [P, D])
        TGB = sb("TGB", [P, D])
        PW = sb("PW", [P, 3, 512])
        PWH = sb("PWH", [P, 3, 512], F32R)
        PWL = sb("PWL", [P, 3, 512], F32R)
        RW = sb("RW", [P, DK, NE])
        RWH = sb("RWH", [P, DK, NE], F32R)
        RWL = sb("RWL", [P, DK, NE], F32R)
        POS = sb("POS", [P, B, 2])
        ANG = sb("ANG", [P, 2, B * 2, 2])
        TURN = sb("TURN", [P, 2, B * 4])
        TRIG = sb("TRIG", [P, 3, B, 4])
        ST1 = sb("ST1", [P, B, 6])
        MV1 = sb("MV1", [P, B, 2])
        RS1 = sb("RS1", [P, B])
        NW1 = sb("NW1", [P, 3, B])
        CTX = sb("CTX", [P, B * P])
        CH = sb("CH", [P, P], F32R)
        CL = sb("CL", [P, P], F32R)
        H = sb("H", [P, D])
        HTH = sb("HTH", [P, DK * P], F32R)
        HTL = sb("HTL", [P, DK * P], F32R)
        QA = sb("QA", [P, D])
        QB = sb("QB", [P, D])
        QR = sb("QR", [P, D])
        KA = sb("KA", [P, D])
        KB = sb("KB", [P, D])
        KR = sb("KR", [P, D])
        QS = sb("QS", [P, HEADS, ROWS], F16)
        KS = sb("KS", [P, HEADS, ROWS], F16)
        KT = sb("KT", [P, GROUPS * P], F16)
        KP = sb("KP", [P, 2, QUAD, GROUPS, P], F16)
        QTA = sb("QTA", [P, GROUPS, P], F16)
        QTB = sb("QTB", [P, GROUPS, P], F16)
        VA = sb("VA", [P, 2, HEADS // 2, 80])
        E = sb("E", [P, 2, UH * P])
        LORA_A = E[:].rearrange("p a n -> p (a n)")[0:R, 0:3 * NL * F].rearrange("r (m l f) -> r m l f", m=3, l=NL)
        OS = sb("OS", [P, 512])
        RSUM = sb("RSUM", [P, HEADS // 2, 2])
        AT = sb("AT", [P, D])
        ATH = sb("ATH", [P, DK * P], F32R)
        ATL = sb("ATL", [P, DK * P], F32R)
        ST2 = sb("ST2", [P, 6])
        MV2 = sb("MV2", [P, 2])
        NW2 = sb("NW2", [P, 5])
        TICK = sb("TICK", [P, 1])
        C15 = sb("C15", [P, 1])
        H2 = sb("H2", [P, D])
        T2H = sb("T2H", [P, DK * P], F32R)
        T2L = sb("T2L", [P, DK * P], F32R)
        RT = sb("RT", [P, 8, B, NE])
        RC = CTX[:].rearrange("p (a b i j) -> p a b i j", a=2, b=B, i=NE)
        RV = sb("RV", [P, 6, B])
        SM = sb("SM", [P, 2, FK, GT])
        SIL, MID = SM[:, 0], SM[:, 1]
        LORA_B = SM[:].rearrange("p a c n -> p (a c n)")[0:R, 0:3 * NL * F].rearrange("r (m l f) -> r m l f", m=3, l=NL)
        MH = sb("MH", [P, 2, FK, GT], F32R)
        ML = sb("ML", [P, 2, FK, GT], F32R)

        PS = ctx.enter_context(nc.psum_tensor("PS", [P, 8, 512], F32))
        LBANK = [PS[:, 0:2, :].rearrange("p a n -> p (a n)"), PS[:, 2:4, :].rearrange("p a n -> p (a n)")]
        TBANK = PS[:, 4, :]
        TB16 = PS[:, 4, :].bitcast(F16)
        YBANK = PS[:, 5, :]
        OBANK = PS[:, 6, :]
        HBANK = PS[:, 7, :]

        d_x = [sem(f"d_x{i}") for i in range(4)]
        d_ws = [sem(f"d_ws{i}") for i in range(2)]
        d_gate, d_pos, d_ctx, d_pw, d_lora, d_const, d_rw = [
            sem(n) for n in ("d_gate", "d_pos", "d_ctx", "d_pw", "d_lora", "d_const", "d_rw")]
        zeroed, tanh_done, inv_temp, tgb_done = sem("zeroed"), sem("tanh_done"), sem("inv_temp"), sem("tgb_done")
        angles, trig, neg_sin = sem("angles"), sem("trig"), sem("neg_sin")
        stats1, guess1, rstd1 = sem("stats1"), sem("guess1"), sem("rstd1")
        pw_hi, pw_lo = sem("pw_hi"), sem("pw_lo")
        lora_ps, lora_added = sem("lora_ps"), sem("lora_added")
        wh_done, wl_done = sem("wh_done"), sem("wl_done")
        h_ready, hT_ps, hT_hi, hT_lo, q_ps = sem("h_ready"), sem("hT_ps"), sem("hT_hi"), sem("hT_lo"), sem("q_ps")
        xb_done = sem("xb_done")
        c_hi, c_lo, kv_ps, v_done = sem("c_hi"), sem("c_lo"), sem("kv_ps"), sem("v_done")
        k_terms, q_terms = sem("k_terms"), sem("q_terms")
        k_rot, k_hi, k_lo = sem("k_rot"), sem("k_hi"), sem("k_lo")
        q_rot, q_hi, q_lo, m_zero = sem("q_rot"), sem("q_hi"), sem("q_lo"), sem("m_zero")
        kT_ps, kT_sb, qT_ps, qT_sb = sem("kT_ps"), sem("kT_sb"), sem("qT_ps"), sem("qT_sb")
        kp_dma = sem("kp_dma")
        p1_ps, max_done = sem("p1_ps"), sem("max_done")
        qmT_ps, qmT_sb = sem("qmT_ps"), sem("qmT_sb")
        p2_ps, exp_done, av_ps = sem("p2_ps"), sem("exp_done"), sem("av_ps")
        o_sb = sem("o_sb")
        oT_ps, sums_inv, attn, aT_ps = sem("oT_ps"), sem("sums_inv"), sem("attn"), sem("aT_ps")
        a_hi, a_lo, proj_ps, x1_done = sem("a_hi"), sem("a_lo"), sem("proj_ps"), sem("x1_done")
        ln2 = sem("ln2")
        LN2, NEWTON = 8, 12
        newton2 = sem("newton2")
        h2_ready, h2T_ps, h2_hi, h2_lo = sem("h2_ready"), sem("h2T_ps"), sem("h2_hi"), sem("h2_lo")
        h2_dma = sem("h2_dma")
        rt_ps, rt_sb = sem("rt_ps"), sem("rt_sb")
        r_pool, r_act, r_dve = sem("r_pool"), sem("r_act"), sem("r_dve")
        g_ps, u_ps, silu_done, m_done = sem("g_ps"), sem("u_ps"), sem("silu_done"), sem("m_done")
        CREDIT = 2 * TG
        mh_done, ml_done, d_ps, acc_done, d_out = sem("mh_done"), sem("ml_done"), sem("d_ps"), sem("acc_done"), sem("d_out")

        block = ctx.enter_context(nc.Block())

        def pipeline(eng, prologue, step, epilogue):
            prologue()
            step(0, 0, True, False)
            step(1, 1, False, False)
            step(2, 0, False, False)
            with eng.Fori(0, (B - 4) // 2) as half:
                i = eng.snap(2 * half + 3)
                step(i, 1, False, False)
                step(i + 1, 0, False, False)
            step(B - 1, 1, False, True)
            epilogue()

        @block.sync
        def _(sp):
            xv = x.rearrange("b t d -> t b d")
            sp.dma_start(X[:, 0:4, :], xv[:, 0:4, :]).then_inc(d_x[0], 16)
            sp.dma_start(PW[:, 0, :].rearrange("p (k n) -> p k n", k=DK),
                         Wq.rearrange("(k p) n -> p k n", p=P)).then_inc(d_pw, 16)
            sp.dma_start(PW[:, 1, :], Wkv).then_inc(d_pw, 16)
            sp.dma_start(PW[:, 2, :].rearrange("p (k n) -> p k n", k=DK),
                         Wout.rearrange("(k p) n -> p k n", p=P)).then_inc(d_pw, 16)
            sp.dma_start(X[:, 4:8, :], xv[:, 4:8, :]).then_inc(d_x[1], 16)
            sp.dma_start(X[:, 8:12, :], xv[:, 8:12, :]).then_inc(d_x[2], 16)
            sp.dma_start(X[:, 12:16, :], xv[:, 12:16, :]).then_inc(d_x[3], 16)
            for e in range(2):
                sp.dma_start(WS[:, e, :], Wexp[e]).then_inc(d_ws[e], 16)

            def spread_k(b, par):
                sp.wait_ge(kT_sb, b + 1)
                if has(b, 2):
                    sp.wait_ge(p2_ps, UNITS * (b - 1))
                if b is 0 or (isinstance(b, int) and b < 2):
                    sp.wait_ge(zeroed, 6)
                for j in range(QUAD):
                    r = slice(j * ROWS, (j + 1) * ROWS)
                    sp.dma_start(KP[r, par, j, :, :].rearrange("p g n -> p (g n)"), KT[r, :]).then_inc(kp_dma, 16)

            def keep_h2(b):
                sp.wait_ge(h2_hi, b + 1)
                sp.wait_ge(h2_lo, b + 1)
                for dst, src in ((H2H, T2H), (H2L, T2L)):
                    sp.dma_start(dst[:, :, bass.ds(b * P, P)].bitcast(F32),
                                 src[:, :].rearrange("p (k n) -> p k n", k=DK).bitcast(F32)).then_inc(h2_dma, 16)

            def step(i, par, first, last):
                if not last:
                    spread_k(i + 1, 1 - par)
                if not first:
                    keep_h2(i - 1)

            pipeline(sp, lambda: spread_k(0, 0), step, lambda: keep_h2(B - 1))

            for e in range(2, NE):
                sp.wait_ge(wl_done, 3 * (e - 1))
                sp.dma_start(WS[:, e % 2, :], Wexp[e]).then_inc(d_ws[e % 2], 16)
            ov = out.rearrange("b t d -> t b d")
            for g in range(NG):
                sp.wait_ge(acc_done, CREDIT + TG * (NG * (NE - 1) + g + 1))
                sp.dma_start(ov[:, TG * g:TG * (g + 1), :], X[:, TG * g:TG * (g + 1), :]).then_inc(d_out, 16)
            sp.wait_ge(d_out, 16 * NG)

        @block.gpsimd
        def _(pool):
            nc.gpsimd.memset(C15[:], 1.5)
            nc.gpsimd.memset(KS[:], 0.0).then_inc(zeroed, 1)
            nc.gpsimd.memset(QS[:], 0.0).then_inc(zeroed, 1)
            nc.gpsimd.memset(VA[:], 0.0).then_inc(zeroed, 1)
            pool.wait_ge(zeroed, 3)
            nc.gpsimd.memset(KS[:, :, 24], -1.0).then_inc(zeroed, 1)
            nc.gpsimd.memset(VA[:, :, :, 16], 1.0)
            nc.gpsimd.memset(VA[:, :, :, 49], 1.0).then_inc(zeroed, 1)
            nc.gpsimd.memset(KP[:].rearrange("p a j g n -> p (a j g n)").bitcast(F32), 0.0).then_inc(zeroed, 1)
            for n in range(3):
                pool.wait_ge(pw_hi, n + 1)
                nc.gpsimd.tensor_tensor(PWL[:, n, :], PW[:, n, :], PWH[:, n, :].bitcast(F32),
                                        ALU.subtract).then_inc(pw_lo, 1)
            pool.wait_ge(pw_hi, 4)
            nc.gpsimd.tensor_tensor(RWL[:], RW[:], RWH[:].bitcast(F32), ALU.subtract).then_inc(pw_lo, 1)
            pool.wait_ge(tanh_done, 1)
            pool.wait_ge(d_const, 16 * 4)
            nc.gpsimd.tensor_scalar(TGB[:], BOUT[:], TG2[:, 0:1], None, ALU.mult).then_inc(tgb_done, 1)

            def c_low(b):
                pool.wait_ge(c_hi, b + 1)
                if has(b, 1):
                    pool.wait_ge(kv_ps, b)
                nc.gpsimd.tensor_tensor(CL[:], CTX[:, bass.ds(b * P, P)], CH[:].bitcast(F32),
                                        ALU.subtract).then_inc(c_lo, 1)

            def add_bias(b):
                pool.wait_ge(h_ready, b + 1)
                pool.wait_ge(tgb_done, 1)
                nc.gpsimd.tensor_tensor(X[:, bass.ds(b, 1), :], X[:, bass.ds(b, 1), :],
                                        TGB[:, :].rearrange("p (o d) -> p o d", o=1), ALU.add).then_inc(xb_done, 1)

            def rotate(b, terms, ta, tb, rot, hi, lo, done):
                pool.wait_ge(terms, 3 * (b + 1))
                if has(b, 1):
                    pool.wait_ge(hi, b)
                    pool.wait_ge(lo, b)
                nc.gpsimd.tensor_tensor(rot[:], ta[:], tb[:], ALU.add).then_inc(done, 1)

            def low16(b, rot, S, at, hi, lo):
                pool.wait_ge(hi, b + 1)
                r = rot[:].rearrange("p (h d) -> p h d", d=HD)
                nc.gpsimd.tensor_tensor(S[:, :, at:at + HD], r, S[:, :, 0:HD], ALU.subtract).then_inc(lo, 1)

            def clear_max(b):
                if has(b, 1):
                    pool.wait_ge(qmT_ps, b)
                else:
                    pool.wait_ge(zeroed, 2)
                nc.gpsimd.tensor_tensor(QS[:, :, 24], KS[:, :, 25], KS[:, :, 25], ALU.add).then_inc(m_zero, 1)

            def newton(b):
                y, v, t = NW2[:, 2:3], NW2[:, 4:5], NW2[:, 3:4]
                pool.wait_ge(ln2, LN2 * (b + 1))
                if has(b, 1):
                    pool.wait_ge(newton2, NEWTON * b)
                n = 0
                for _ in range(3):
                    for o, a, c, op in ((t, y, y, ALU.mult), (t, t, v, ALU.mult), (t, t, C15[:], ALU.add),
                                        (y, y, t, ALU.mult)):
                        if n:
                            pool.wait_ge(newton2, NEWTON * b + n)
                        nc.gpsimd.tensor_tensor(o, a, c, op).then_inc(newton2, 1)
                        n += 1

            def front(b):
                c_low(b)
                add_bias(b)
                rotate(b, k_terms, KA, KB, KR, k_hi, k_lo, k_rot)
                rotate(b, q_terms, QA, QB, QR, q_hi, q_lo, q_rot)
                low16(b, KR, KS, HD, k_hi, k_lo)
                clear_max(b)
                low16(b, QR, QS, 2 * HD, q_hi, q_lo)

            v1, y1, t1 = NW1[:, 0, :], RS1[:, :], NW1[:, 2, :]
            n = 0
            pool.wait_ge(guess1, 3)
            for k in range(3):
                for o, a, c in ((t1, y1, y1), (t1, t1, v1)):
                    if n:
                        pool.wait_ge(rstd1, n)
                    nc.gpsimd.tensor_tensor(o, a, c, ALU.mult).then_inc(rstd1, 1)
                    n += 1
                pool.wait_ge(rstd1, n)
                nc.gpsimd.tensor_scalar(t1, t1, -0.5, 1.5, ALU.mult, ALU.add).then_inc(rstd1, 1)
                n += 1
                pool.wait_ge(rstd1, n)
                nc.gpsimd.tensor_tensor(y1, y1, t1, ALU.mult).then_inc(rstd1, 1)
                n += 1

            def split_expert(e, slot):
                for n in range(3):
                    c = slice(512 * n, 512 * (n + 1))
                    nc.gpsimd.tensor_scalar(WH[:, slot, c], WS[:, slot, c], 1.0, None, ALU.mult).then_inc(wh_done, 1)
                    pool.wait_ge(wh_done, 3 * e + n + 1)
                    nc.gpsimd.tensor_tensor(WL[:, slot, c], WS[:, slot, c], WH[:, slot, c].bitcast(F32),
                                            ALU.subtract).then_inc(wl_done, 1)

            def step(i, par, first, last):
                if not last:
                    front(i + 1)
                if not first:
                    newton(i - 1)
                if first:
                    pool.wait_ge(lora_added, 3)
                    split_expert(0, 0)
                if last:
                    pool.wait_ge(lora_added, 6)
                    split_expert(1, 1)

            def router(lo, hi, rp, ra, rd):
                cnt = [rp]
                s = slice(lo, hi)
                n = hi - lo

                def did(ins):
                    cnt[0] += 1
                    ins.then_inc(r_pool, 1)
                    pool.wait_ge(r_pool, cnt[0])

                th, sig, dist, zone, tmp, e1, e3, w = [RT[:, k, s, :] for k in range(8)]
                gt, eq = RC[:, 0, s], RC[:, 1, s]
                diff = gt
                wsum, none, some, fsum = [RV[:, k, s] for k in range(4)]

                def wide(v):
                    return v.unsqueeze(2).to_broadcast([P, n, NE])

                if rp == 0:
                    pool.wait_ge(c_lo, B)
                pool.wait_ge(r_act, ra + 1)
                did(nc.gpsimd.tensor_scalar(sig, th, 0.5, 0.5, ALU.mult, ALU.add))
                did(nc.gpsimd.tensor_scalar(zone, sig, LOWER, None, ALU.is_ge))
                did(nc.gpsimd.tensor_scalar(tmp, sig, UPPER, None, ALU.is_le))
                did(nc.gpsimd.tensor_tensor(zone, zone, tmp, ALU.mult))
                did(nc.gpsimd.tensor_scalar(sig, sig, CENTER, None, ALU.subtract))
                assert cnt[0] == rp + 5
                pool.wait_ge(r_act, ra + 2)
                mine = dist.unsqueeze(3).to_broadcast([P, n, NE, NE])
                other = dist.unsqueeze(2).to_broadcast([P, n, NE, NE])
                did(nc.gpsimd.tensor_tensor(diff, mine, other, ALU.subtract))
                did(nc.gpsimd.tensor_scalar(eq, diff, 0.0, None, ALU.is_equal))
                did(nc.gpsimd.tensor_scalar(gt, diff, 0.0, None, ALU.is_gt))
                did(nc.gpsimd.tensor_tensor(eq, eq, TRI[:].unsqueeze(1).to_broadcast([P, n, NE, NE]), ALU.mult))
                did(nc.gpsimd.tensor_tensor(gt, gt, eq, ALU.add))
                pool.wait_ge(r_dve, rd + 1)
                did(nc.gpsimd.tensor_scalar(tmp, tmp, 1.5, None, ALU.is_lt))
                pool.wait_ge(r_act, ra + 4)
                did(nc.gpsimd.tensor_tensor(e3, e3, tmp, ALU.mult))
                did(nc.gpsimd.tensor_tensor(w, e1, zone, ALU.mult))
                pool.wait_ge(r_dve, rd + 5)
                did(nc.gpsimd.tensor_tensor(e3, e3, wide(fsum), ALU.mult))
                did(nc.gpsimd.tensor_scalar(none, wsum, 1e-8, None, ALU.is_lt))
                did(nc.gpsimd.tensor_scalar(some, none, -1.0, 1.0, ALU.mult, ALU.add))
                did(nc.gpsimd.tensor_tensor(e3, e3, wide(none), ALU.mult))
                did(nc.gpsimd.tensor_tensor(w, w, wide(some), ALU.mult))
                did(nc.gpsimd.tensor_tensor(w, w, e3, ALU.add))
                pool.wait_ge(r_dve, rd + 8)
                did(nc.gpsimd.tensor_scalar(tmp, w, TG2[:, 1:2], None, ALU.mult))
                did(nc.gpsimd.tensor_tensor(WT[:, s, :], tmp, wide(wsum), ALU.mult))
                assert cnt[0] == rp + 21

            def prologue():
                front(0)

            def step_r(i, par, first, last):
                step(i, par, first, last)
                if last:
                    router(0, B - 2, 0, 0, 0)

            def epilogue():
                newton(B - 1)
                router(B - 2, B, 21, 4, 8)

            pipeline(pool, prologue, step_r, epilogue)

            for e in range(2, NE):
                pool.wait_ge(d_ws[e % 2], 16 * (e // 2 + 1))
                pool.wait_ge(d_ps, NG * (e - 1))
                split_expert(e, e % 2)

        @block.scalar
        def _(act):
            act.dma_start(POS[:], pos.rearrange("b t c -> t b c")).then_inc(d_pos, 16)
            act.dma_start(ID[:], ident).then_inc(d_const, 16)
            act.dma_start(ID16[:], ident16).then_inc(d_const, 16)
            act.dma_start(CTX[:], ctxT).then_inc(d_ctx, 16)
            act.dma_start(GATE[:, 0:1], g_xattn.partition_broadcast(P)).then_inc(d_gate, 16)
            act.dma_start(GATE[:, 1:2], g_ffn.partition_broadcast(P)).then_inc(d_gate, 16)
            act.dma_start(TEMP[:], temperature.partition_broadcast(P)).then_inc(d_gate, 16)
            act.dma_start(BOUT[:], bout.partition_broadcast(P)).then_inc(d_const, 16)
            act.dma_start(TRI[:], lower_tri).then_inc(d_const, 16)
            for n, (a, c) in enumerate(((GaT, Gb), (UaT, Ub), (DaT, Db))):
                act.dma_start(LORA_A[:, n], a.rearrange("l r f -> r l f")).then_inc(d_lora, 16)
                act.dma_start(LORA_B[:, n], c.rearrange("l r f -> r l f")).then_inc(d_lora, 16)
            act.dma_start(RW[:], Wr.rearrange("(k p) e -> p k e", p=P)).then_inc(d_rw, 16)

            act.wait_ge(angles, 8)
            nc.scalar.activation(TRIG[:, 0:2].rearrange("p a b c -> p (a b c)"),
                                 ANG[:].rearrange("p a b c -> p (a b c)"), ACT.Sin).then_inc(trig, 1)
            act.wait_ge(d_gate, 48)
            nc.scalar.activation(TG2[:], GATE[:], ACT.Tanh).then_inc(tanh_done, 1)
            act.wait_ge(d_pw, 48)
            for n in range(3):
                nc.scalar.activation(PWH[:, n, :], PW[:, n, :], ACT.Copy).then_inc(pw_hi, 1)
            act.wait_ge(d_rw, 16)
            nc.scalar.activation(RWH[:], RW[:], ACT.Copy).then_inc(pw_hi, 1)

            def c_high(b):
                if has(b, 1):
                    act.wait_ge(kv_ps, b)
                    act.wait_ge(c_lo, b)
                else:
                    act.wait_ge(d_ctx, 16)
                nc.scalar.activation(CH[:], CTX[:, bass.ds(b * P, P)], ACT.Copy).then_inc(c_hi, 1)

            def hT_high(b):
                act.wait_ge(hT_ps, b + 1)
                if has(b, 1):
                    act.wait_ge(q_ps, b)
                    act.wait_ge(hT_lo, b)
                nc.scalar.activation(HTH[:], HBANK[:, 0:D], ACT.Copy).then_inc(hT_hi, 1)

            def v_copy(b, par):
                act.wait_ge(k_terms, 3 * (b + 1))
                if has(b, 2):
                    act.wait_ge(av_ps, UNITS * (b - 1))
                if isinstance(b, int):
                    act.wait_ge(zeroed, 5)
                nc.scalar.activation(VA[:, par].rearrange("p n (s c) -> p n s c", s=2)[:, :, :, 0:HD],
                                     TBANK[:, D:2 * D].rearrange("p (n s c) -> p n s c", s=2, c=HD),
                                     ACT.Copy).then_inc(v_done, 1)

            def k_evac(b):
                act.wait_ge(kT_ps, b + 1)
                if has(b, 1):
                    act.wait_ge(kp_dma, 16 * QUAD * b)
                nc.scalar.activation(KT[:], TB16, ACT.Copy).then_inc(kT_sb, 1)

            def qm_evac(b):
                act.wait_ge(qmT_ps, b + 1)
                if has(b, 1):
                    act.wait_ge(p2_ps, UNITS * b)
                nc.scalar.activation(QTB[:].rearrange("p g n -> p (g n)"), TB16, ACT.Copy).then_inc(qmT_sb, 1)

            def exps(b, u):
                act.wait_ge(p2_ps, UNITS * b + u + 1)
                if has(b, 1) or u >= 2:
                    act.wait_ge(av_ps, UNITS * b + u - 1)
                nc.scalar.activation(E[:, u % 2, :], LBANK[u % 2], ACT.Exp, scale=SCALE).then_inc(exp_done, 1)

            def o_evac(b):
                act.wait_ge(av_ps, UNITS * (b + 1))
                if has(b, 1):
                    act.wait_ge(oT_ps, b)
                nc.scalar.activation(OS[:], OBANK, ACT.Copy).then_inc(o_sb, 1)

            def a_high(b):
                act.wait_ge(aT_ps, b + 1)
                if has(b, 1):
                    act.wait_ge(proj_ps, b)
                    act.wait_ge(a_lo, b)
                nc.scalar.activation(ATH[:], YBANK[:, 0:D], ACT.Copy).then_inc(a_hi, 1)

            def h2_high(b):
                act.wait_ge(h2T_ps, b + 1)
                if has(b, 1):
                    act.wait_ge(rt_ps, b)
                    act.wait_ge(h2_dma, 32 * b)
                    act.wait_ge(h2_lo, b)
                nc.scalar.activation(T2H[:], YBANK[:, 0:D], ACT.Copy).then_inc(h2_hi, 1)

            def prologue():
                c_high(0)
                hT_high(0)
                v_copy(0, 0)
                k_evac(0)
                qm_evac(0)

            def step(i, par, first, last):
                f, b, t = i + 1, i, i - 1
                if not last:
                    c_high(f)
                    hT_high(f)
                exps(b, 0)
                if not last:
                    v_copy(f, 1 - par)
                exps(b, 1)
                if not first:
                    a_high(t)
                exps(b, 2)
                if not last:
                    k_evac(f)
                exps(b, 3)
                if not first:
                    h2_high(t)
                o_evac(b)
                if not last:
                    qm_evac(f)

            def router(lo, hi, rp, ra):
                s = slice(lo, hi)
                act.wait_ge(rt_sb, hi)
                act.wait_ge(inv_temp, 2)
                nc.scalar.activation(RT[:, 0, s, :], LG[:, s, :], ACT.Tanh, scale=HIT[:, 1:2]).then_inc(r_act, 1)
                act.wait_ge(r_pool, rp + 5)
                nc.scalar.activation(RT[:, 2, s, :], RT[:, 1, s, :], ACT.Abs).then_inc(r_act, 1)
                act.wait_ge(r_act, ra + 2)
                nc.scalar.activation(RT[:, 5, s, :], RT[:, 2, s, :], ACT.Exp, scale=-1.0 / 0.1).then_inc(r_act, 1)
                nc.scalar.activation(RT[:, 6, s, :], RT[:, 2, s, :], ACT.Exp, scale=-1.0 / 0.3).then_inc(r_act, 1)

            def epilogue():
                router(0, B - 2, 0, 0)
                a_high(B - 1)
                h2_high(B - 1)
                router(B - 2, B, 21, 4)

            pipeline(act, prologue, step, epilogue)

            def silu(n, c):
                act.wait_ge(g_ps, FK * n + c + 1)
                if has(n, 1):
                    act.wait_ge(m_done, FK * (n - 1) + c + 1)
                nc.scalar.activation(SIL[:, c, :], PS[:, c, :], ACT.Silu).then_inc(silu_done, 1)

            def mid_high(n, c, par):
                act.wait_ge(m_done, FK * n + c + 1)
                if has(n, 2):
                    act.wait_ge(d_ps, n - 1)
                    act.wait_ge(ml_done, FK * (n - 2) + c + 1)
                nc.scalar.activation(MH[:, par, c, :], MID[:, c, :], ACT.Copy).then_inc(mh_done, 1)

            def group(n, par):
                for c in range(FK):
                    silu(n, c)
                for c in range(FK):
                    mid_high(n, c, par)

            group(0, 0)
            group(1, 1)
            with act.Fori(2, NE * NG, 2) as n:
                n = act.snap(n)
                group(n, 0)
                group(n + 1, 1)

        @block.vector
        def _(dve):
            dve.wait_ge(d_pos, 16)
            posv = POS[:].rearrange("p b c -> p (b c)")
            for n in range(2):
                nc.vector.tensor_scalar(ANG[:, 0, :, n], posv, FREQ[n], None, ALU.mult).then_inc(angles, 1)
            dve.wait_ge(angles, 2)
            flat = ANG[:].rearrange("p a b c -> p a (b c)")
            nc.vector.tensor_scalar(flat[:, 1, :], flat[:, 0, :], math.pi / 2, None, ALU.add).then_inc(angles, 1)
            dve.wait_ge(angles, 3)
            nc.vector.tensor_scalar(TURN[:], flat, 1.0 / TWO_PI, ROUND, ALU.mult, ALU.add).then_inc(angles, 1)
            dve.wait_ge(angles, 4)
            nc.vector.tensor_scalar(TURN[:], TURN[:], ROUND, None, ALU.subtract).then_inc(angles, 1)
            dve.wait_ge(angles, 5)
            nc.vector.scalar_tensor_tensor(flat, TURN[:], -PI2_HI, flat, ALU.mult, ALU.add).then_inc(angles, 1)
            dve.wait_ge(angles, 6)
            nc.vector.scalar_tensor_tensor(flat, TURN[:], -PI2_LO, flat, ALU.mult, ALU.add).then_inc(angles, 1)
            dve.wait_ge(angles, 7)
            nc.vector.tensor_scalar(flat, flat, 3.1415925, -3.1415925, ALU.min, ALU.max).then_inc(angles, 1)
            dve.wait_ge(d_gate, 48)
            nc.vector.reciprocal(HIT[:, 0:1], TEMP[:]).then_inc(inv_temp, 1)
            dve.wait_ge(inv_temp, 1)
            nc.vector.tensor_scalar(HIT[:, 1:2], HIT[:, 0:1], 0.5, None, ALU.mult).then_inc(inv_temp, 1)
            for b in range(B):
                if b % 4 == 0:
                    dve.wait_ge(d_x[b // 4], 16)
                nc.vector.bn_stats(ST1[:, b, :], X[:, b, :]).then_inc(stats1, 1)
            for b in range(B):
                dve.wait_ge(stats1, b + 1)
                nc.vector.bn_aggr(MV1[:, b, :], ST1[:, b, :]).then_inc(stats1, 1)
            dve.wait_ge(stats1, 2 * B)
            v1 = NW1[:, 0, :]
            nc.vector.tensor_scalar(v1, MV1[:, :, 1], EPS, None, ALU.add).then_inc(guess1, 1)
            dve.wait_ge(guess1, 1)
            nc.vector.tensor_scalar(NW1[:, 1, :].bitcast(I32), v1.bitcast(I32), 1, None,
                                    ALU.arith_shift_right).then_inc(guess1, 1)
            dve.wait_ge(guess1, 2)
            nc.vector.tensor_scalar(RS1[:].bitcast(I32), NW1[:, 1, :].bitcast(I32), -1.0, float(0x5f3759df),
                                    ALU.mult, ALU.add).then_inc(guess1, 1)
            dve.wait_ge(trig, 1)
            nc.vector.tensor_scalar(TRIG[:, 2], TRIG[:, 0], -1.0, None, ALU.mult).then_inc(neg_sin, 1)

            def norm1(b):
                dve.wait_ge(rstd1, 12)
                if has(b, 1):
                    dve.wait_ge(hT_ps, b)
                nc.vector.tensor_scalar(H[:].unsqueeze(1), X[:, bass.ds(b, 1), :], MV1[:, bass.ds(b, 1), 0],
                                        RS1[:, bass.ds(b, 1)], ALU.subtract, ALU.mult).then_inc(h_ready, 1)

            def hT_low(b):
                dve.wait_ge(hT_hi, b + 1)
                if has(b, 1):
                    dve.wait_ge(q_ps, b)
                nc.vector.tensor_tensor(HTL[:], HBANK[:, 0:D], HTH[:].bitcast(F32), ALU.subtract).then_inc(hT_lo, 1)

            def rope(b, bank, ready, ta, tb, rot, terms):
                dve.wait_ge(ready, b + 1)
                if has(b, 1):
                    dve.wait_ge(rot, b)
                src = bank.rearrange("p (h a c) -> p h a c", h=HEADS, a=4)
                da = ta[:].rearrange("p (h a c) -> p h a c", h=HEADS, a=4)
                db = tb[:].rearrange("p (h a c) -> p h a c", h=HEADS, a=4)
                sin, cos, nsin = [TRIG[:, k, bass.ds(b, 1), :] for k in range(3)]
                nc.vector.tensor_tensor(da, src, cos.unsqueeze(3).to_broadcast([P, HEADS, 4, 2]),
                                        ALU.mult).then_inc(terms, 1)
                nc.vector.tensor_tensor(db[:, :, :, 0], src[:, :, :, 1], nsin.to_broadcast([P, HEADS, 4]),
                                        ALU.mult).then_inc(terms, 1)
                nc.vector.tensor_tensor(db[:, :, :, 1], src[:, :, :, 0], sin.to_broadcast([P, HEADS, 4]),
                                        ALU.mult).then_inc(terms, 1)

            def high16(b, rot, S, gap, done, hi, free):
                dve.wait_ge(done, b + 1)
                if has(b, 1):
                    dve.wait_ge(free, b)
                else:
                    dve.wait_ge(zeroed, 4)
                src = rot[:].rearrange("p (h d) -> p h d", d=HD).unsqueeze(2).to_broadcast([P, HEADS, 2, HD])
                dst = S[:, :, 0:2 * gap].rearrange("p h (r d) -> p h r d", r=2)[:, :, :, 0:HD]
                nc.vector.tensor_copy(dst, src).then_inc(hi, 1)

            def q_evac(b):
                dve.wait_ge(qT_ps, b + 1)
                if has(b, 1):
                    dve.wait_ge(p1_ps, UNITS * b)
                nc.vector.tensor_copy(QTA[:].rearrange("p g n -> p (g n)"), TB16).then_inc(qT_sb, 1)

            def row_max(b, u):
                dve.wait_ge(p1_ps, UNITS * b + u + 1)
                nc.vector.tensor_reduce(QS[:, UH * u:UH * (u + 1), 24],
                                        LBANK[u % 2].rearrange("p (h n) -> p h n", h=UH),
                                        AX_X, ALU.max).then_inc(max_done, 1)

            def divide(b):
                dve.wait_ge(oT_ps, b + 1)
                o = YBANK.rearrange("p (n c) -> p n c", c=ROWS)
                if has(b, 1):
                    dve.wait_ge(attn, b)
                nc.vector.reciprocal(RSUM[:], o[:, :, 16:18]).then_inc(sums_inv, 1)
                dve.wait_ge(sums_inv, b + 1)
                if has(b, 1):
                    dve.wait_ge(aT_ps, b)
                nc.vector.tensor_tensor(AT[:].rearrange("p (n s c) -> p n s c", s=2, c=HD),
                                        o[:, :, 0:16].rearrange("p n (s c) -> p n s c", s=2),
                                        RSUM[:].unsqueeze(3).to_broadcast([P, HEADS // 2, 2, HD]),
                                        ALU.mult).then_inc(attn, 1)

            def a_low(b):
                dve.wait_ge(a_hi, b + 1)
                nc.vector.tensor_tensor(ATL[:], YBANK[:, 0:D], ATH[:].bitcast(F32), ALU.subtract).then_inc(a_lo, 1)

            def residual(b):
                dve.wait_ge(proj_ps, b + 1)
                dve.wait_ge(xb_done, b + 1)
                nc.vector.scalar_tensor_tensor(X[:, bass.ds(b, 1), :], YBANK[:, 0:D].unsqueeze(1), TG2[:, 0:1],
                                               X[:, bass.ds(b, 1), :], ALU.mult, ALU.add).then_inc(x1_done, 1)

            def stats2(b):
                dve.wait_ge(x1_done, b + 1)
                if has(b, 1):
                    dve.wait_ge(h2_ready, b)
                    dve.wait_ge(ln2, LN2 * b)
                nc.vector.memset(TICK[:], 0.0).then_inc(ln2, 1)
                nc.vector.bn_stats(ST2[:].unsqueeze(1), X[:, bass.ds(b, 1), :]).then_inc(ln2, 1)
                dve.wait_ge(ln2, LN2 * b + 2)
                nc.vector.memset(TICK[:], 0.0).then_inc(ln2, 1)
                nc.vector.bn_aggr(MV2[:], ST2[:]).then_inc(ln2, 1)
                dve.wait_ge(ln2, LN2 * b + 4)
                if has(b, 1):
                    dve.wait_ge(newton2, NEWTON * b)
                nc.vector.tensor_scalar(NW2[:, 0:1], MV2[:, 1:2], EPS, None, ALU.add).then_inc(ln2, 1)
                dve.wait_ge(ln2, LN2 * b + 5)
                nc.vector.tensor_scalar(NW2[:, 1:2].bitcast(I32), NW2[:, 0:1].bitcast(I32), 1, None,
                                        ALU.arith_shift_right).then_inc(ln2, 1)
                nc.vector.tensor_scalar(NW2[:, 4:5], NW2[:, 0:1], -0.5, None, ALU.mult).then_inc(ln2, 1)
                dve.wait_ge(ln2, LN2 * b + 7)
                nc.vector.tensor_scalar(NW2[:, 2:3].bitcast(I32), NW2[:, 1:2].bitcast(I32), -1.0,
                                        float(0x5f3759df), ALU.mult, ALU.add).then_inc(ln2, 1)

            def norm2(b):
                dve.wait_ge(newton2, NEWTON * (b + 1))
                if has(b, 1):
                    dve.wait_ge(h2T_ps, b)
                nc.vector.tensor_scalar(H2[:].unsqueeze(1), X[:, bass.ds(b, 1), :], MV2[:, 0:1], NW2[:, 2:3],
                                        ALU.subtract, ALU.mult).then_inc(h2_ready, 1)

            def h2_low(b):
                dve.wait_ge(h2_hi, b + 1)
                nc.vector.tensor_tensor(T2L[:], YBANK[:, 0:D], T2H[:].bitcast(F32), ALU.subtract).then_inc(h2_lo, 1)

            def logits_evac(b):
                dve.wait_ge(rt_ps, b + 1)
                nc.vector.tensor_copy(LG[:, bass.ds(b, 1), :], YBANK[:, 0:NE].unsqueeze(1)).then_inc(rt_sb, 1)

            def add_lora(e):
                dve.wait_ge(d_ws[e], 16)
                for n in range(3):
                    dve.wait_ge(lora_ps, 3 * e + n + 1)
                    w = WS[:, e, 512 * n:512 * (n + 1)]
                    nc.vector.tensor_tensor(w, w, PS[:, 3 * e + n, :], ALU.add).then_inc(lora_added, 1)

            def prologue():
                dve.wait_ge(neg_sin, 1)
                add_lora(0)
                add_lora(1)
                norm1(0)
                hT_low(0)
                rope(0, TBANK[:, 0:D], kv_ps, KA, KB, k_rot, k_terms)
                rope(0, HBANK[:, D:2 * D], q_ps, QA, QB, q_rot, q_terms)
                high16(0, KR, KS, 2 * HD, k_rot, k_hi, kT_ps)
                high16(0, QR, QS, HD, q_rot, q_hi, qmT_ps)
                q_evac(0)
                for u in range(UNITS):
                    row_max(0, u)

            def step(i, par, first, last):
                f, b, t = i + 1, i, i - 1
                if not last:
                    norm1(f)
                if not first:
                    divide(t)
                if not last:
                    hT_low(f)
                if not last:
                    rope(f, TBANK[:, 0:D], kv_ps, KA, KB, k_rot, k_terms)
                    rope(f, HBANK[:, D:2 * D], q_ps, QA, QB, q_rot, q_terms)
                if not first:
                    a_low(t)
                if not last:
                    high16(f, KR, KS, 2 * HD, k_rot, k_hi, kT_ps)
                    high16(f, QR, QS, HD, q_rot, q_hi, qmT_ps)
                if not first:
                    residual(t)
                    stats2(t)
                if not last:
                    q_evac(f)
                if not first:
                    norm2(t)
                if not last:
                    row_max(f, 0)
                if not first:
                    h2_low(t)
                if not last:
                    row_max(f, 1)
                if not first:
                    logits_evac(t)
                if not last:
                    row_max(f, 2)
                    row_max(f, 3)

            def router(lo, hi, rp, rd):
                s = slice(lo, hi)
                tmp, e3, w = RT[:, 4, s, :], RT[:, 6, s, :], RT[:, 7, s, :]
                wsum, fsum, raw = RV[:, 0, s], RV[:, 3, s], RV[:, 4, s]
                dve.wait_ge(r_pool, rp + 10)
                nc.vector.tensor_reduce(tmp, RC[:, 0, s], AX_X, ALU.add).then_inc(r_dve, 1)
                dve.wait_ge(r_pool, rp + 13)
                nc.vector.tensor_reduce(wsum, w, AX_X, ALU.add).then_inc(r_dve, 1)
                nc.vector.tensor_reduce(raw, e3, AX_X, ALU.add).then_inc(r_dve, 1)
                dve.wait_ge(r_dve, rd + 3)
                nc.vector.tensor_scalar(raw, raw, 1e-8, None, ALU.max).then_inc(r_dve, 1)
                dve.wait_ge(r_dve, rd + 4)
                nc.vector.reciprocal(fsum, raw).then_inc(r_dve, 1)
                dve.wait_ge(r_pool, rp + 19)
                dve.wait_ge(r_dve, rd + 5)
                nc.vector.tensor_reduce(raw, w, AX_X, ALU.add).then_inc(r_dve, 1)
                dve.wait_ge(r_dve, rd + 6)
                nc.vector.tensor_scalar(raw, raw, 1e-8, None, ALU.max).then_inc(r_dve, 1)
                dve.wait_ge(r_dve, rd + 7)
                nc.vector.reciprocal(wsum, raw).then_inc(r_dve, 1)

            def epilogue():
                t = B - 1
                divide(t)
                a_low(t)
                residual(t)
                stats2(t)
                router(0, B - 2, 0, 0)
                norm2(t)
                h2_low(t)
                logits_evac(t)
                router(B - 2, B, 21, 8)

            pipeline(dve, prologue, step, epilogue)

            def mid(n, par):
                for c in range(FK):
                    dve.wait_ge(silu_done, FK * n + c + 1)
                    dve.wait_ge(u_ps, FK * n + c + 1)
                    if has(n, 1):
                        dve.wait_ge(mh_done, FK * (n - 1) + c + 1)
                        dve.wait_ge(ml_done, FK * (n - 1) + c + 1)
                    nc.vector.tensor_tensor(MID[:, c, :], SIL[:, c, :], PS[:, 2 + c, :], ALU.mult).then_inc(m_done, 1)
                for c in range(FK):
                    dve.wait_ge(mh_done, FK * n + c + 1)
                    if has(n, 2):
                        dve.wait_ge(d_ps, n - 1)
                    nc.vector.tensor_tensor(ML[:, par, c, :], MID[:, c, :], MH[:, par, c, :].bitcast(F32),
                                            ALU.subtract).then_inc(ml_done, 1)

            def accumulate(n, e, g, par):
                dve.wait_ge(d_ps, n + 1)
                if has(n, NG):
                    dve.wait_ge(acc_done, CREDIT + TG * (n - NG + 1))
                else:
                    dve.wait_ge(r_pool, 42 if g == NG - 1 else 21)
                for k in range(TG):
                    tile = TG * g + k
                    o = PS[:, 4 + 2 * par:6 + 2 * par, :].rearrange("p a (c d) -> p (a c) d", c=2)[:, k, :]
                    nc.vector.scalar_tensor_tensor(X[:, tile, :], o, WT[:, tile, bass.ds(e, 1)], X[:, tile, :],
                                                   ALU.mult, ALU.add).then_inc(acc_done, 1)

            mid(0, 0)
            for g in range(NG):
                mid(g + 1, (g + 1) % 2)
                accumulate(g, 0, g, g % 2)
            with dve.Fori(1, NE - 1, 1) as e:
                e = dve.snap(e)
                for g in range(NG):
                    mid(e * NG + (g + 1), (g + 1) % 2)
                    accumulate(e * NG + g, e, g, g % 2)
            for g in range(NG):
                n = NG * (NE - 1) + g
                if g < NG - 1:
                    mid(n + 1, (g + 1) % 2)
                accumulate(n, NE - 1, g, g % 2)

        @block.tensor
        def _(pe):
            mm = nc.tensor.matmul
            pe.wait_ge(d_lora, 16 * 6)
            for e in range(NL):
                for n in range(3):
                    for k in range(DK):
                        last = mm(PS[:, 3 * e + n, F * k:F * (k + 1)], LORA_A[:, n, e, P * k:P * (k + 1)],
                                  LORA_B[:, n, e, :], start=True, stop=True)
                    last.then_inc(lora_ps, 1)

            def product(dst, pairs):
                last = None
                ops = []
                for (sh, sl), (mh, ml) in pairs:
                    ops += [(sh, mh), (sh, ml), (sl, mh)]
                for n, (s, m) in enumerate(ops):
                    last = mm(dst, s, m, start=n == 0, stop=n == len(ops) - 1)
                return last

            def transpose_h(b):
                pe.wait_ge(h_ready, b + 1)
                if has(b, 1):
                    pe.wait_ge(q_terms, 3 * b)
                else:
                    pe.wait_ge(d_const, 16 * 4)
                for k in range(DK):
                    last = nc.tensor.transpose(HBANK[:, P * k:P * (k + 1)], H[:, P * k:P * (k + 1)], ID[:])
                last.then_inc(hT_ps, 1)

            def project_kv(b):
                pe.wait_ge(c_lo, b + 1)
                if has(b, 1):
                    pe.wait_ge(qmT_sb, b)
                else:
                    pe.wait_ge(pw_lo, 3)
                    pe.wait_ge(lora_added, 5)
                product(TBANK, [((CH[:], CL[:]), (PWH[:, 1, :], PWL[:, 1, :]))]).then_inc(kv_ps, 1)

            def project_q(b):
                pe.wait_ge(hT_lo, b + 1)
                if not has(b, 1):
                    pe.wait_ge(pw_lo, 1)
                product(HBANK[:, D:2 * D],
                        [((HTH[:, P * k:P * (k + 1)], HTL[:, P * k:P * (k + 1)]),
                          (PWH[:, 0, D * k:D * (k + 1)], PWL[:, 0, D * k:D * (k + 1)]))
                         for k in range(DK)]).then_inc(q_ps, 1)

            def transpose16(S, done):
                for g in range(GROUPS):
                    last = nc.tensor.transpose(TB16[:, P * g:P * (g + 1)],
                                               S[:, QUAD * g:QUAD * (g + 1), :].rearrange("p h r -> p (h r)"), ID16[:])
                last.then_inc(done, 1)

            def transpose_k(b):
                pe.wait_ge(k_lo, b + 1)
                pe.wait_ge(v_done, b + 1)
                pe.wait_ge(k_terms, 3 * (b + 1))
                transpose16(KS, kT_ps)

            def transpose_q(b):
                pe.wait_ge(q_lo, b + 1)
                pe.wait_ge(m_zero, b + 1)
                pe.wait_ge(kT_sb, b + 1)
                transpose16(QS, qT_ps)

            def logits(b, u, par):
                if u == 0:
                    pe.wait_ge(kp_dma, 16 * QUAD * (b + 1))
                    pe.wait_ge(qT_sb, b + 1)
                if u >= 2:
                    pe.wait_ge(max_done, UNITS * b + u - 1)
                elif has(b, 1):
                    pe.wait_ge(exp_done, UNITS * (b - 1) + u + 3)
                elif u == 0:
                    pe.wait_ge(lora_added, 6)
                for j in range(UH // QUAD):
                    g = (UH // QUAD) * u + j
                    last = mm(LBANK[u % 2][:, 512 * j:512 * (j + 1)].rearrange("p (a n) -> p a n", a=QUAD),
                              QTA[:, g, :], KP[:, par, :, g, :], start=True, stop=True)
                last.then_inc(p1_ps, 1)

            def transpose_qm(b):
                pe.wait_ge(max_done, UNITS * (b + 1))
                pe.wait_ge(qT_sb, b + 1)
                transpose16(QS, qmT_ps)

            def logits_t(b, u, par):
                if u == 0:
                    pe.wait_ge(qmT_sb, b + 1)
                if u >= 2:
                    pe.wait_ge(exp_done, UNITS * b + u - 1)
                else:
                    pe.wait_ge(max_done, UNITS * b + u + 3)
                for n in range(UH):
                    g, j = divmod(UH * u + n, QUAD)
                    last = mm(LBANK[u % 2][:, P * n:P * (n + 1)], KP[:, par, j, g, :], QTB[:, g, :],
                              start=True, stop=True)
                last.then_inc(p2_ps, 1)

            def attend(b, u, par):
                pe.wait_ge(exp_done, UNITS * b + u + 1)
                if u == 0:
                    pe.wait_ge(v_done, b + 1)
                    if has(b, 1):
                        pe.wait_ge(o_sb, b)
                for s in range(2):
                    for c in range(4):
                        pair = 4 * u + c
                        last = mm(OBANK[32 * c:32 * (c + 1), P * u:P * (u + 1)],
                                  VA[:, par, pair, 32 * s:32 * (s + 1)],
                                  E[:, u % 2, P * (2 * c + s):P * (2 * c + s + 1)],
                                  start=s == 0, stop=s == 1)
                last.then_inc(av_ps, 1)

            def transpose_o(b):
                pe.wait_ge(o_sb, b + 1)
                if has(b, 1):
                    pe.wait_ge(rt_sb, b)
                for r in range(4):
                    last = nc.tensor.transpose(YBANK[:, P * r:P * (r + 1)], OS[:, P * r:P * (r + 1)], ID[:])
                last.then_inc(oT_ps, 1)

            def transpose_a(b):
                pe.wait_ge(attn, b + 1)
                for k in range(DK):
                    last = nc.tensor.transpose(YBANK[:, P * k:P * (k + 1)], AT[:, P * k:P * (k + 1)], ID[:])
                last.then_inc(aT_ps, 1)

            def project_o(b):
                pe.wait_ge(a_lo, b + 1)
                product(YBANK[:, 0:D],
                        [((ATH[:, P * k:P * (k + 1)], ATL[:, P * k:P * (k + 1)]),
                          (PWH[:, 2, D * k:D * (k + 1)], PWL[:, 2, D * k:D * (k + 1)]))
                         for k in range(DK)]).then_inc(proj_ps, 1)

            def transpose_h2(b):
                pe.wait_ge(h2_ready, b + 1)
                for k in range(DK):
                    last = nc.tensor.transpose(YBANK[:, P * k:P * (k + 1)], H2[:, P * k:P * (k + 1)], ID[:])
                last.then_inc(h2T_ps, 1)

            def router(b):
                pe.wait_ge(h2_lo, b + 1)
                if not has(b, 1):
                    pe.wait_ge(pw_lo, 4)
                product(YBANK[:, 0:NE],
                        [((T2H[:, P * k:P * (k + 1)], T2L[:, P * k:P * (k + 1)]), (RWH[:, k, :], RWL[:, k, :]))
                         for k in range(DK)]).then_inc(rt_ps, 1)

            def prologue():
                transpose_h(0)
                project_kv(0)
                project_q(0)
                transpose_k(0)
                transpose_q(0)
                for u in range(UNITS):
                    logits(0, u, 0)
                transpose_qm(0)

            def step(i, par, first, last):
                f, b, t = i + 1, i, i - 1
                if not first:
                    transpose_o(t)
                logits_t(b, 0, par)
                if not last:
                    transpose_h(f)
                if not last:
                    project_kv(f)
                    project_q(f)
                logits_t(b, 1, par)
                if not first:
                    transpose_a(t)
                logits_t(b, 2, par)
                attend(b, 0, par)
                if not first:
                    project_o(t)
                logits_t(b, 3, par)
                attend(b, 1, par)
                if not last:
                    transpose_k(f)
                attend(b, 2, par)
                if not last:
                    transpose_q(f)
                if not first:
                    transpose_h2(t)
                attend(b, 3, par)
                if not last:
                    logits(f, 0, 1 - par)
                if not first:
                    router(t)
                if not last:
                    for u in range(1, UNITS):
                        logits(f, u, 1 - par)
                    transpose_qm(f)

            def epilogue():
                transpose_o(B - 1)
                transpose_a(B - 1)
                project_o(B - 1)
                transpose_h2(B - 1)
                router(B - 1)

            pipeline(pe, prologue, step, epilogue)

            def gate_up(n, g, slot):
                for c in range(FK):
                    for part, base, done in ((0, 0, g_ps), (1, 2, u_ps)):
                        if has(n, 1):
                            if part == 0:
                                pe.wait_ge(silu_done, FK * (n - 1) + c + 1)
                            else:
                                pe.wait_ge(m_done, FK * (n - 1) + c + 1)
                        cols = [slice(512 * part + F * k + P * c, 512 * part + F * k + P * (c + 1)) for k in range(DK)]
                        product(PS[:, base + c, :],
                                [((WH[:, slot, cols[k]], WL[:, slot, cols[k]]),
                                  (H2H[:, k, GT * g:GT * (g + 1)], H2L[:, k, GT * g:GT * (g + 1)]))
                                 for k in range(DK)]).then_inc(done, 1)

            def down(n, slot, par):
                pe.wait_ge(ml_done, FK * (n + 1))
                pe.wait_ge(acc_done, TG * (n + 1))
                for k in range(TG):
                    bank = PS[:, 4 + 2 * par + k // 2, D * (k % 2):D * (k % 2 + 1)]
                    t = slice(P * k, P * (k + 1))
                    last = product(bank, [((MH[:, par, c, t], ML[:, par, c, t]),
                                           (WH[:, slot, 1024 + D * c:1024 + D * (c + 1)],
                                            WL[:, slot, 1024 + D * c:1024 + D * (c + 1)])) for c in range(FK)])
                last.then_inc(d_ps, 1)

            def weights(e):
                pe.wait_ge(wl_done, 3 * (e + 1))

            def pair_of_experts(e, final):
                for s in range(2):
                    for g in range(NG):
                        n = NG * (e + s) + g
                        nxt = NG * s + g + 1
                        if not (final and nxt == 2 * NG):
                            if nxt % NG == 0:
                                weights(e + s + 1)
                            gate_up(n + 1, nxt % NG, (nxt // NG) % 2)
                        down(n, s, g % 2)

            pe.wait_ge(h2_dma, 32 * B)
            pe.wait_ge(exp_done, UNITS * B)
            pe.wait_ge(max_done, UNITS * B)
            pe.wait_ge(o_sb, B)
            pe.wait_ge(rt_sb, B)
            pe.wait_ge(qmT_sb, B)
            pe.wait_ge(q_terms, 3 * B)
            pe.sem_inc(acc_done, CREDIT)
            weights(0)
            gate_up(0, 0, 0)
            with pe.Fori(0, NE - 2, 2) as e:
                e = pe.snap(e)
                pair_of_experts(e, False)
            pair_of_experts(NE - 2, True)


def kernel(x, ctx_1024, fside_BxSx2_0, g_xattn, g_ffn, L0_xattn_Wq, L0_xattn_Wkv, L0_xattn_Wout, L0_xattn_bout,
           L0_ffn_Wg, L0_ffn_Wu, L0_ffn_Wd, L0_ffn_Ga, L0_ffn_Gb, L0_ffn_Ua, L0_ffn_Ub, L0_ffn_Da, L0_ffn_Db,
           L0_ffn_Wr, L0_ffn_temperature):
    import numpy as np
    import concourse.bacc as bacc
    from concourse import mybir as _mybir
    from concourse.bass_utils import run_bass_kernel_spmd

    def rows(w):
        w = np.asarray(w)
        e, r, n = w.shape
        return w.reshape(e, r // 128, 128, n).transpose(0, 2, 1, 3).reshape(e, 128, -1)

    arrays = {
        "x": np.asarray(x),
        "ctxT": np.asarray(ctx_1024).transpose(2, 0, 1).reshape(ctx_1024.shape[2], -1),
        "pos": np.asarray(fside_BxSx2_0),
        "g_xattn": np.asarray(g_xattn), "g_ffn": np.asarray(g_ffn),
        "Wq": np.asarray(L0_xattn_Wq), "Wkv": np.asarray(L0_xattn_Wkv),
        "Wout": np.asarray(L0_xattn_Wout), "bout": np.asarray(L0_xattn_bout),
        "Wexp": np.concatenate([rows(L0_ffn_Wg), rows(L0_ffn_Wu), rows(L0_ffn_Wd)], axis=2),
        "GaT": np.asarray(L0_ffn_Ga).transpose(0, 2, 1), "Gb": np.asarray(L0_ffn_Gb),
        "UaT": np.asarray(L0_ffn_Ua).transpose(0, 2, 1), "Ub": np.asarray(L0_ffn_Ub),
        "DaT": np.asarray(L0_ffn_Da).transpose(0, 2, 1), "Db": np.asarray(L0_ffn_Db),
        "Wr": np.asarray(L0_ffn_Wr), "temperature": np.asarray(L0_ffn_temperature),
        "ident": np.eye(128, dtype=np.float32),
        "ident16": np.eye(128, dtype=np.float16),
        "lower_tri": np.broadcast_to(np.tril(np.ones((8, 8), np.float32), -1), (128, 8, 8)),
    }
    nc = bacc.Bacc("TRN2", target_bir_lowering=False, num_devices=1)
    arrays = {f"in_{k}": np.ascontiguousarray(a) for k, a in arrays.items()}
    args = [nc.dram_tensor(k, a.shape, _mybir.dt.from_np(a.dtype), kind="ExternalInput").ap()
            for k, a in arrays.items()]
    out = nc.dram_tensor("out", x.shape, _mybir.dt.from_np(np.dtype("float32")), kind="ExternalOutput").ap()
    flamingo_kernel(nc, *args, out)
    r = run_bass_kernel_spmd(nc, [arrays], core_ids=[0])
    return r.results[0]["out"]
```

```python
import math
from contextlib import ExitStack

import concourse.bass as bass
from concourse import mybir

F32 = mybir.dt.float32
F32R = mybir.dt.float32r
F16 = mybir.dt.float16
I32 = mybir.dt.int32
ALU = mybir.AluOpType
ACT = mybir.ActivationFunctionType
AX_X = mybir.AxisListType.X

P = 128


def has(b, back):
    return not isinstance(b, int) or b >= back


def flamingo_kernel(nc, x, ctxT, pos, g_xattn, g_ffn, Wq, Wkv, Wout, bout, Wexp, GaT, Gb, UaT, Ub, DaT, Db,
                    Wr, temperature, ident, ident16, lower_tri, out):
    B, T, D = x.shape
    DK = D // P
    HEADS, HD = 32, 8
    QUAD = 4
    GROUPS = HEADS // QUAD
    ROWS = P // QUAD
    UNITS = 8
    UH = HEADS // UNITS
    AV = UNITS // 2
    NE, WCOLS = Wexp.shape[0], Wexp.shape[2]
    F = WCOLS // (3 * DK)
    FK = F // P
    NL, R = GaT.shape[0], GaT.shape[1]
    TG = 4
    NG = B // TG
    GT = TG * P
    SCALE = 1.0 / math.sqrt(HD)
    EPS = 1e-5
    TWO_PI = 2.0 * math.pi
    PI2_HI = 6.28125
    PI2_LO = TWO_PI - PI2_HI
    ROUND = 1.5 * 2.0 ** 23
    FREQ = [1.0, 10000.0 ** -0.5]
    LOWER, UPPER, CENTER = 0.5 - math.log(4.0 / 3.0), 0.5, 1.0 / math.e
    assert T == P and D == HEADS * HD and WCOLS == 6 * 256 and NL == 2 and B % 4 == 0

    ctx = ExitStack()
    with ctx:
        def sb(name, shape, dt=F32):
            return ctx.enter_context(nc.sbuf_tensor(name, shape, dt))

        def sem(name):
            return ctx.enter_context(nc.semaphore(name))

        X = sb("X", [P, B, D])
        H2H = sb("H2H", [P, DK, B * P], F32R)
        H2L = sb("H2L", [P, DK, B * P], F32R)
        WH = sb("WH", [P, 2, WCOLS], F32R)
        WL = sb("WL", [P, 2, WCOLS], F32R)
        WS = sb("WS", [P, 2, WCOLS])
        LG = sb("LG", [P, B, NE])
        WT = sb("WT", [P, B, NE])
        ID = sb("ID", [P, P])
        ID16 = sb("ID16", [P, P], F16)
        TRI = sb("TRI", [P, NE, NE])
        GATE = sb("GATE", [P, 2])
        TG2 = sb("TG2", [P, 2])
        TEMP = sb("TEMP", [P, 1])
        HIT = sb("HIT", [P, 2])
        BOUT = sb("BOUT", [P, D])
        TGB = sb("TGB", [P, D])
        PW = sb("PW", [P, 3, 512])
        PWH = sb("PWH", [P, 3, 512], F32R)
        PWL = sb("PWL", [P, 3, 512], F32R)
        RW = sb("RW", [P, DK, NE])
        RWH = sb("RWH", [P, DK, NE], F32R)
        RWL = sb("RWL", [P, DK, NE], F32R)
        POS = sb("POS", [P, B, 2])
        ANG = sb("ANG", [P, 2, B * 2, 2])
        TURN = sb("TURN", [P, 2, B * 4])
        TRIG = sb("TRIG", [P, 3, B, 4])
        ST1 = sb("ST1", [P, B, 6])
        MV1 = sb("MV1", [P, B, 2])
        RS1 = sb("RS1", [P, B])
        NW1 = sb("NW1", [P, 3, B])
        CTX = sb("CTX", [P, B * P])
        CH = sb("CH", [P, P], F32R)
        CL = sb("CL", [P, P], F32R)
        H = sb("H", [P, D])
        HTH = sb("HTH", [P, DK * P], F32R)
        HTL = sb("HTL", [P, DK * P], F32R)
        QA = sb("QA", [P, D])
        QB = sb("QB", [P, D])
        QR = sb("QR", [P, D])
        KA = sb("KA", [P, D])
        KB = sb("KB", [P, D])
        KR = sb("KR", [P, D])
        QS = sb("QS", [P, 2, HEADS, ROWS], F16)
        KS = sb("KS", [P, HEADS, ROWS], F16)
        KT = sb("KT", [P, GROUPS * P], F16)
        KP = sb("KP", [P, 2, QUAD, GROUPS, P], F16)
        QTA = sb("QTA", [P, GROUPS, P], F16)
        QTB = sb("QTB", [P, GROUPS, P], F16)
        VA = sb("VA", [P, 2, HEADS // 2, 80])
        E = sb("E", [P, 4, UH * P])
        LORA_A = E[:].rearrange("p a n -> p (a n)")[0:R, 0:3 * NL * F].rearrange("r (m l f) -> r m l f", m=3, l=NL)
        OS = sb("OS", [P, 512])
        RSUM = sb("RSUM", [P, HEADS // 2, 2])
        AT = sb("AT", [P, D])
        ATH = sb("ATH", [P, DK * P], F32R)
        ATL = sb("ATL", [P, DK * P], F32R)
        ST2 = sb("ST2", [P, 6])
        MV2 = sb("MV2", [P, 2])
        NW2 = sb("NW2", [P, 5])
        TICK = sb("TICK", [P, 1])
        C15 = sb("C15", [P, 1])
        H2 = sb("H2", [P, D])
        RTS = KT[0:NE, :].bitcast(F32)
        RT = sb("RT", [P, 8, B, NE])
        VRAW = RT[:, 0:2].rearrange("p a b e -> p (a b e)")
        RC = CTX[:].rearrange("p (a b i j) -> p a b i j", a=2, b=B, i=NE)
        RV = sb("RV", [P, 6, B])
        SM = sb("SM", [P, 2, FK, GT])
        SIL, MID = SM[:, 0], SM[:, 1]
        LORA_B = SM[:].rearrange("p a c n -> p (a c n)")[0:R, 0:3 * NL * F].rearrange("r (m l f) -> r m l f", m=3, l=NL)
        MH = sb("MH", [P, 2, FK, GT], F32R)
        ML = sb("ML", [P, 2, FK, GT], F32R)

        PS = ctx.enter_context(nc.psum_tensor("PS", [P, 8, 512], F32))
        LT = [PS[:, n, :] for n in (0, 1)]
        LM = [PS[:, n, :] for n in (2, 3)]
        LORA_BANK = [0, 1, 5, 6, 5, 6]
        TBANK = PS[:, 4, :]
        TB16 = PS[:, 4, :].bitcast(F16)
        YBANK = PS[:, 5, :]
        OBANK = PS[:, 6, :]
        HBANK = PS[:, 7, :]

        d_x = [sem(f"d_x{i}") for i in range(4)]
        d_ws = [sem(f"d_ws{i}") for i in range(2)]
        d_gate, d_pos, d_ctx, d_pw, d_lora, d_const, d_rw = [
            sem(n) for n in ("d_gate", "d_pos", "d_ctx", "d_pw", "d_lora", "d_const", "d_rw")]
        zeroed, tanh_done, inv_temp, tgb_done = sem("zeroed"), sem("tanh_done"), sem("inv_temp"), sem("tgb_done")
        angles, trig, neg_sin = sem("angles"), sem("trig"), sem("neg_sin")
        stats1, guess1, rstd1 = sem("stats1"), sem("guess1"), sem("rstd1")
        pw_hi, pw_lo = sem("pw_hi"), sem("pw_lo")
        lora_ps, lora_added = sem("lora_ps"), sem("lora_added")
        wh_done, wl_done = sem("wh_done"), sem("wl_done")
        h_ready, hT_ps, hT_hi, hT_lo, q_ps = sem("h_ready"), sem("hT_ps"), sem("hT_hi"), sem("hT_lo"), sem("q_ps")
        xb_done = sem("xb_done")
        c_hi, c_lo, kv_ps, v_raw, v_done = sem("c_hi"), sem("c_lo"), sem("kv_ps"), sem("v_raw"), sem("v_done")
        k_terms, q_terms = sem("k_terms"), sem("q_terms")
        k_rot, k_hi, k_lo = sem("k_rot"), sem("k_hi"), sem("k_lo")
        q_rot, q_hi, q_lo, m_zero = sem("q_rot"), sem("q_hi"), sem("q_lo"), sem("m_zero")
        kT_ps, kT_sb, qT_ps, qT_sb = sem("kT_ps"), sem("kT_sb"), sem("qT_ps"), sem("qT_sb")
        kp_dma = sem("kp_dma")
        p1_ps, max_done = sem("p1_ps"), sem("max_done")
        qmT_ps, qmT_sb = sem("qmT_ps"), sem("qmT_sb")
        p2_ps, exp_done, av_ps = sem("p2_ps"), sem("exp_done"), sem("av_ps")
        o_sb = sem("o_sb")
        oT_ps, sums_inv, attn, aT_ps = sem("oT_ps"), sem("sums_inv"), sem("attn"), sem("aT_ps")
        a_hi, a_lo, proj_ps, x1_done = sem("a_hi"), sem("a_lo"), sem("proj_ps"), sem("x1_done")
        ln2 = sem("ln2")
        LN2, NEWTON = 8, 12
        newton2 = sem("newton2")
        h2_ready, h2T_ps, h2_hi, h2_lo = sem("h2_ready"), sem("h2T_ps"), sem("h2_hi"), sem("h2_lo")
        rt_ps, rt_sb, rtT_ps, rtT_sb = sem("rt_ps"), sem("rt_sb"), sem("rtT_ps"), sem("rtT_sb")
        r_pool, r_act, r_dve = sem("r_pool"), sem("r_act"), sem("r_dve")
        g_ps, u_ps, silu_done, m_done = sem("g_ps"), sem("u_ps"), sem("silu_done"), sem("m_done")
        CREDIT = 2 * TG
        mh_done, ml_done, d_ps, acc_done, d_out = sem("mh_done"), sem("ml_done"), sem("d_ps"), sem("acc_done"), sem("d_out")

        block = ctx.enter_context(nc.Block())

        def pipeline(eng, step):
            for i in (-2, -1, 0, 1, 2):
                step(i, i % 2)
            with eng.Fori(0, (B - 6) // 2) as half:
                i = eng.snap(2 * half + 3)
                step(i, 1)
                step(i + 1, 0)
            for i in range(B - 3, B + 2):
                step(i, i % 2)

        def live(b):
            return not isinstance(b, int) or 0 <= b < B

        @block.sync
        def _(sp):
            xv = x.rearrange("b t d -> t b d")
            sp.dma_start(X[:, 0:4, :], xv[:, 0:4, :]).then_inc(d_x[0], 16)
            sp.dma_start(PW[:, 0, :].rearrange("p (k n) -> p k n", k=DK),
                         Wq.rearrange("(k p) n -> p k n", p=P)).then_inc(d_pw, 16)
            sp.dma_start(PW[:, 1, :], Wkv).then_inc(d_pw, 16)
            sp.dma_start(PW[:, 2, :].rearrange("p (k n) -> p k n", k=DK),
                         Wout.rearrange("(k p) n -> p k n", p=P)).then_inc(d_pw, 16)
            sp.dma_start(X[:, 4:8, :], xv[:, 4:8, :]).then_inc(d_x[1], 16)
            sp.dma_start(X[:, 8:12, :], xv[:, 8:12, :]).then_inc(d_x[2], 16)
            sp.dma_start(X[:, 12:16, :], xv[:, 12:16, :]).then_inc(d_x[3], 16)
            for e in range(2):
                sp.dma_start(WS[:, e, :], Wexp[e]).then_inc(d_ws[e], 16)

            def spread_k(b, par):
                sp.wait_ge(kT_sb, b + 1)
                if has(b, 2):
                    sp.wait_ge(p2_ps, UNITS * (b - 1))
                if isinstance(b, int) and b < 2:
                    sp.wait_ge(zeroed, 6)
                for j in range(QUAD):
                    r = slice(j * ROWS, (j + 1) * ROWS)
                    sp.dma_start(KP[r, par, j, :, :].rearrange("p g n -> p (g n)"), KT[r, :]).then_inc(kp_dma, 16)

            def step(i, par):
                if live(i + 2):
                    spread_k(i + 2, par)

            pipeline(sp, step)

            for e in range(2, NE):
                sp.wait_ge(wl_done, 3 * (e - 1))
                sp.dma_start(WS[:, e % 2, :], Wexp[e]).then_inc(d_ws[e % 2], 16)
            ov = out.rearrange("b t d -> t b d")
            for g in range(NG):
                sp.wait_ge(acc_done, CREDIT + TG * (NG * (NE - 1) + g + 1))
                sp.dma_start(ov[:, TG * g:TG * (g + 1), :], X[:, TG * g:TG * (g + 1), :]).then_inc(d_out, 16)
            sp.wait_ge(d_out, 16 * NG)

        @block.gpsimd
        def _(pool):
            nc.gpsimd.memset(C15[:], 1.5)
            nc.gpsimd.memset(KS[:], 0.0).then_inc(zeroed, 1)
            nc.gpsimd.memset(QS[:], 0.0).then_inc(zeroed, 1)
            nc.gpsimd.memset(VA[:], 0.0).then_inc(zeroed, 1)
            pool.wait_ge(zeroed, 3)
            nc.gpsimd.memset(KS[:, :, 24], -1.0).then_inc(zeroed, 1)
            nc.gpsimd.memset(VA[:, :, :, 16], 1.0)
            nc.gpsimd.memset(VA[:, :, :, 49], 1.0).then_inc(zeroed, 1)
            nc.gpsimd.memset(KP[:].rearrange("p a j g n -> p (a j g n)").bitcast(F32), 0.0).then_inc(zeroed, 1)
            for n in range(3):
                pool.wait_ge(pw_hi, n + 1)
                nc.gpsimd.tensor_tensor(PWL[:, n, :], PW[:, n, :], PWH[:, n, :].bitcast(F32),
                                        ALU.subtract).then_inc(pw_lo, 1)
            pool.wait_ge(pw_hi, 4)
            nc.gpsimd.tensor_tensor(RWL[:], RW[:], RWH[:].bitcast(F32), ALU.subtract).then_inc(pw_lo, 1)
            pool.wait_ge(tanh_done, 1)
            pool.wait_ge(d_const, 16 * 4)
            nc.gpsimd.tensor_scalar(TGB[:], BOUT[:], TG2[:, 0:1], None, ALU.mult).then_inc(tgb_done, 1)

            def c_low(b):
                pool.wait_ge(c_hi, b + 1)
                if has(b, 1):
                    pool.wait_ge(kv_ps, b)
                nc.gpsimd.tensor_tensor(CL[:], CTX[:, bass.ds(b * P, P)], CH[:].bitcast(F32),
                                        ALU.subtract).then_inc(c_lo, 1)

            def add_bias(b):
                pool.wait_ge(h_ready, b + 1)
                pool.wait_ge(tgb_done, 1)
                nc.gpsimd.tensor_tensor(X[:, bass.ds(b, 1), :], X[:, bass.ds(b, 1), :],
                                        TGB[:, :].rearrange("p (o d) -> p o d", o=1), ALU.add).then_inc(xb_done, 1)

            def rotate(b, terms, ta, tb, rot, hi, lo, done):
                pool.wait_ge(terms, 3 * (b + 1))
                if has(b, 1):
                    pool.wait_ge(hi, b)
                    pool.wait_ge(lo, b)
                nc.gpsimd.tensor_tensor(rot[:], ta[:], tb[:], ALU.add).then_inc(done, 1)

            def low16(b, rot, S, at, hi, lo):
                pool.wait_ge(hi, b + 1)
                r = rot[:].rearrange("p (h d) -> p h d", d=HD)
                nc.gpsimd.tensor_tensor(S[:, :, at:at + HD], r, S[:, :, 0:HD], ALU.subtract).then_inc(lo, 1)

            def clear_max(b, par):
                if has(b, 2):
                    pool.wait_ge(qmT_ps, 2 * (b - 1))
                else:
                    pool.wait_ge(zeroed, 2)
                nc.gpsimd.tensor_tensor(QS[:, par, :, 24], KS[:, :, 25], KS[:, :, 25], ALU.add).then_inc(m_zero, 1)

            def newton(b):
                y, v, t = NW2[:, 2:3], NW2[:, 4:5], NW2[:, 3:4]
                pool.wait_ge(ln2, LN2 * (b + 1))
                if has(b, 1):
                    pool.wait_ge(newton2, NEWTON * b)
                n = 0
                for _ in range(3):
                    for o, a, c, op in ((t, y, y, ALU.mult), (t, t, v, ALU.mult), (t, t, C15[:], ALU.add),
                                        (y, y, t, ALU.mult)):
                        if n:
                            pool.wait_ge(newton2, NEWTON * b + n)
                        nc.gpsimd.tensor_tensor(o, a, c, op).then_inc(newton2, 1)
                        n += 1

            def v_place(b, par):
                pool.wait_ge(v_raw, b + 1)
                if has(b, 2):
                    pool.wait_ge(av_ps, AV * (b - 1))
                zero = KS[:, 0:16, 25:26].unsqueeze(2).to_broadcast([P, 16, 2, HD])
                nc.gpsimd.tensor_tensor(VA[:, par].rearrange("p n (s c) -> p n s c", s=2)[:, :, :, 0:HD],
                                        VRAW.rearrange("p (n s c) -> p n s c", s=2, c=HD), zero,
                                        ALU.add).then_inc(v_done, 1)

            def front(b, par):
                rotate(b, k_terms, KA, KB, KR, k_hi, k_lo, k_rot)
                clear_max(b, par)
                rotate(b, q_terms, QA, QB, QR, q_hi, q_lo, q_rot)
                low16(b, KR, KS, HD, k_hi, k_lo)
                low16(b, QR, QS[:, par], 2 * HD, q_hi, q_lo)
                add_bias(b)
                v_place(b, par)
                if live(b + 1):
                    c_low(b + 1)

            v1, y1, t1 = NW1[:, 0, :], RS1[:, :], NW1[:, 2, :]
            n = 0
            pool.wait_ge(guess1, 3)
            for k in range(3):
                for o, a, c in ((t1, y1, y1), (t1, t1, v1)):
                    if n:
                        pool.wait_ge(rstd1, n)
                    nc.gpsimd.tensor_tensor(o, a, c, ALU.mult).then_inc(rstd1, 1)
                    n += 1
                pool.wait_ge(rstd1, n)
                nc.gpsimd.tensor_scalar(t1, t1, -0.5, 1.5, ALU.mult, ALU.add).then_inc(rstd1, 1)
                n += 1
                pool.wait_ge(rstd1, n)
                nc.gpsimd.tensor_tensor(y1, y1, t1, ALU.mult).then_inc(rstd1, 1)
                n += 1

            def split_expert(e, slot):
                for n in range(3):
                    c = slice(512 * n, 512 * (n + 1))
                    nc.gpsimd.tensor_scalar(WH[:, slot, c], WS[:, slot, c], 1.0, None, ALU.mult).then_inc(wh_done, 1)
                    pool.wait_ge(wh_done, 3 * e + n + 1)
                    nc.gpsimd.tensor_tensor(WL[:, slot, c], WS[:, slot, c], WH[:, slot, c].bitcast(F32),
                                            ALU.subtract).then_inc(wl_done, 1)

            def step(i, par):
                if isinstance(i, int) and i == -2:
                    c_low(0)
                if live(i + 2):
                    front(i + 2, par)
                if live(i - 1):
                    newton(i - 1)
                if isinstance(i, int) and i in (0, 1):
                    e = i
                    pool.wait_ge(lora_added, 3 * (e + 1))
                    split_expert(e, e)

            def router(lo, hi, rp, ra, rd):
                cnt = [rp]
                s = slice(lo, hi)
                n = hi - lo

                def did(ins):
                    cnt[0] += 1
                    ins.then_inc(r_pool, 1)
                    pool.wait_ge(r_pool, cnt[0])

                th, sig, dist, zone, tmp, e1, e3, w = [RT[:, k, s, :] for k in range(8)]
                gt, eq = RC[:, 0, s], RC[:, 1, s]
                diff = gt
                wsum, none, some, fsum = [RV[:, k, s] for k in range(4)]

                def wide(v):
                    return v.unsqueeze(2).to_broadcast([P, n, NE])

                if rp == 0:
                    pool.wait_ge(c_lo, B)
                pool.wait_ge(r_act, ra + 1)
                did(nc.gpsimd.tensor_scalar(sig, th, 0.5, 0.5, ALU.mult, ALU.add))
                did(nc.gpsimd.tensor_scalar(zone, sig, LOWER, None, ALU.is_ge))
                did(nc.gpsimd.tensor_scalar(tmp, sig, UPPER, None, ALU.is_le))
                did(nc.gpsimd.tensor_tensor(zone, zone, tmp, ALU.mult))
                did(nc.gpsimd.tensor_scalar(sig, sig, CENTER, None, ALU.subtract))
                assert cnt[0] == rp + 5
                pool.wait_ge(r_act, ra + 2)
                mine = dist.unsqueeze(3).to_broadcast([P, n, NE, NE])
                other = dist.unsqueeze(2).to_broadcast([P, n, NE, NE])
                did(nc.gpsimd.tensor_tensor(diff, mine, other, ALU.subtract))
                did(nc.gpsimd.tensor_scalar(eq, diff, 0.0, None, ALU.is_equal))
                did(nc.gpsimd.tensor_scalar(gt, diff, 0.0, None, ALU.is_gt))
                did(nc.gpsimd.tensor_tensor(eq, eq, TRI[:].unsqueeze(1).to_broadcast([P, n, NE, NE]), ALU.mult))
                did(nc.gpsimd.tensor_tensor(gt, gt, eq, ALU.add))
                pool.wait_ge(r_dve, rd + 1)
                did(nc.gpsimd.tensor_scalar(tmp, tmp, 1.5, None, ALU.is_lt))
                pool.wait_ge(r_act, ra + 4)
                did(nc.gpsimd.tensor_tensor(e3, e3, tmp, ALU.mult))
                did(nc.gpsimd.tensor_tensor(w, e1, zone, ALU.mult))
                pool.wait_ge(r_dve, rd + 5)
                did(nc.gpsimd.tensor_tensor(e3, e3, wide(fsum), ALU.mult))
                did(nc.gpsimd.tensor_scalar(none, wsum, 1e-8, None, ALU.is_lt))
                did(nc.gpsimd.tensor_scalar(some, none, -1.0, 1.0, ALU.mult, ALU.add))
                did(nc.gpsimd.tensor_tensor(e3, e3, wide(none), ALU.mult))
                did(nc.gpsimd.tensor_tensor(w, w, wide(some), ALU.mult))
                did(nc.gpsimd.tensor_tensor(w, w, e3, ALU.add))
                pool.wait_ge(r_dve, rd + 8)
                did(nc.gpsimd.tensor_scalar(tmp, w, TG2[:, 1:2], None, ALU.mult))
                did(nc.gpsimd.tensor_tensor(WT[:, s, :], tmp, wide(wsum), ALU.mult))
                assert cnt[0] == rp + 21

            def step_and_router(i, par):
                step(i, par)
                if isinstance(i, int) and i == B - 1:
                    router(0, B - TG, 0, 0, 0)
                if isinstance(i, int) and i == B + 1:
                    router(B - TG, B, 21, 4, 8)

            pipeline(pool, step_and_router)

            for e in range(2, NE):
                pool.wait_ge(d_ws[e % 2], 16 * (e // 2 + 1))
                pool.wait_ge(d_ps, NG * (e - 1))
                split_expert(e, e % 2)

        @block.scalar
        def _(act):
            act.dma_start(POS[:], pos.rearrange("b t c -> t b c")).then_inc(d_pos, 16)
            act.dma_start(ID[:], ident).then_inc(d_const, 16)
            act.dma_start(ID16[:], ident16).then_inc(d_const, 16)
            act.dma_start(CTX[:], ctxT).then_inc(d_ctx, 16)
            act.dma_start(GATE[:, 0:1], g_xattn.partition_broadcast(P)).then_inc(d_gate, 16)
            act.dma_start(GATE[:, 1:2], g_ffn.partition_broadcast(P)).then_inc(d_gate, 16)
            act.dma_start(TEMP[:], temperature.partition_broadcast(P)).then_inc(d_gate, 16)
            act.dma_start(BOUT[:], bout.partition_broadcast(P)).then_inc(d_const, 16)
            act.dma_start(TRI[:], lower_tri).then_inc(d_const, 16)
            for n, (a, c) in enumerate(((GaT, Gb), (UaT, Ub), (DaT, Db))):
                act.dma_start(LORA_A[:, n], a.rearrange("l r f -> r l f")).then_inc(d_lora, 16)
                act.dma_start(LORA_B[:, n], c.rearrange("l r f -> r l f")).then_inc(d_lora, 16)
            act.dma_start(RW[:], Wr.rearrange("(k p) e -> p k e", p=P)).then_inc(d_rw, 16)

            act.wait_ge(angles, 8)
            nc.scalar.activation(TRIG[:, 0:2].rearrange("p a b c -> p (a b c)"),
                                 ANG[:].rearrange("p a b c -> p (a b c)"), ACT.Sin).then_inc(trig, 1)
            act.wait_ge(d_gate, 48)
            nc.scalar.activation(TG2[:], GATE[:], ACT.Tanh).then_inc(tanh_done, 1)
            act.wait_ge(d_pw, 48)
            for n in range(3):
                nc.scalar.activation(PWH[:, n, :], PW[:, n, :], ACT.Copy).then_inc(pw_hi, 1)
            act.wait_ge(d_rw, 16)
            nc.scalar.activation(RWH[:], RW[:], ACT.Copy).then_inc(pw_hi, 1)

            def c_high(b):
                if has(b, 1):
                    act.wait_ge(kv_ps, b)
                    act.wait_ge(c_lo, b)
                else:
                    act.wait_ge(d_ctx, 16)
                nc.scalar.activation(CH[:], CTX[:, bass.ds(b * P, P)], ACT.Copy).then_inc(c_hi, 1)

            def hT_high(b):
                act.wait_ge(hT_ps, b + 1)
                if has(b, 1):
                    act.wait_ge(q_ps, b)
                    act.wait_ge(hT_lo, b)
                nc.scalar.activation(HTH[:], HBANK[:, 0:D], ACT.Copy).then_inc(hT_hi, 1)

            def v_evac(b):
                act.wait_ge(k_terms, 3 * (b + 1))
                if has(b, 1):
                    act.wait_ge(v_done, b)
                nc.scalar.activation(VRAW, TBANK[:, D:2 * D], ACT.Copy).then_inc(v_raw, 1)

            def k_evac(b):
                act.wait_ge(kT_ps, b + 1)
                if has(b, 1):
                    act.wait_ge(kp_dma, 16 * QUAD * b)
                nc.scalar.activation(KT[:], TB16, ACT.Copy).then_inc(kT_sb, 1)

            def q_evac(b):
                act.wait_ge(qT_ps, b + 1)
                if has(b, 1):
                    act.wait_ge(p1_ps, UNITS * b)
                nc.scalar.activation(QTA[:].rearrange("p g n -> p (g n)"), TB16, ACT.Copy).then_inc(qT_sb, 1)

            def qm_evac(b, half):
                act.wait_ge(qmT_ps, 2 * b + half + 1)
                if has(b, 1):
                    act.wait_ge(p2_ps, UNITS * (b - 1) + 4 * (half + 1))
                s = slice(GROUPS // 2 * half, GROUPS // 2 * (half + 1))
                nc.scalar.activation(QTB[:, s, :].rearrange("p g n -> p (g n)"), TB16[:, 512 * half:512 * (half + 1)],
                                     ACT.Copy).then_inc(qmT_sb, 1)

            def exps(b, u):
                act.wait_ge(p2_ps, UNITS * b + u + 1)
                if has(b, 1) or u >= 4:
                    act.wait_ge(av_ps, AV * b + u // 2 - 1)
                nc.scalar.activation(E[:, u % 4, :], LT[u % 2], ACT.Exp, scale=SCALE).then_inc(exp_done, 1)

            def o_evac(b):
                act.wait_ge(av_ps, AV * (b + 1))
                if has(b, 1):
                    act.wait_ge(oT_ps, b)
                nc.scalar.activation(OS[:], OBANK, ACT.Copy).then_inc(o_sb, 1)

            def a_high(b):
                act.wait_ge(aT_ps, b + 1)
                if has(b, 1):
                    act.wait_ge(proj_ps, b)
                    act.wait_ge(a_lo, b)
                nc.scalar.activation(ATH[:], YBANK[:, 0:D], ACT.Copy).then_inc(a_hi, 1)

            def h2_high(b):
                act.wait_ge(h2T_ps, b + 1)
                nc.scalar.activation(H2H[:, :, bass.ds(b * P, P)],
                                     YBANK[:, 0:D].rearrange("p (k n) -> p k n", k=DK), ACT.Copy).then_inc(h2_hi, 1)

            def step(i, par):
                a, f, b, t, w = i + 2, i + 1, i, i - 1, i - 2
                A, Fr, Bk, Tl, Wl = [live(n) for n in (a, f, b, t, w)]
                if isinstance(i, int) and i == -2:
                    c_high(0)
                if Bk:
                    exps(b, 0)
                    qm_evac(b, 1)
                    exps(b, 1)
                if Fr:
                    q_evac(f)
                if Bk:
                    exps(b, 2)
                if A:
                    hT_high(a)
                if Bk:
                    exps(b, 3)
                if A:
                    v_evac(a)
                if Bk:
                    exps(b, 4)
                if Tl:
                    a_high(t)
                if Bk:
                    exps(b, 5)
                    exps(b, 6)
                    exps(b, 7)
                if A:
                    k_evac(a)
                if Bk:
                    o_evac(b)
                if Wl:
                    h2_high(w)
                if Fr:
                    qm_evac(f, 0)
                if A and live(a + 1):
                    c_high(a + 1)
                if isinstance(i, int) and i == B - 1:
                    router(0, B - TG, 0, 0)
                if isinstance(i, int) and i == B + 1:
                    router(B - TG, B, 21, 4)

            def router(lo, hi, rp, ra):
                s = slice(lo, hi)
                act.wait_ge(rtT_sb, hi // TG)
                act.wait_ge(inv_temp, 2)
                nc.scalar.activation(RT[:, 0, s, :], LG[:, s, :], ACT.Tanh, scale=HIT[:, 1:2]).then_inc(r_act, 1)
                act.wait_ge(r_pool, rp + 5)
                nc.scalar.activation(RT[:, 2, s, :], RT[:, 1, s, :], ACT.Abs).then_inc(r_act, 1)
                act.wait_ge(r_act, ra + 2)
                nc.scalar.activation(RT[:, 5, s, :], RT[:, 2, s, :], ACT.Exp, scale=-1.0 / 0.1).then_inc(r_act, 1)
                nc.scalar.activation(RT[:, 6, s, :], RT[:, 2, s, :], ACT.Exp, scale=-1.0 / 0.3).then_inc(r_act, 1)

            pipeline(act, step)

            def silu(n, c):
                act.wait_ge(g_ps, FK * n + c + 1)
                if has(n, 1):
                    act.wait_ge(m_done, FK * (n - 1) + c + 1)
                nc.scalar.activation(SIL[:, c, :], PS[:, c, :], ACT.Silu).then_inc(silu_done, 1)

            def mid_high(n, c, par):
                act.wait_ge(m_done, FK * n + c + 1)
                if has(n, 2):
                    act.wait_ge(d_ps, n - 1)
                    act.wait_ge(ml_done, FK * (n - 2) + c + 1)
                nc.scalar.activation(MH[:, par, c, :], MID[:, c, :], ACT.Copy).then_inc(mh_done, 1)

            def group(n, par):
                for c in range(FK):
                    silu(n, c)
                for c in range(FK):
                    mid_high(n, c, par)

            group(0, 0)
            group(1, 1)
            with act.Fori(2, NE * NG, 2) as n:
                n = act.snap(n)
                group(n, 0)
                group(n + 1, 1)

        @block.vector
        def _(dve):
            dve.wait_ge(d_pos, 16)
            posv = POS[:].rearrange("p b c -> p (b c)")
            for n in range(2):
                nc.vector.tensor_scalar(ANG[:, 0, :, n], posv, FREQ[n], None, ALU.mult).then_inc(angles, 1)
            dve.wait_ge(angles, 2)
            flat = ANG[:].rearrange("p a b c -> p a (b c)")
            nc.vector.tensor_scalar(flat[:, 1, :], flat[:, 0, :], math.pi / 2, None, ALU.add).then_inc(angles, 1)
            dve.wait_ge(angles, 3)
            nc.vector.tensor_scalar(TURN[:], flat, 1.0 / TWO_PI, ROUND, ALU.mult, ALU.add).then_inc(angles, 1)
            dve.wait_ge(angles, 4)
            nc.vector.tensor_scalar(TURN[:], TURN[:], ROUND, None, ALU.subtract).then_inc(angles, 1)
            dve.wait_ge(angles, 5)
            nc.vector.scalar_tensor_tensor(flat, TURN[:], -PI2_HI, flat, ALU.mult, ALU.add).then_inc(angles, 1)
            dve.wait_ge(angles, 6)
            nc.vector.scalar_tensor_tensor(flat, TURN[:], -PI2_LO, flat, ALU.mult, ALU.add).then_inc(angles, 1)
            dve.wait_ge(angles, 7)
            nc.vector.tensor_scalar(flat, flat, 3.1415925, -3.1415925, ALU.min, ALU.max).then_inc(angles, 1)
            dve.wait_ge(d_gate, 48)
            nc.vector.reciprocal(HIT[:, 0:1], TEMP[:]).then_inc(inv_temp, 1)
            dve.wait_ge(inv_temp, 1)
            nc.vector.tensor_scalar(HIT[:, 1:2], HIT[:, 0:1], 0.5, None, ALU.mult).then_inc(inv_temp, 1)
            for b in range(B):
                if b % 4 == 0:
                    dve.wait_ge(d_x[b // 4], 16)
                nc.vector.bn_stats(ST1[:, b, :], X[:, b, :]).then_inc(stats1, 1)
            for b in range(B):
                dve.wait_ge(stats1, b + 1)
                nc.vector.bn_aggr(MV1[:, b, :], ST1[:, b, :]).then_inc(stats1, 1)
            dve.wait_ge(stats1, 2 * B)
            v1 = NW1[:, 0, :]
            nc.vector.tensor_scalar(v1, MV1[:, :, 1], EPS, None, ALU.add).then_inc(guess1, 1)
            dve.wait_ge(guess1, 1)
            nc.vector.tensor_scalar(NW1[:, 1, :].bitcast(I32), v1.bitcast(I32), 1, None,
                                    ALU.arith_shift_right).then_inc(guess1, 1)
            dve.wait_ge(guess1, 2)
            nc.vector.tensor_scalar(RS1[:].bitcast(I32), NW1[:, 1, :].bitcast(I32), -1.0, float(0x5f3759df),
                                    ALU.mult, ALU.add).then_inc(guess1, 1)
            dve.wait_ge(trig, 1)
            nc.vector.tensor_scalar(TRIG[:, 2], TRIG[:, 0], -1.0, None, ALU.mult).then_inc(neg_sin, 1)
            dve.wait_ge(neg_sin, 1)

            def norm1(b):
                dve.wait_ge(rstd1, 12)
                if has(b, 1):
                    dve.wait_ge(hT_ps, b)
                nc.vector.tensor_scalar(H[:].unsqueeze(1), X[:, bass.ds(b, 1), :], MV1[:, bass.ds(b, 1), 0],
                                        RS1[:, bass.ds(b, 1)], ALU.subtract, ALU.mult).then_inc(h_ready, 1)

            def hT_low(b):
                dve.wait_ge(hT_hi, b + 1)
                if has(b, 1):
                    dve.wait_ge(q_ps, b)
                nc.vector.tensor_tensor(HTL[:], HBANK[:, 0:D], HTH[:].bitcast(F32), ALU.subtract).then_inc(hT_lo, 1)

            def rope(b, bank, ready, ta, tb, rot, terms):
                dve.wait_ge(ready, b + 1)
                if has(b, 1):
                    dve.wait_ge(rot, b)
                src = bank.rearrange("p (h a c) -> p h a c", h=HEADS, a=4)
                da = ta[:].rearrange("p (h a c) -> p h a c", h=HEADS, a=4)
                db = tb[:].rearrange("p (h a c) -> p h a c", h=HEADS, a=4)
                sin, cos, nsin = [TRIG[:, k, bass.ds(b, 1), :] for k in range(3)]
                nc.vector.tensor_tensor(da, src, cos.unsqueeze(3).to_broadcast([P, HEADS, 4, 2]),
                                        ALU.mult).then_inc(terms, 1)
                nc.vector.tensor_tensor(db[:, :, :, 0], src[:, :, :, 1], nsin.to_broadcast([P, HEADS, 4]),
                                        ALU.mult).then_inc(terms, 1)
                nc.vector.tensor_tensor(db[:, :, :, 1], src[:, :, :, 0], sin.to_broadcast([P, HEADS, 4]),
                                        ALU.mult).then_inc(terms, 1)

            def high16(b, rot, S, gap, done, hi, free, back, per):
                dve.wait_ge(done, b + 1)
                if has(b, back):
                    dve.wait_ge(free, per * (b - back + 1))
                else:
                    dve.wait_ge(zeroed, 4)
                src = rot[:].rearrange("p (h d) -> p h d", d=HD).unsqueeze(2).to_broadcast([P, HEADS, 2, HD])
                dst = S[:, :, 0:2 * gap].rearrange("p h (r d) -> p h r d", r=2)[:, :, :, 0:HD]
                nc.vector.tensor_copy(dst, src).then_inc(hi, 1)

            def row_max(b, u, par):
                dve.wait_ge(p1_ps, UNITS * b + u + 1)
                if u == 0:
                    dve.wait_ge(qT_ps, b + 1)
                nc.vector.tensor_reduce(QS[:, par, UH * u:UH * (u + 1), 24],
                                        LM[u % 2].rearrange("p (h n) -> p h n", h=UH),
                                        AX_X, ALU.max).then_inc(max_done, 1)

            def divide(b):
                dve.wait_ge(oT_ps, b + 1)
                o = YBANK.rearrange("p (n c) -> p n c", c=ROWS)
                if has(b, 1):
                    dve.wait_ge(attn, b)
                nc.vector.reciprocal(RSUM[:], o[:, :, 16:18]).then_inc(sums_inv, 1)
                dve.wait_ge(sums_inv, b + 1)
                if has(b, 1):
                    dve.wait_ge(aT_ps, b)
                nc.vector.tensor_tensor(AT[:].rearrange("p (n s c) -> p n s c", s=2, c=HD),
                                        o[:, :, 0:16].rearrange("p n (s c) -> p n s c", s=2),
                                        RSUM[:].unsqueeze(3).to_broadcast([P, HEADS // 2, 2, HD]),
                                        ALU.mult).then_inc(attn, 1)

            def a_low(b):
                dve.wait_ge(a_hi, b + 1)
                nc.vector.tensor_tensor(ATL[:], YBANK[:, 0:D], ATH[:].bitcast(F32), ALU.subtract).then_inc(a_lo, 1)

            def residual(b):
                dve.wait_ge(proj_ps, b + 1)
                dve.wait_ge(xb_done, b + 1)
                nc.vector.scalar_tensor_tensor(X[:, bass.ds(b, 1), :], YBANK[:, 0:D].unsqueeze(1), TG2[:, 0:1],
                                               X[:, bass.ds(b, 1), :], ALU.mult, ALU.add).then_inc(x1_done, 1)

            def stats2(b):
                dve.wait_ge(x1_done, b + 1)
                if has(b, 1):
                    dve.wait_ge(h2_ready, b)
                    dve.wait_ge(ln2, LN2 * b)
                nc.vector.memset(TICK[:], 0.0).then_inc(ln2, 1)
                nc.vector.bn_stats(ST2[:].unsqueeze(1), X[:, bass.ds(b, 1), :]).then_inc(ln2, 1)
                dve.wait_ge(ln2, LN2 * b + 2)
                nc.vector.memset(TICK[:], 0.0).then_inc(ln2, 1)
                nc.vector.bn_aggr(MV2[:], ST2[:]).then_inc(ln2, 1)
                dve.wait_ge(ln2, LN2 * b + 4)
                if has(b, 1):
                    dve.wait_ge(newton2, NEWTON * b)
                nc.vector.tensor_scalar(NW2[:, 0:1], MV2[:, 1:2], EPS, None, ALU.add).then_inc(ln2, 1)
                dve.wait_ge(ln2, LN2 * b + 5)
                nc.vector.tensor_scalar(NW2[:, 1:2].bitcast(I32), NW2[:, 0:1].bitcast(I32), 1, None,
                                        ALU.arith_shift_right).then_inc(ln2, 1)
                nc.vector.tensor_scalar(NW2[:, 4:5], NW2[:, 0:1], -0.5, None, ALU.mult).then_inc(ln2, 1)
                dve.wait_ge(ln2, LN2 * b + 7)
                nc.vector.tensor_scalar(NW2[:, 2:3].bitcast(I32), NW2[:, 1:2].bitcast(I32), -1.0,
                                        float(0x5f3759df), ALU.mult, ALU.add).then_inc(ln2, 1)

            def norm2(b):
                dve.wait_ge(newton2, NEWTON * (b + 1))
                if has(b, 1):
                    dve.wait_ge(h2T_ps, b)
                nc.vector.tensor_scalar(H2[:].unsqueeze(1), X[:, bass.ds(b, 1), :], MV2[:, 0:1], NW2[:, 2:3],
                                        ALU.subtract, ALU.mult).then_inc(h2_ready, 1)

            def h2_low(b):
                dve.wait_ge(h2_hi, b + 1)
                part = (slice(None), slice(None), bass.ds(b * P, P))
                nc.vector.tensor_tensor(H2L[part], YBANK[:, 0:D].rearrange("p (k n) -> p k n", k=DK),
                                        H2H[part].bitcast(F32), ALU.subtract).then_inc(h2_lo, 1)

            def add_lora(k):
                e, n = divmod(k, 3)
                if n == 0:
                    dve.wait_ge(d_ws[e], 16)
                dve.wait_ge(lora_ps, k + 1)
                w = WS[:, e, 512 * n:512 * (n + 1)]
                nc.vector.tensor_tensor(w, w, PS[:, LORA_BANK[k], :], ALU.add).then_inc(lora_added, 1)

            def router_evac(g):
                dve.wait_ge(rt_ps, g + 1)
                if g:
                    dve.wait_ge(rtT_ps, g)
                else:
                    dve.wait_ge(kp_dma, 16 * QUAD * B)
                nc.vector.tensor_copy(RTS[:], LM[0][0:NE, :]).then_inc(rt_sb, 1)
                dve.wait_ge(rtT_ps, g + 1)
                nc.vector.tensor_copy(LG[:, TG * g:TG * (g + 1), :].rearrange("p b e -> p (b e)"),
                                      LM[1][:, 0:TG * NE]).then_inc(rtT_sb, 1)

            def step(i, par):
                a, f, b, t, w = i + 2, i + 1, i, i - 1, i - 2
                A, Fr, Tl, Wl = [live(n) for n in (a, f, t, w)]

                def row(u):
                    if Fr:
                        row_max(f, u, 1 - par)

                if isinstance(i, int) and i == -2:
                    norm1(0)
                if Tl:
                    divide(t)
                if A:
                    hT_low(a)
                    rope(a, TBANK[:, 0:D], kv_ps, KA, KB, k_rot, k_terms)
                row(0)
                if A:
                    rope(a, HBANK[:, D:2 * D], q_ps, QA, QB, q_rot, q_terms)
                if Wl:
                    norm2(w)
                row(1)
                if Tl:
                    a_low(t)
                if A:
                    high16(a, KR, KS, 2 * HD, k_rot, k_hi, kT_ps, 1, 1)
                row(2)
                row(3)
                if Tl:
                    residual(t)
                if A:
                    high16(a, QR, QS[:, par], HD, q_rot, q_hi, qmT_ps, 2, 2)
                row(4)
                if Tl:
                    stats2(t)
                row(5)
                if Wl:
                    h2_low(w)
                row(6)
                row(7)
                if A and live(a + 1):
                    norm1(a + 1)
                if isinstance(i, int):
                    if i == -2:
                        for k in range(4):
                            add_lora(k)
                    if i == -1:
                        add_lora(4)
                        add_lora(5)
                    if i == B - 1:
                        for g in range(NG - 1):
                            router_evac(g)
                        router(0, B - TG, 0, 0)
                    if i == B + 1:
                        router_evac(NG - 1)
                        router(B - TG, B, 21, 8)

            def router(lo, hi, rp, rd):
                s = slice(lo, hi)
                tmp, e3, w = RT[:, 4, s, :], RT[:, 6, s, :], RT[:, 7, s, :]
                wsum, fsum, raw = RV[:, 0, s], RV[:, 3, s], RV[:, 4, s]
                dve.wait_ge(r_pool, rp + 10)
                nc.vector.tensor_reduce(tmp, RC[:, 0, s], AX_X, ALU.add).then_inc(r_dve, 1)
                dve.wait_ge(r_pool, rp + 13)
                nc.vector.tensor_reduce(wsum, w, AX_X, ALU.add).then_inc(r_dve, 1)
                nc.vector.tensor_reduce(raw, e3, AX_X, ALU.add).then_inc(r_dve, 1)
                dve.wait_ge(r_dve, rd + 3)
                nc.vector.tensor_scalar(raw, raw, 1e-8, None, ALU.max).then_inc(r_dve, 1)
                dve.wait_ge(r_dve, rd + 4)
                nc.vector.reciprocal(fsum, raw).then_inc(r_dve, 1)
                dve.wait_ge(r_pool, rp + 19)
                dve.wait_ge(r_dve, rd + 5)
                nc.vector.tensor_reduce(raw, w, AX_X, ALU.add).then_inc(r_dve, 1)
                dve.wait_ge(r_dve, rd + 6)
                nc.vector.tensor_scalar(raw, raw, 1e-8, None, ALU.max).then_inc(r_dve, 1)
                dve.wait_ge(r_dve, rd + 7)
                nc.vector.reciprocal(wsum, raw).then_inc(r_dve, 1)

            pipeline(dve, step)

            def mid(n, par):
                for c in range(FK):
                    dve.wait_ge(silu_done, FK * n + c + 1)
                    dve.wait_ge(u_ps, FK * n + c + 1)
                    if has(n, 1):
                        dve.wait_ge(mh_done, FK * (n - 1) + c + 1)
                        dve.wait_ge(ml_done, FK * (n - 1) + c + 1)
                    nc.vector.tensor_tensor(MID[:, c, :], SIL[:, c, :], PS[:, 2 + c, :], ALU.mult).then_inc(m_done, 1)
                for c in range(FK):
                    dve.wait_ge(mh_done, FK * n + c + 1)
                    if has(n, 2):
                        dve.wait_ge(d_ps, n - 1)
                    nc.vector.tensor_tensor(ML[:, par, c, :], MID[:, c, :], MH[:, par, c, :].bitcast(F32),
                                            ALU.subtract).then_inc(ml_done, 1)

            def accumulate(n, e, g, par):
                dve.wait_ge(d_ps, n + 1)
                if has(n, NG):
                    dve.wait_ge(acc_done, CREDIT + TG * (n - NG + 1))
                else:
                    dve.wait_ge(r_pool, 42 if g == NG - 1 else 21)
                for k in range(TG):
                    tile = TG * g + k
                    o = PS[:, 4 + 2 * par:6 + 2 * par, :].rearrange("p a (c d) -> p (a c) d", c=2)[:, k, :]
                    nc.vector.scalar_tensor_tensor(X[:, tile, :], o, WT[:, tile, bass.ds(e, 1)], X[:, tile, :],
                                                   ALU.mult, ALU.add).then_inc(acc_done, 1)

            mid(0, 0)
            for g in range(NG):
                mid(g + 1, (g + 1) % 2)
                accumulate(g, 0, g, g % 2)
            with dve.Fori(1, NE - 1, 1) as e:
                e = dve.snap(e)
                for g in range(NG):
                    mid(e * NG + (g + 1), (g + 1) % 2)
                    accumulate(e * NG + g, e, g, g % 2)
            for g in range(NG):
                n = NG * (NE - 1) + g
                if g < NG - 1:
                    mid(n + 1, (g + 1) % 2)
                accumulate(n, NE - 1, g, g % 2)

        @block.tensor
        def _(pe):
            mm = nc.tensor.matmul
            def low_rank(k):
                e, n = divmod(k, 3)
                if k == 0:
                    pe.wait_ge(d_lora, 16 * 6)
                if k >= 4:
                    pe.wait_ge(lora_added, k - 1)
                for j in range(DK):
                    last = mm(PS[:, LORA_BANK[k], F * j:F * (j + 1)], LORA_A[:, n, e, P * j:P * (j + 1)],
                              LORA_B[:, n, e, :], start=True, stop=True)
                last.then_inc(lora_ps, 1)

            def product(dst, pairs):
                last = None
                ops = []
                for (sh, sl), (mh, ml) in pairs:
                    ops += [(sh, mh), (sh, ml), (sl, mh)]
                for n, (s, m) in enumerate(ops):
                    last = mm(dst, s, m, start=n == 0, stop=n == len(ops) - 1)
                return last

            def transpose_h(b):
                pe.wait_ge(h_ready, b + 1)
                if has(b, 1):
                    pe.wait_ge(q_terms, 3 * b)
                else:
                    pe.wait_ge(d_const, 16 * 4)
                for k in range(DK):
                    last = nc.tensor.transpose(HBANK[:, P * k:P * (k + 1)], H[:, P * k:P * (k + 1)], ID[:])
                last.then_inc(hT_ps, 1)

            def project_kv(b):
                pe.wait_ge(c_lo, b + 1)
                if has(b, 1):
                    pe.wait_ge(qT_sb, b)
                else:
                    pe.wait_ge(pw_lo, 3)
                product(TBANK, [((CH[:], CL[:]), (PWH[:, 1, :], PWL[:, 1, :]))]).then_inc(kv_ps, 1)

            def project_q(b):
                pe.wait_ge(hT_lo, b + 1)
                if not has(b, 1):
                    pe.wait_ge(pw_lo, 1)
                product(HBANK[:, D:2 * D],
                        [((HTH[:, P * k:P * (k + 1)], HTL[:, P * k:P * (k + 1)]),
                          (PWH[:, 0, D * k:D * (k + 1)], PWL[:, 0, D * k:D * (k + 1)]))
                         for k in range(DK)]).then_inc(q_ps, 1)

            def transpose16(S, lo, hi, done):
                for g in range(lo, hi):
                    last = nc.tensor.transpose(TB16[:, P * g:P * (g + 1)],
                                               S[:, QUAD * g:QUAD * (g + 1), :].rearrange("p h r -> p (h r)"), ID16[:])
                last.then_inc(done, 1)

            def transpose_k(b):
                pe.wait_ge(k_lo, b + 1)
                pe.wait_ge(v_raw, b + 1)
                transpose16(KS, 0, GROUPS, kT_ps)

            def transpose_q(b, par):
                pe.wait_ge(q_lo, b + 1)
                pe.wait_ge(m_zero, b + 1)
                if has(b, 1):
                    pe.wait_ge(qmT_sb, 2 * b)
                else:
                    pe.wait_ge(kT_sb, 1)
                transpose16(QS[:, par], 0, GROUPS, qT_ps)

            def logits(b, u, par):
                if u == 0:
                    pe.wait_ge(kp_dma, 16 * QUAD * (b + 1))
                    pe.wait_ge(qT_sb, b + 1)
                if has(b, 1) or u >= 2:
                    pe.wait_ge(max_done, UNITS * b + u - 1)
                mm(LM[u % 2].rearrange("p (a n) -> p a n", a=QUAD), QTA[:, u, :], KP[:, par, :, u, :],
                   start=True, stop=True).then_inc(p1_ps, 1)

            def transpose_qm(b, half, par):
                pe.wait_ge(max_done, UNITS * b + 4 * (half + 1))
                if half:
                    pe.wait_ge(qmT_sb, 2 * b + 1)
                else:
                    if live(b + 1):
                        pe.wait_ge(kT_sb, b + 2)
                transpose16(QS[:, par], GROUPS // 2 * half, GROUPS // 2 * (half + 1), qmT_ps)

            def logits_t(b, u, par):
                if u % 4 == 0:
                    pe.wait_ge(qmT_sb, 2 * b + u // 4 + 1)
                if has(b, 1) or u >= 2:
                    pe.wait_ge(exp_done, UNITS * b + u - 1)
                elif u == 0:
                    pe.wait_ge(lora_added, 6)
                for j in range(QUAD):
                    last = mm(LT[u % 2][:, P * j:P * (j + 1)], KP[:, par, j, u, :], QTB[:, u, :],
                              start=True, stop=True)
                last.then_inc(p2_ps, 1)

            def attend(b, u, par):
                pe.wait_ge(exp_done, UNITS * b + 2 * (u + 1))
                if u == 0:
                    pe.wait_ge(v_done, b + 1)
                    if has(b, 1):
                        pe.wait_ge(o_sb, b)
                for s in range(2):
                    for c in range(4):
                        pair = 4 * u + c
                        last = mm(OBANK[32 * c:32 * (c + 1), P * u:P * (u + 1)],
                                  VA[:, par, pair, 32 * s:32 * (s + 1)],
                                  E[:, 2 * (u % 2) + c // 2, P * (2 * (c % 2) + s):P * (2 * (c % 2) + s + 1)],
                                  start=s == 0, stop=s == 1)
                last.then_inc(av_ps, 1)

            def transpose_o(b):
                pe.wait_ge(o_sb, b + 1)
                if has(b, 2):
                    pe.wait_ge(h2_lo, b - 1)
                for r in range(4):
                    last = nc.tensor.transpose(YBANK[:, P * r:P * (r + 1)], OS[:, P * r:P * (r + 1)], ID[:])
                last.then_inc(oT_ps, 1)

            def transpose_a(b):
                pe.wait_ge(attn, b + 1)
                for k in range(DK):
                    last = nc.tensor.transpose(YBANK[:, P * k:P * (k + 1)], AT[:, P * k:P * (k + 1)], ID[:])
                last.then_inc(aT_ps, 1)

            def project_o(b):
                pe.wait_ge(a_lo, b + 1)
                product(YBANK[:, 0:D],
                        [((ATH[:, P * k:P * (k + 1)], ATL[:, P * k:P * (k + 1)]),
                          (PWH[:, 2, D * k:D * (k + 1)], PWL[:, 2, D * k:D * (k + 1)]))
                         for k in range(DK)]).then_inc(proj_ps, 1)

            def transpose_h2(b):
                pe.wait_ge(h2_ready, b + 1)
                if live(b + 1):
                    pe.wait_ge(x1_done, b + 2)
                for k in range(DK):
                    last = nc.tensor.transpose(YBANK[:, P * k:P * (k + 1)], H2[:, P * k:P * (k + 1)], ID[:])
                last.then_inc(h2T_ps, 1)

            def router(g):
                pe.wait_ge(h2_lo, TG * (g + 1))
                pe.wait_ge(max_done, UNITS * B)
                if g:
                    pe.wait_ge(rt_sb, g)
                else:
                    pe.wait_ge(pw_lo, 4)
                s = slice(GT * g, GT * (g + 1))
                product(LM[0][0:NE, :], [((RWH[:, k, :], RWL[:, k, :]), (H2H[:, k, s], H2L[:, k, s]))
                                         for k in range(DK)]).then_inc(rt_ps, 1)
                pe.wait_ge(rt_sb, g + 1)
                if g:
                    pe.wait_ge(rtT_sb, g)
                for k in range(TG):
                    last = nc.tensor.transpose(LM[1][:, NE * k:NE * (k + 1)], RTS[:, P * k:P * (k + 1)],
                                               ID[0:NE, 0:NE])
                last.then_inc(rtT_ps, 1)

            def step(i, par):
                a, f, b, t, w = i + 2, i + 1, i, i - 1, i - 2
                A, Fr, Bk, Tl, Wl = [live(n) for n in (a, f, b, t, w)]

                def lt(u):
                    if Bk:
                        logits_t(b, u, par)

                def lm(u):
                    if Fr:
                        logits(f, u, 1 - par)

                def av(u):
                    if Bk:
                        attend(b, u, par)

                if i == -2 if isinstance(i, int) else False:
                    for k in range(4):
                        low_rank(k)
                if i == -1 if isinstance(i, int) else False:
                    low_rank(4)
                    low_rank(5)
                lt(0)
                if Bk:
                    transpose_qm(b, 1, par)
                lt(1)
                if Tl:
                    transpose_o(t)
                if Fr:
                    transpose_q(f, 1 - par)
                if A:
                    transpose_h(a)
                lt(2)
                if A:
                    project_kv(a)
                lt(3)
                av(0)
                lm(0)
                if A:
                    project_q(a)
                lt(4)
                if Tl:
                    transpose_a(t)
                lm(1)
                lt(5)
                av(1)
                lm(2)
                lt(6)
                lm(3)
                if Tl:
                    project_o(t)
                lt(7)
                av(2)
                lm(4)
                av(3)
                lm(5)
                if A:
                    transpose_k(a)
                if Wl:
                    transpose_h2(w)
                lm(6)
                if Fr:
                    transpose_qm(f, 0, 1 - par)
                lm(7)
                if isinstance(i, int) and i == B - 1:
                    for g in range(NG - 1):
                        router(g)
                if isinstance(i, int) and i == B + 1:
                    router(NG - 1)

            pipeline(pe, step)

            def gate_up(n, g, slot):
                for c in range(FK):
                    for part, base, done in ((0, 0, g_ps), (1, 2, u_ps)):
                        if has(n, 1):
                            if part == 0:
                                pe.wait_ge(silu_done, FK * (n - 1) + c + 1)
                            else:
                                pe.wait_ge(m_done, FK * (n - 1) + c + 1)
                        cols = [slice(512 * part + F * k + P * c, 512 * part + F * k + P * (c + 1)) for k in range(DK)]
                        product(PS[:, base + c, :],
                                [((WH[:, slot, cols[k]], WL[:, slot, cols[k]]),
                                  (H2H[:, k, GT * g:GT * (g + 1)], H2L[:, k, GT * g:GT * (g + 1)]))
                                 for k in range(DK)]).then_inc(done, 1)

            def down(n, slot, par):
                pe.wait_ge(ml_done, FK * (n + 1))
                pe.wait_ge(acc_done, TG * (n + 1))
                for k in range(TG):
                    bank = PS[:, 4 + 2 * par + k // 2, D * (k % 2):D * (k % 2 + 1)]
                    t = slice(P * k, P * (k + 1))
                    last = product(bank, [((MH[:, par, c, t], ML[:, par, c, t]),
                                           (WH[:, slot, 1024 + D * c:1024 + D * (c + 1)],
                                            WL[:, slot, 1024 + D * c:1024 + D * (c + 1)])) for c in range(FK)])
                last.then_inc(d_ps, 1)

            def weights(e):
                pe.wait_ge(wl_done, 3 * (e + 1))

            def pair_of_experts(e, final):
                for s in range(2):
                    for g in range(NG):
                        n = NG * (e + s) + g
                        nxt = NG * s + g + 1
                        if not (final and nxt == 2 * NG):
                            if nxt % NG == 0:
                                weights(e + s + 1)
                            gate_up(n + 1, nxt % NG, (nxt // NG) % 2)
                        down(n, s, g % 2)

            for s, n in ((exp_done, UNITS * B), (max_done, UNITS * B), (o_sb, B), (h2_lo, B), (rtT_sb, NG),
                         (qmT_sb, 2 * B), (q_terms, 3 * B)):
                pe.wait_ge(s, n)
            pe.sem_inc(acc_done, CREDIT)
            weights(0)
            gate_up(0, 0, 0)
            with pe.Fori(0, NE - 2, 2) as e:
                e = pe.snap(e)
                pair_of_experts(e, False)
            pair_of_experts(NE - 2, True)


def kernel(x, ctx_1024, fside_BxSx2_0, g_xattn, g_ffn, L0_xattn_Wq, L0_xattn_Wkv, L0_xattn_Wout, L0_xattn_bout,
           L0_ffn_Wg, L0_ffn_Wu, L0_ffn_Wd, L0_ffn_Ga, L0_ffn_Gb, L0_ffn_Ua, L0_ffn_Ub, L0_ffn_Da, L0_ffn_Db,
           L0_ffn_Wr, L0_ffn_temperature):
    import numpy as np
    import concourse.bacc as bacc
    from concourse import mybir as _mybir
    from concourse.bass_utils import run_bass_kernel_spmd

    def rows(w):
        w = np.asarray(w)
        e, r, n = w.shape
        return w.reshape(e, r // 128, 128, n).transpose(0, 2, 1, 3).reshape(e, 128, -1)

    arrays = {
        "x": np.asarray(x),
        "ctxT": np.asarray(ctx_1024).transpose(2, 0, 1).reshape(ctx_1024.shape[2], -1),
        "pos": np.asarray(fside_BxSx2_0),
        "g_xattn": np.asarray(g_xattn), "g_ffn": np.asarray(g_ffn),
        "Wq": np.asarray(L0_xattn_Wq), "Wkv": np.asarray(L0_xattn_Wkv),
        "Wout": np.asarray(L0_xattn_Wout), "bout": np.asarray(L0_xattn_bout),
        "Wexp": np.concatenate([rows(L0_ffn_Wg), rows(L0_ffn_Wu), rows(L0_ffn_Wd)], axis=2),
        "GaT": np.asarray(L0_ffn_Ga).transpose(0, 2, 1), "Gb": np.asarray(L0_ffn_Gb),
        "UaT": np.asarray(L0_ffn_Ua).transpose(0, 2, 1), "Ub": np.asarray(L0_ffn_Ub),
        "DaT": np.asarray(L0_ffn_Da).transpose(0, 2, 1), "Db": np.asarray(L0_ffn_Db),
        "Wr": np.asarray(L0_ffn_Wr), "temperature": np.asarray(L0_ffn_temperature),
        "ident": np.eye(128, dtype=np.float32),
        "ident16": np.eye(128, dtype=np.float16),
        "lower_tri": np.broadcast_to(np.tril(np.ones((8, 8), np.float32), -1), (128, 8, 8)),
    }
    nc = bacc.Bacc("TRN2", target_bir_lowering=False, num_devices=1)
    arrays = {f"in_{k}": np.ascontiguousarray(a) for k, a in arrays.items()}
    args = [nc.dram_tensor(k, a.shape, _mybir.dt.from_np(a.dtype), kind="ExternalInput").ap()
            for k, a in arrays.items()]
    out = nc.dram_tensor("out", x.shape, _mybir.dt.from_np(np.dtype("float32")), kind="ExternalOutput").ap()
    flamingo_kernel(nc, *args, out)
    r = run_bass_kernel_spmd(nc, [arrays], core_ids=[0])
    return r.results[0]["out"]
```

```python
import math
from contextlib import ExitStack

import concourse.bass as bass
from concourse import mybir

F32 = mybir.dt.float32
F32R = mybir.dt.float32r
F16 = mybir.dt.float16
I32 = mybir.dt.int32
ALU = mybir.AluOpType
ACT = mybir.ActivationFunctionType
AX_X = mybir.AxisListType.X

P = 128


def has(b, back):
    return not isinstance(b, int) or b >= back


def i_is(i, n):
    return isinstance(i, int) and i == n


def flamingo_kernel(nc, x, ctxT, pos, g_xattn, g_ffn, Wq, Wkv, Wout, bout, Wexp, GaT, Gb, UaT, Ub, DaT, Db,
                    Wr, temperature, ident, ident16, lower_tri, out):
    B, T, D = x.shape
    DK = D // P
    HEADS, HD = 32, 8
    QUAD = 4
    GROUPS = HEADS // QUAD
    ROWS = P // QUAD
    UNITS = 8
    UH = HEADS // UNITS
    AV = UNITS // 2
    NE, WCOLS = Wexp.shape[0], Wexp.shape[2]
    F = WCOLS // (3 * DK)
    FK = F // P
    NL, R = GaT.shape[0], GaT.shape[1]
    PARTS = [slice(0, 4), slice(4, 16)]
    SPLIT_STEPS = (0, 1, 2, B - 3, B - 2, B - 1)
    PW_ORDER = (1, 0, 2)
    TG = 4
    NG = B // TG
    HALVES = TG // 2
    GT = TG * P
    SCALE = 1.0 / math.sqrt(HD)
    EPS = 1e-5
    TWO_PI = 2.0 * math.pi
    PI2_HI = 6.28125
    PI2_LO = TWO_PI - PI2_HI
    ROUND = 1.5 * 2.0 ** 23
    FREQ = [1.0, 10000.0 ** -0.5]
    LOWER, UPPER, CENTER = 0.5 - math.log(4.0 / 3.0), 0.5, 1.0 / math.e
    CTX0 = 2 * P
    assert T == P and D == HEADS * HD and WCOLS == 6 * 256 and NL == 2 and B % 4 == 0

    ctx = ExitStack()
    with ctx:
        def sb(name, shape, dt=F32):
            return ctx.enter_context(nc.sbuf_tensor(name, shape, dt))

        def sem(name):
            return ctx.enter_context(nc.semaphore(name))

        X = sb("X", [P, B, D])
        H2H = sb("H2H", [P, DK, B * P], F32R)
        H2L = sb("H2L", [P, DK, B * P], F32R)
        WH = sb("WH", [P, 2, WCOLS], F32R)
        WL = sb("WL", [P, 2, WCOLS], F32R)
        WS = sb("WS", [P, 2, WCOLS])
        LG = sb("LG", [P, B, NE])
        WT = sb("WT", [P, B, NE])
        ID = sb("ID", [P, P])
        ID16 = sb("ID16", [P, P], F16)
        TRI = sb("TRI", [P, NE, NE])
        GATE = sb("GATE", [P, 2])
        TG2 = sb("TG2", [P, 2])
        TEMP = sb("TEMP", [P, 1])
        HIT = sb("HIT", [P, 2])
        BOUT = sb("BOUT", [P, D])
        TGB = sb("TGB", [P, D])
        PW = sb("PW", [P, 3, 512])
        PWH = sb("PWH", [P, 3, 512], F32R)
        PWL = sb("PWL", [P, 3, 512], F32R)
        RW = sb("RW", [P, DK, NE])
        RWH = sb("RWH", [P, DK, NE], F32R)
        RWL = sb("RWL", [P, DK, NE], F32R)
        POS = sb("POS", [P, B, 2])
        ANG = sb("ANG", [P, 2, B * 2, 2])
        TURN = sb("TURN", [P, 2, B * 4])
        TRIG = sb("TRIG", [P, 3, B, 4])
        ST1 = sb("ST1", [P, B, 6])
        MV1 = sb("MV1", [P, B, 2])
        RS1 = sb("RS1", [P, B])
        NB1 = sb("NB1", [P, B])
        NW1 = sb("NW1", [P, 3, B])
        CTX = sb("CTX", [P, B * P])
        CH = sb("CH", [P, P], F32R)
        CL = sb("CL", [P, P], F32R)
        H = sb("H", [P, D])
        HTH = sb("HTH", [P, DK * P], F32R)
        HTL = sb("HTL", [P, DK * P], F32R)
        QA = sb("QA", [P, D])
        QB = sb("QB", [P, D])
        QR = sb("QR", [P, D])
        KA = sb("KA", [P, D])
        KB = sb("KB", [P, D])
        KR = sb("KR", [P, D])
        QS = sb("QS", [P, 2, HEADS, ROWS], F16)
        KS = sb("KS", [P, HEADS, ROWS], F16)
        KT = sb("KT", [P, GROUPS * P], F16)
        KP = sb("KP", [P, 2, QUAD, GROUPS, P], F16)
        QT0 = sb("QT0", [P, GROUPS, P], F16)
        QTB = sb("QTB", [P, GROUPS, P], F16)
        VA = sb("VA", [P, 2, HEADS // 2, 80])
        E = sb("E", [P, 4, UH * P])
        LORA_A = E[:].rearrange("p a n -> p (a n)")[0:R, 0:3 * NL * F].rearrange("r (m l f) -> r m l f", m=3, l=NL)
        OS = sb("OS", [P, 512])
        RSUM = sb("RSUM", [P, HEADS // 2, 2])
        AT = sb("AT", [P, D])
        ATH = sb("ATH", [P, DK * P], F32R)
        ATL = sb("ATL", [P, DK * P], F32R)
        ST2 = sb("ST2", [P, 6])
        MV2 = sb("MV2", [P, 2])
        NW2 = sb("NW2", [P, 5])
        TICK = sb("TICK", [P, 1])
        C15 = sb("C15", [P, 1])
        ZERO = sb("ZERO", [P, 1])
        H2 = sb("H2", [P, D])
        RTS = KT[0:NE, :].bitcast(F32)
        RT = sb("RT", [P, 8, B, NE])
        VRAW = RT[:, 0:2].rearrange("p a b e -> p (a b e)")
        RC = CTX[:].rearrange("p (a b i j) -> p a b i j", a=2, b=B, i=NE)
        RV = sb("RV", [P, 6, B])
        SM = sb("SM", [P, 2, FK, GT])
        SIL, MID = SM[:, 0], SM[:, 1]
        LORA_B = SM[:].rearrange("p a c n -> p (a c n)")[0:R, 0:3 * NL * F].rearrange("r (m l f) -> r m l f", m=3, l=NL)
        MH = sb("MH", [P, 2, FK, GT], F32R)
        ML = sb("ML", [P, 2, FK, GT], F32R)
        QTA = [QT0[:], SM[:].rearrange("p a c n -> p (a c n)")[:, 3 * NL * F:].bitcast(F16).rearrange(
            "p (g n) -> p g n", g=GROUPS)]

        PS = ctx.enter_context(nc.psum_tensor("PS", [P, 8, 512], F32))
        LT = [PS[:, n, :] for n in (0, 1)]
        LM = [PS[:, n, :] for n in (2, 3)]
        RT_BANKS = [(LM[0], LM[1])] * (NG - 1) + [(PS[:, 5, :], PS[:, 4, :])]
        OUT_BANK = [6, 4]
        LORA_BANK = [2, 3, 6, 0, 1, 5]
        TBANK = PS[:, 4, :]
        TB16 = PS[:, 4, :].bitcast(F16)
        YBANK = PS[:, 5, :]
        OBANK = PS[:, 6, :]
        OB16 = PS[:, 6, :].bitcast(F16)
        HBANK = PS[:, 7, :]
        HB16 = PS[:, 7, :].bitcast(F16)

        d_x = [sem(f"d_x{i}") for i in range(4)]
        d_ws = [sem(f"d_ws{i}") for i in range(2)]
        d_ctx = [sem(f"d_ctx{i}") for i in range(2)]
        d_pw = [sem(f"d_pw{i}") for i in range(3)]
        d_gate, d_pos, d_lora, d_const, d_late = [
            sem(n) for n in ("d_gate", "d_pos", "d_lora", "d_const", "d_late")]
        kp_zeroed = sem("kp_zeroed")
        zeroed, tanh_done, inv_temp, tgb_done = sem("zeroed"), sem("tanh_done"), sem("inv_temp"), sem("tgb_done")
        angles, trig, neg_sin = sem("angles"), sem("trig"), sem("neg_sin")
        shift1_done = sem("shift1_done")
        stats1, guess1, rstd1 = sem("stats1"), sem("guess1"), sem("rstd1")
        pw_hi, pw_lo, out_lo = sem("pw_hi"), sem("pw_lo"), sem("out_lo")
        lora_ps, lora_added = sem("lora_ps"), sem("lora_added")
        wh_done, wl_done = sem("wh_done"), sem("wl_done")
        h_ready, hT_ps, hT_hi, hT_lo, q_ps = sem("h_ready"), sem("hT_ps"), sem("hT_hi"), sem("hT_lo"), sem("q_ps")
        xb_done = sem("xb_done")
        c_hi, c_lo, kv_ps, v_raw, v_done = sem("c_hi"), sem("c_lo"), sem("kv_ps"), sem("v_raw"), sem("v_done")
        k_terms, q_terms = sem("k_terms"), sem("q_terms")
        k_rot, k_hi, k_lo = sem("k_rot"), sem("k_hi"), sem("k_lo")
        q_rot, q_hi, q_lo, m_zero = sem("q_rot"), sem("q_hi"), sem("q_lo"), sem("m_zero")
        kT_ps, kT_sb, qT_ps, qT_sb = sem("kT_ps"), sem("kT_sb"), sem("qT_ps"), sem("qT_sb")
        kp_dma = sem("kp_dma")
        p1_ps, max_done = sem("p1_ps"), sem("max_done")
        qmT_ps, qmT_sb = sem("qmT_ps"), sem("qmT_sb")
        p2_ps, exp_done, av_ps = sem("p2_ps"), sem("exp_done"), sem("av_ps")
        o_sb = sem("o_sb")
        oT_ps, sums_inv, attn, aT_ps = sem("oT_ps"), sem("sums_inv"), sem("attn"), sem("aT_ps")
        a_hi, a_lo, proj_ps, x1_done = sem("a_hi"), sem("a_lo"), sem("proj_ps"), sem("x1_done")
        ln2 = sem("ln2")
        LN2, NEWTON = 8, 12
        newton2 = sem("newton2")
        h2_ready, h2T_ps, h2_hi, h2_lo = sem("h2_ready"), sem("h2T_ps"), sem("h2_hi"), sem("h2_lo")
        rt_ps, rt_sb, rtT_ps, rtT_sb = sem("rt_ps"), sem("rt_sb"), sem("rtT_ps"), sem("rtT_sb")
        r_pool, r_act, r_dve = sem("r_pool"), sem("r_act"), sem("r_dve")
        g_ps, u_ps, silu_done, m_done = sem("g_ps"), sem("u_ps"), sem("silu_done"), sem("m_done")
        CREDIT = 2 * TG
        mh_done, ml_done, d_ps, acc_done, d_out = sem("mh_done"), sem("ml_done"), sem("d_ps"), sem("acc_done"), sem("d_out")

        block = ctx.enter_context(nc.Block())

        def pipeline(eng, step):
            for i in (-2, -1, 0, 1, 2):
                step(i, i % 2)
            with eng.Fori(0, (B - 6) // 2) as half:
                i = eng.snap(2 * half + 3)
                step(i, 1)
                step(i + 1, 0)
            for i in range(B - 3, B):
                step(i, i % 2)

        def live(b):
            return not isinstance(b, int) or 0 <= b < B

        @block.sync
        def _(sp):
            xv = x.rearrange("b t d -> t b d")
            sp.dma_start(X[:, 0:4, :], xv[:, 0:4, :]).then_inc(d_x[0], 16)
            sp.dma_start(PW[:, 0, :].rearrange("p (k n) -> p k n", k=DK),
                         Wq.rearrange("(k p) n -> p k n", p=P)).then_inc(d_pw[0], 16)
            sp.dma_start(ID16[:], ident16).then_inc(d_const, 16)
            sp.dma_start(PW[:, 2, :].rearrange("p (k n) -> p k n", k=DK),
                         Wout.rearrange("(k p) n -> p k n", p=P)).then_inc(d_pw[2], 16)
            sp.dma_start(CTX[:, CTX0:], ctxT[:, CTX0:]).then_inc(d_ctx[1], 16)
            for n, (a, c) in enumerate(((GaT, Gb), (UaT, Ub), (DaT, Db))):
                sp.dma_start(LORA_A[:, n], a.rearrange("l r f -> r l f")).then_inc(d_lora, 16)
                sp.dma_start(LORA_B[:, n], c.rearrange("l r f -> r l f")).then_inc(d_lora, 16)
            sp.dma_start(X[:, 4:8, :], xv[:, 4:8, :]).then_inc(d_x[1], 16)
            sp.dma_start(X[:, 8:12, :], xv[:, 8:12, :]).then_inc(d_x[2], 16)
            sp.dma_start(X[:, 12:16, :], xv[:, 12:16, :]).then_inc(d_x[3], 16)
            sp.dma_start(GATE[:, 0:1], g_xattn.partition_broadcast(P)).then_inc(d_gate, 16)
            sp.dma_start(GATE[:, 1:2], g_ffn.partition_broadcast(P)).then_inc(d_gate, 16)
            sp.dma_start(TEMP[:], temperature.partition_broadcast(P)).then_inc(d_gate, 16)
            sp.dma_start(BOUT[:], bout.partition_broadcast(P)).then_inc(d_late, 16)
            sp.dma_start(TRI[:], lower_tri).then_inc(d_late, 16)
            sp.dma_start(RW[:], Wr.rearrange("(k p) e -> p k e", p=P)).then_inc(d_late, 16)
            for e in range(2):
                sp.dma_start(WS[:, e, :], Wexp[e]).then_inc(d_ws[e], 16)

            def spread_k(b, par):
                sp.wait_ge(kT_sb, b + 1)
                if has(b, 2):
                    sp.wait_ge(p2_ps, UNITS * (b - 1))
                if isinstance(b, int) and b < 2:
                    sp.wait_ge(kp_zeroed, b + 1)
                for j in range(QUAD):
                    r = slice(j * ROWS, (j + 1) * ROWS)
                    sp.dma_start(KP[r, par, j, :, :].rearrange("p g n -> p (g n)"), KT[r, :]).then_inc(kp_dma, 16)

            def step(i, par):
                if live(i + 2):
                    spread_k(i + 2, par)

            pipeline(sp, step)

            for e in range(2, NE):
                sp.wait_ge(wl_done, 3 * (e - 1))
                sp.dma_start(WS[:, e % 2, :], Wexp[e]).then_inc(d_ws[e % 2], 16)
            ov = out.rearrange("b t d -> t b d")
            for g in range(NG):
                for h in range(HALVES):
                    tiles = slice(TG * g + 2 * h, TG * g + 2 * (h + 1))
                    sp.wait_ge(acc_done, CREDIT + TG * NG * (NE - 1) + tiles.stop)
                    sp.dma_start(ov[:, tiles, :], X[:, tiles, :]).then_inc(d_out, 16)
            sp.wait_ge(d_out, 16 * NG * HALVES)

        @block.gpsimd
        def _(pool):
            nc.gpsimd.memset(C15[:], 1.5)
            nc.gpsimd.memset(ZERO[:], 0.0)
            nc.gpsimd.memset(KS[:], 0.0).then_inc(zeroed, 1)
            nc.gpsimd.memset(QS[:], 0.0).then_inc(zeroed, 1)
            nc.gpsimd.memset(VA[:], 0.0).then_inc(zeroed, 1)
            pool.wait_ge(zeroed, 3)
            nc.gpsimd.memset(KS[:, :, 24], -1.0).then_inc(zeroed, 1)
            nc.gpsimd.memset(VA[:, :, :, 16], 1.0)
            nc.gpsimd.memset(VA[:, :, :, 49], 1.0).then_inc(zeroed, 1)

            def project_low(n):
                pool.wait_ge(pw_hi, n + 1)
                if n == 3:
                    nc.gpsimd.tensor_tensor(RWL[:], RW[:], RWH[:].bitcast(F32), ALU.subtract).then_inc(out_lo, 1)
                else:
                    nc.gpsimd.tensor_tensor(PWL[:, 2, :], PW[:, 2, :], PWH[:, 2, :].bitcast(F32),
                                            ALU.subtract).then_inc(out_lo, 1)

            def c_low(b):
                pool.wait_ge(c_hi, b + 1)
                if has(b, 1):
                    pool.wait_ge(kv_ps, b)
                nc.gpsimd.tensor_tensor(CL[:], CTX[:, bass.ds(b * P, P)], CH[:].bitcast(F32),
                                        ALU.subtract).then_inc(c_lo, 1)

            def add_bias(b):
                pool.wait_ge(h_ready, b + 1)
                pool.wait_ge(tgb_done, 1)
                nc.gpsimd.tensor_tensor(X[:, bass.ds(b, 1), :], X[:, bass.ds(b, 1), :],
                                        TGB[:, :].rearrange("p (o d) -> p o d", o=1), ALU.add).then_inc(xb_done, 1)

            def rotate(b, terms, ta, tb, rot, hi, lo, done):
                pool.wait_ge(terms, 3 * (b + 1))
                if has(b, 1):
                    pool.wait_ge(hi, b)
                    pool.wait_ge(lo, b)
                nc.gpsimd.tensor_tensor(rot[:], ta[:], tb[:], ALU.add).then_inc(done, 1)

            def low16(b, rot, S, at, hi, lo):
                pool.wait_ge(hi, b + 1)
                r = rot[:].rearrange("p (h d) -> p h d", d=HD)
                nc.gpsimd.tensor_tensor(S[:, :, at:at + HD], r, S[:, :, 0:HD], ALU.subtract).then_inc(lo, 1)

            def clear_max(b, par):
                if has(b, 2):
                    pool.wait_ge(qmT_ps, 2 * (b - 1))
                else:
                    pool.wait_ge(zeroed, 2)
                nc.gpsimd.tensor_tensor(QS[:, par, :, 24], KS[:, :, 25], KS[:, :, 25], ALU.add).then_inc(m_zero, 1)

            def newton(b):
                y, v, t = NW2[:, 2:3], NW2[:, 4:5], NW2[:, 3:4]
                pool.wait_ge(ln2, LN2 * (b + 1))
                if has(b, 1):
                    pool.wait_ge(newton2, NEWTON * b)
                n = 0
                for _ in range(3):
                    for o, a, c, op in ((t, y, y, ALU.mult), (t, t, v, ALU.mult), (t, t, C15[:], ALU.add),
                                        (y, y, t, ALU.mult)):
                        if n:
                            pool.wait_ge(newton2, NEWTON * b + n)
                        nc.gpsimd.tensor_tensor(o, a, c, op).then_inc(newton2, 1)
                        n += 1

            def v_place(b, par):
                pool.wait_ge(v_raw, b + 1)
                if has(b, 2):
                    pool.wait_ge(av_ps, AV * (b - 1))
                zero = KS[:, 0:16, 25:26].unsqueeze(2).to_broadcast([P, 16, 2, HD])
                nc.gpsimd.tensor_tensor(VA[:, par].rearrange("p n (s c) -> p n s c", s=2)[:, :, :, 0:HD],
                                        VRAW.rearrange("p (n s c) -> p n s c", s=2, c=HD), zero,
                                        ALU.add).then_inc(v_done, 1)

            def front(b, par):
                rotate(b, k_terms, KA, KB, KR, k_hi, k_lo, k_rot)
                low16(b, KR, KS, HD, k_hi, k_lo)
                rotate(b, q_terms, QA, QB, QR, q_hi, q_lo, q_rot)
                clear_max(b, par)
                low16(b, QR, QS[:, par], 2 * HD, q_hi, q_lo)
                if live(b + 1):
                    c_low(b + 1)
                v_place(b, par)
                if has(b, 2):
                    add_bias(b)

            def newton1(part):
                s = PARTS[part]
                v, y, t = NW1[:, 0, s], RS1[:, s], NW1[:, 2, s]
                n = NEWTON * part
                pool.wait_ge(guess1, 3 * (part + 1))
                for k in range(3):
                    for o, a, c in ((t, y, y), (t, t, v), (t, t, None), (y, y, t)):
                        if n > NEWTON * part:
                            pool.wait_ge(rstd1, n)
                        if c is None:
                            nc.gpsimd.tensor_scalar(o, a, -0.5, 1.5, ALU.mult, ALU.add).then_inc(rstd1, 1)
                        else:
                            nc.gpsimd.tensor_tensor(o, a, c, ALU.mult).then_inc(rstd1, 1)
                        n += 1

            def low_third(e, n):
                c = slice(512 * n, 512 * (n + 1))
                pool.wait_ge(wh_done, 3 * e + n + 1)
                nc.gpsimd.tensor_tensor(WL[:, e, c], WS[:, e, c], WH[:, e, c].bitcast(F32),
                                        ALU.subtract).then_inc(wl_done, 1)

            def split_expert(e, slot):
                for n in range(3):
                    c = slice(512 * n, 512 * (n + 1))
                    nc.gpsimd.tensor_scalar(WH[:, slot, c], WS[:, slot, c], 1.0, None, ALU.mult).then_inc(wh_done, 1)
                    pool.wait_ge(wh_done, 3 * e + n + 1)
                    nc.gpsimd.tensor_tensor(WL[:, slot, c], WS[:, slot, c], WH[:, slot, c].bitcast(F32),
                                            ALU.subtract).then_inc(wl_done, 1)

            def step(i, par):
                if i_is(i, -2):
                    newton1(0)
                    c_low(0)
                if live(i + 2):
                    front(i + 2, par)
                if i_is(i, -2):
                    project_low(2)
                if i_is(i, 0):
                    newton1(1)
                if i_is(i, -1):
                    project_low(3)
                    pool.wait_ge(tanh_done, 1)
                    nc.gpsimd.tensor_scalar(TGB[:], BOUT[:], TG2[:, 0:1], None, ALU.mult).then_inc(tgb_done, 1)
                    add_bias(0)
                    add_bias(1)
                if live(i - 1):
                    newton(i - 1)
                if isinstance(i, int) and i in SPLIT_STEPS[:-1]:
                    low_third(*divmod(SPLIT_STEPS.index(i), 3))

            def router(lo, hi, rp, ra, rd, between=None):
                cnt = [rp]
                s = slice(lo, hi)
                n = hi - lo

                def did(ins):
                    cnt[0] += 1
                    ins.then_inc(r_pool, 1)
                    pool.wait_ge(r_pool, cnt[0])

                th, sig, dist, zone, tmp, e1, e3, w = [RT[:, k, s, :] for k in range(8)]
                gt, eq = RC[:, 0, s], RC[:, 1, s]
                diff = gt
                wsum, none, some, fsum = [RV[:, k, s] for k in range(4)]

                def wide(v):
                    return v.unsqueeze(2).to_broadcast([P, n, NE])

                if rp == 0:
                    pool.wait_ge(c_lo, B)
                pool.wait_ge(r_act, ra + 1)
                did(nc.gpsimd.tensor_scalar(sig, th, 0.5, 0.5, ALU.mult, ALU.add))
                did(nc.gpsimd.tensor_scalar(zone, sig, LOWER, None, ALU.is_ge))
                did(nc.gpsimd.tensor_scalar(tmp, sig, UPPER, None, ALU.is_le))
                did(nc.gpsimd.tensor_tensor(zone, zone, tmp, ALU.mult))
                did(nc.gpsimd.tensor_scalar(sig, sig, CENTER, None, ALU.subtract))
                assert cnt[0] == rp + 5
                pool.wait_ge(r_act, ra + 2)
                mine = dist.unsqueeze(3).to_broadcast([P, n, NE, NE])
                other = dist.unsqueeze(2).to_broadcast([P, n, NE, NE])
                did(nc.gpsimd.tensor_tensor(diff, mine, other, ALU.subtract))
                if between is not None:
                    newton(between)
                did(nc.gpsimd.tensor_scalar(eq, diff, 0.0, None, ALU.is_equal))
                did(nc.gpsimd.tensor_scalar(gt, diff, 0.0, None, ALU.is_gt))
                did(nc.gpsimd.tensor_tensor(eq, eq, TRI[:].unsqueeze(1).to_broadcast([P, n, NE, NE]), ALU.mult))
                did(nc.gpsimd.tensor_tensor(gt, gt, eq, ALU.add))
                pool.wait_ge(r_dve, rd + 1)
                did(nc.gpsimd.tensor_scalar(tmp, tmp, 1.5, None, ALU.is_lt))
                pool.wait_ge(r_act, ra + 4)
                did(nc.gpsimd.tensor_tensor(e3, e3, tmp, ALU.mult))
                did(nc.gpsimd.tensor_tensor(w, e1, zone, ALU.mult))
                pool.wait_ge(r_dve, rd + 5)
                did(nc.gpsimd.tensor_tensor(e3, e3, wide(fsum), ALU.mult))
                did(nc.gpsimd.tensor_scalar(none, wsum, 1e-8, None, ALU.is_lt))
                did(nc.gpsimd.tensor_scalar(some, none, -1.0, 1.0, ALU.mult, ALU.add))
                did(nc.gpsimd.tensor_tensor(e3, e3, wide(none), ALU.mult))
                did(nc.gpsimd.tensor_tensor(w, w, wide(some), ALU.mult))
                did(nc.gpsimd.tensor_tensor(w, w, e3, ALU.add))
                pool.wait_ge(r_dve, rd + 8)
                did(nc.gpsimd.tensor_scalar(tmp, w, TG2[:, 1:2], None, ALU.mult))
                did(nc.gpsimd.tensor_tensor(WT[:, s, :], tmp, wide(wsum), ALU.mult))
                assert cnt[0] == rp + 21

            pipeline(pool, step)
            router(0, B - TG, 0, 0, 0, between=B - 1)
            low_third(1, 2)
            router(B - TG, B, 21, 4, 8)

            for e in range(2, NE):
                pool.wait_ge(d_ws[e % 2], 16 * (e // 2 + 1))
                pool.wait_ge(d_ps, HALVES * NG * (e - 1))
                split_expert(e, e % 2)

        @block.scalar
        def _(act):
            act.dma_start(POS[:], pos.rearrange("b t c -> t b c")).then_inc(d_pos, 16)
            act.dma_start(CTX[:, 0:CTX0], ctxT[:, 0:CTX0]).then_inc(d_ctx[0], 16)
            act.dma_start(PW[:, 1, :], Wkv).then_inc(d_pw[1], 16)
            act.dma_start(ID[:], ident).then_inc(d_const, 16)

            def project_high(n):
                if n == 3:
                    act.wait_ge(d_late, 48)
                    nc.scalar.activation(RWH[:], RW[:], ACT.Copy).then_inc(pw_hi, 1)
                else:
                    act.wait_ge(d_pw[PW_ORDER[n]], 16)
                    nc.scalar.activation(PWH[:, PW_ORDER[n], :], PW[:, PW_ORDER[n], :], ACT.Copy).then_inc(pw_hi, 1)

            def clear_kp(par):
                act.wait_ge(zeroed, 1)
                nc.scalar.activation(KP[:, par].rearrange("p j g n -> p (j g n)").bitcast(F32),
                                     ZERO[:].to_broadcast([P, QUAD * GROUPS * P // 2]), ACT.Copy).then_inc(kp_zeroed, 1)

            def c_high(b):
                if has(b, 1):
                    act.wait_ge(kv_ps, b)
                    act.wait_ge(c_lo, b)
                else:
                    act.wait_ge(d_ctx[0], 16)
                if isinstance(b, int) and b == CTX0 // P:
                    act.wait_ge(d_ctx[1], 16)
                nc.scalar.activation(CH[:], CTX[:, bass.ds(b * P, P)], ACT.Copy).then_inc(c_hi, 1)

            def norm1(b):
                act.wait_ge(shift1_done, 1 if isinstance(b, int) and b < PARTS[1].start else 2)
                if has(b, 1):
                    act.wait_ge(hT_ps, b)
                nc.scalar.activation(H[:].unsqueeze(1), X[:, bass.ds(b, 1), :], ACT.Identity,
                                     bias=NB1[:, bass.ds(b, 1)], scale=RS1[:, bass.ds(b, 1)]).then_inc(h_ready, 1)

            def hT_high(b):
                act.wait_ge(hT_ps, b + 1)
                if has(b, 1):
                    act.wait_ge(q_ps, b)
                    act.wait_ge(hT_lo, b)
                nc.scalar.activation(HTH[:], HBANK[:, 0:D], ACT.Copy).then_inc(hT_hi, 1)

            def v_evac(b):
                act.wait_ge(k_terms, 3 * (b + 1))
                if has(b, 1):
                    act.wait_ge(v_done, b)
                nc.scalar.activation(VRAW, TBANK[:, D:2 * D], ACT.Copy).then_inc(v_raw, 1)

            def k_evac(b):
                act.wait_ge(kT_ps, b + 1)
                if has(b, 1):
                    act.wait_ge(kp_dma, 16 * QUAD * b)
                nc.scalar.activation(KT[:], TB16, ACT.Copy).then_inc(kT_sb, 1)

            def q_evac(b, par):
                act.wait_ge(qT_ps, b + 1)
                if has(b, 2):
                    act.wait_ge(p1_ps, UNITS * (b - 1))
                nc.scalar.activation(QTA[par].rearrange("p g n -> p (g n)"), HB16, ACT.Copy).then_inc(qT_sb, 1)

            def qm_evac(b, half):
                act.wait_ge(qmT_ps, 2 * b + half + 1)
                if has(b, 1):
                    act.wait_ge(p2_ps, UNITS * (b - 1) + 4 * (half + 1))
                s = slice(GROUPS // 2 * half, GROUPS // 2 * (half + 1))
                nc.scalar.activation(QTB[:, s, :].rearrange("p g n -> p (g n)"),
                                     [TB16, OB16][half][:, 512 * half:512 * (half + 1)],
                                     ACT.Copy).then_inc(qmT_sb, 1)

            def exps(b, u):
                act.wait_ge(p2_ps, UNITS * b + u + 1)
                if has(b, 1) or u >= 4:
                    act.wait_ge(av_ps, AV * b + u // 2 - 1)
                nc.scalar.activation(E[:, u % 4, :], LT[u % 2], ACT.Exp, scale=SCALE).then_inc(exp_done, 1)

            def o_evac(b):
                act.wait_ge(av_ps, AV * (b + 1))
                if has(b, 1):
                    act.wait_ge(oT_ps, b)
                nc.scalar.activation(OS[:], OBANK, ACT.Copy).then_inc(o_sb, 1)

            def a_high(b):
                act.wait_ge(aT_ps, b + 1)
                if has(b, 1):
                    act.wait_ge(proj_ps, b)
                    act.wait_ge(a_lo, b)
                nc.scalar.activation(ATH[:], YBANK[:, 0:D], ACT.Copy).then_inc(a_hi, 1)

            def h2_high(b):
                act.wait_ge(h2T_ps, b + 1)
                nc.scalar.activation(H2H[:, :, bass.ds(b * P, P)],
                                     YBANK[:, 0:D].rearrange("p (k n) -> p k n", k=DK), ACT.Copy).then_inc(h2_hi, 1)

            def step(i, par):
                a, f, b, t, w = i + 2, i + 1, i, i - 1, i - 2
                A, Fr, Bk, Tl, Wl = [live(n) for n in (a, f, b, t, w)]
                if i_is(i, -2):
                    c_high(0)
                    project_high(0)
                    project_high(1)
                    act.wait_ge(angles, 8)
                    nc.scalar.activation(TRIG[:, 0:2].rearrange("p a b c -> p (a b c)"),
                                         ANG[:].rearrange("p a b c -> p (a b c)"), ACT.Sin).then_inc(trig, 1)
                    norm1(0)
                if Bk:
                    exps(b, 0)
                    qm_evac(b, 1)
                if A:
                    hT_high(a)
                if i_is(i, -2):
                    clear_kp(0)
                if Bk:
                    exps(b, 1)
                    exps(b, 2)
                    exps(b, 3)
                if A:
                    v_evac(a)
                if A and live(a + 1):
                    c_high(a + 1)
                if isinstance(i, int) and i in SPLIT_STEPS:
                    k = SPLIT_STEPS.index(i)
                    act.wait_ge(lora_added, k + 1)
                    c = slice(512 * (k % 3), 512 * (k % 3 + 1))
                    nc.scalar.activation(WH[:, k // 3, c], WS[:, k // 3, c], ACT.Copy).then_inc(wh_done, 1)
                if i_is(i, -2):
                    clear_kp(1)
                if i_is(i, -1):
                    act.wait_ge(d_gate, 48)
                    nc.scalar.activation(TG2[:], GATE[:], ACT.Tanh).then_inc(tanh_done, 1)
                    project_high(3)
                if Tl:
                    a_high(t)
                if Bk:
                    exps(b, 4)
                    exps(b, 5)
                if Bk:
                    exps(b, 6)
                if A:
                    k_evac(a)
                if Bk:
                    exps(b, 7)
                if Fr:
                    qm_evac(f, 0)
                if Wl:
                    h2_high(w)
                if Bk:
                    o_evac(b)
                if A and live(a + 1):
                    norm1(a + 1)
                if A:
                    q_evac(a, par)
                if i_is(i, -2):
                    project_high(2)

            def router_tanh(lo, hi):
                s = slice(lo, hi)
                act.wait_ge(rtT_sb, hi // TG)
                act.wait_ge(inv_temp, 2)
                nc.scalar.activation(RT[:, 0, s, :], LG[:, s, :], ACT.Tanh, scale=HIT[:, 1:2]).then_inc(r_act, 1)

            def router_exps(lo, hi, rp, ra):
                s = slice(lo, hi)
                act.wait_ge(r_pool, rp + 5)
                nc.scalar.activation(RT[:, 2, s, :], RT[:, 1, s, :], ACT.Abs).then_inc(r_act, 1)
                act.wait_ge(r_act, ra + 2)
                nc.scalar.activation(RT[:, 5, s, :], RT[:, 2, s, :], ACT.Exp, scale=-1.0 / 0.1).then_inc(r_act, 1)
                nc.scalar.activation(RT[:, 6, s, :], RT[:, 2, s, :], ACT.Exp, scale=-1.0 / 0.3).then_inc(r_act, 1)

            pipeline(act, step)

            def silu(n, c):
                act.wait_ge(g_ps, FK * n + c + 1)
                if has(n, 1):
                    act.wait_ge(m_done, FK * (n - 1) + c + 1)
                nc.scalar.activation(SIL[:, c, :], PS[:, c, :], ACT.Silu).then_inc(silu_done, 1)

            def mid_high(n, c, par):
                act.wait_ge(m_done, FK * n + c + 1)
                if has(n, 2):
                    act.wait_ge(d_ps, HALVES * (n - 1))
                    act.wait_ge(ml_done, FK * (n - 2) + c + 1)
                nc.scalar.activation(MH[:, par, c, :], MID[:, c, :], ACT.Copy).then_inc(mh_done, 1)

            def group(n, par):
                for c in range(FK):
                    silu(n, c)
                for c in range(FK):
                    mid_high(n, c, par)

            router_tanh(0, B - TG)
            a_high(B - 1)
            router_exps(0, B - TG, 0, 0)
            silu(0, 0)
            h2_high(B - 2)
            silu(0, 1)
            mid_high(0, 0, 0)
            h2_high(B - 1)
            mid_high(0, 1, 0)
            silu(1, 0)
            silu(1, 1)
            mid_high(1, 0, 1)
            router_tanh(B - TG, B)
            mid_high(1, 1, 1)
            group(2, 0)
            router_exps(B - TG, B, 21, 4)
            group(3, 1)
            with act.Fori(4, NE * NG, 2) as n:
                n = act.snap(n)
                group(n, 0)
                group(n + 1, 1)

        @block.vector
        def _(dve):
            def stats1_of(b):
                if b % 4 == 0:
                    dve.wait_ge(d_x[b // 4], 16)
                nc.vector.bn_stats(ST1[:, b, :], X[:, b, :]).then_inc(stats1, 1)

            def guess1_of(part):
                s = PARTS[part]
                for b in range(s.start, s.stop):
                    dve.wait_ge(stats1, s.start + b + 1)
                    nc.vector.bn_aggr(MV1[:, b, :], ST1[:, b, :]).then_inc(stats1, 1)
                dve.wait_ge(stats1, 2 * s.stop)
                v = NW1[:, 0, s]
                nc.vector.tensor_scalar(v, MV1[:, s, 1], EPS, None, ALU.add).then_inc(guess1, 1)
                dve.wait_ge(guess1, 3 * part + 1)
                nc.vector.tensor_scalar(NW1[:, 1, s].bitcast(I32), v.bitcast(I32), 1, None,
                                        ALU.arith_shift_right).then_inc(guess1, 1)
                dve.wait_ge(guess1, 3 * part + 2)
                nc.vector.tensor_scalar(RS1[:, s].bitcast(I32), NW1[:, 1, s].bitcast(I32), -1.0, float(0x5f3759df),
                                        ALU.mult, ALU.add).then_inc(guess1, 1)

            for b in range(PARTS[0].stop):
                stats1_of(b)
            guess1_of(0)
            dve.wait_ge(d_pos, 16)
            posv = POS[:].rearrange("p b c -> p (b c)")
            for n in range(2):
                nc.vector.tensor_scalar(ANG[:, 0, :, n], posv, FREQ[n], None, ALU.mult).then_inc(angles, 1)
            dve.wait_ge(angles, 2)
            flat = ANG[:].rearrange("p a b c -> p a (b c)")
            nc.vector.tensor_scalar(flat[:, 1, :], flat[:, 0, :], math.pi / 2, None, ALU.add).then_inc(angles, 1)
            dve.wait_ge(angles, 3)
            nc.vector.tensor_scalar(TURN[:], flat, 1.0 / TWO_PI, ROUND, ALU.mult, ALU.add).then_inc(angles, 1)
            dve.wait_ge(angles, 4)
            nc.vector.tensor_scalar(TURN[:], TURN[:], ROUND, None, ALU.subtract).then_inc(angles, 1)
            dve.wait_ge(angles, 5)
            nc.vector.scalar_tensor_tensor(flat, TURN[:], -PI2_HI, flat, ALU.mult, ALU.add).then_inc(angles, 1)
            dve.wait_ge(angles, 6)
            nc.vector.scalar_tensor_tensor(flat, TURN[:], -PI2_LO, flat, ALU.mult, ALU.add).then_inc(angles, 1)
            dve.wait_ge(angles, 7)
            nc.vector.tensor_scalar(flat, flat, 3.1415925, -3.1415925, ALU.min, ALU.max).then_inc(angles, 1)

            def project_low(n):
                w = PW_ORDER[n]
                dve.wait_ge(pw_hi, n + 1)
                nc.vector.tensor_tensor(PWL[:, w, :], PW[:, w, :], PWH[:, w, :].bitcast(F32),
                                        ALU.subtract).then_inc(pw_lo, 1)

            def shift1(part):
                dve.wait_ge(rstd1, NEWTON * (part + 1))
                r = PARTS[part]
                nc.vector.scalar_tensor_tensor(NB1[:, r], MV1[:, r, 0], -1.0, RS1[:, r],
                                               ALU.mult, ALU.mult).then_inc(shift1_done, 1)

            def hT_low(b):
                dve.wait_ge(hT_hi, b + 1)
                if has(b, 1):
                    dve.wait_ge(q_ps, b)
                nc.vector.tensor_tensor(HTL[:], HBANK[:, 0:D], HTH[:].bitcast(F32), ALU.subtract).then_inc(hT_lo, 1)

            def rope(b, bank, ready, ta, tb, rot, terms):
                dve.wait_ge(ready, b + 1)
                if has(b, 1):
                    dve.wait_ge(rot, b)
                src = bank.rearrange("p (h a c) -> p h a c", h=HEADS, a=4)
                da = ta[:].rearrange("p (h a c) -> p h a c", h=HEADS, a=4)
                db = tb[:].rearrange("p (h a c) -> p h a c", h=HEADS, a=4)
                sin, cos, nsin = [TRIG[:, k, bass.ds(b, 1), :] for k in range(3)]
                nc.vector.tensor_tensor(da, src, cos.unsqueeze(3).to_broadcast([P, HEADS, 4, 2]),
                                        ALU.mult).then_inc(terms, 1)
                nc.vector.tensor_tensor(db[:, :, :, 0], src[:, :, :, 1], nsin.to_broadcast([P, HEADS, 4]),
                                        ALU.mult).then_inc(terms, 1)
                nc.vector.tensor_tensor(db[:, :, :, 1], src[:, :, :, 0], sin.to_broadcast([P, HEADS, 4]),
                                        ALU.mult).then_inc(terms, 1)

            def high16(b, rot, S, gap, done, hi, free, back, per):
                dve.wait_ge(done, b + 1)
                if has(b, back):
                    dve.wait_ge(free, per * (b - back + 1))
                else:
                    dve.wait_ge(zeroed, 4)
                src = rot[:].rearrange("p (h d) -> p h d", d=HD).unsqueeze(2).to_broadcast([P, HEADS, 2, HD])
                dst = S[:, :, 0:2 * gap].rearrange("p h (r d) -> p h r d", r=2)[:, :, :, 0:HD]
                nc.vector.tensor_copy(dst, src).then_inc(hi, 1)

            def row_max(b, u, par):
                dve.wait_ge(p1_ps, UNITS * b + u + 1)
                if u == 0:
                    dve.wait_ge(qT_ps, b + 1)
                nc.vector.tensor_reduce(QS[:, par, UH * u:UH * (u + 1), 24],
                                        LM[u % 2].rearrange("p (h n) -> p h n", h=UH),
                                        AX_X, ALU.max).then_inc(max_done, 1)

            def divide(b):
                dve.wait_ge(oT_ps, b + 1)
                o = YBANK.rearrange("p (n c) -> p n c", c=ROWS)
                if has(b, 1):
                    dve.wait_ge(attn, b)
                nc.vector.reciprocal(RSUM[:], o[:, :, 16:18]).then_inc(sums_inv, 1)
                dve.wait_ge(sums_inv, b + 1)
                if has(b, 1):
                    dve.wait_ge(aT_ps, b)
                nc.vector.tensor_tensor(AT[:].rearrange("p (n s c) -> p n s c", s=2, c=HD),
                                        o[:, :, 0:16].rearrange("p n (s c) -> p n s c", s=2),
                                        RSUM[:].unsqueeze(3).to_broadcast([P, HEADS // 2, 2, HD]),
                                        ALU.mult).then_inc(attn, 1)

            def a_low(b):
                dve.wait_ge(a_hi, b + 1)
                nc.vector.tensor_tensor(ATL[:], YBANK[:, 0:D], ATH[:].bitcast(F32), ALU.subtract).then_inc(a_lo, 1)

            def residual(b):
                dve.wait_ge(proj_ps, b + 1)
                dve.wait_ge(xb_done, b + 1)
                nc.vector.scalar_tensor_tensor(X[:, bass.ds(b, 1), :], YBANK[:, 0:D].unsqueeze(1), TG2[:, 0:1],
                                               X[:, bass.ds(b, 1), :], ALU.mult, ALU.add).then_inc(x1_done, 1)

            def stats2(b):
                dve.wait_ge(x1_done, b + 1)
                if has(b, 1):
                    dve.wait_ge(ln2, LN2 * b)
                nc.vector.memset(TICK[:], 0.0).then_inc(ln2, 1)
                nc.vector.bn_stats(ST2[:].unsqueeze(1), X[:, bass.ds(b, 1), :]).then_inc(ln2, 1)

            def variance2(b):
                dve.wait_ge(ln2, LN2 * b + 2)
                if has(b, 1):
                    dve.wait_ge(h2_ready, b)
                nc.vector.memset(TICK[:], 0.0).then_inc(ln2, 1)
                nc.vector.bn_aggr(MV2[:], ST2[:]).then_inc(ln2, 1)

            def add_eps2(b):
                dve.wait_ge(ln2, LN2 * b + 4)
                if has(b, 1):
                    dve.wait_ge(newton2, NEWTON * b)
                nc.vector.tensor_scalar(NW2[:, 0:1], MV2[:, 1:2], EPS, None, ALU.add).then_inc(ln2, 1)

            def halves2(b):
                dve.wait_ge(ln2, LN2 * b + 5)
                nc.vector.tensor_scalar(NW2[:, 1:2].bitcast(I32), NW2[:, 0:1].bitcast(I32), 1, None,
                                        ALU.arith_shift_right).then_inc(ln2, 1)
                nc.vector.tensor_scalar(NW2[:, 4:5], NW2[:, 0:1], -0.5, None, ALU.mult).then_inc(ln2, 1)

            def guess2(b):
                dve.wait_ge(ln2, LN2 * b + 7)
                nc.vector.tensor_scalar(NW2[:, 2:3].bitcast(I32), NW2[:, 1:2].bitcast(I32), -1.0,
                                        float(0x5f3759df), ALU.mult, ALU.add).then_inc(ln2, 1)

            def norm2(b):
                dve.wait_ge(newton2, NEWTON * (b + 1))
                if has(b, 1):
                    dve.wait_ge(h2T_ps, b)
                nc.vector.tensor_scalar(H2[:].unsqueeze(1), X[:, bass.ds(b, 1), :], MV2[:, 0:1], NW2[:, 2:3],
                                        ALU.subtract, ALU.mult).then_inc(h2_ready, 1)

            def h2_low(b):
                dve.wait_ge(h2_hi, b + 1)
                part = (slice(None), slice(None), bass.ds(b * P, P))
                nc.vector.tensor_tensor(H2L[part], YBANK[:, 0:D].rearrange("p (k n) -> p k n", k=DK),
                                        H2H[part].bitcast(F32), ALU.subtract).then_inc(h2_lo, 1)

            def add_lora(k):
                e, n = divmod(k, 3)
                if n == 0:
                    dve.wait_ge(d_ws[e], 16)
                dve.wait_ge(lora_ps, k + 1)
                w = WS[:, e, 512 * n:512 * (n + 1)]
                nc.vector.tensor_tensor(w, w, PS[:, LORA_BANK[k], :], ALU.add).then_inc(lora_added, 1)

            def logits_evac(g):
                dve.wait_ge(rt_ps, g + 1)
                if g:
                    dve.wait_ge(rtT_ps, g)
                else:
                    dve.wait_ge(kp_dma, 16 * QUAD * B)
                nc.vector.tensor_copy(RTS[:], RT_BANKS[g][0][0:NE, :]).then_inc(rt_sb, 1)

            def logits_place(g):
                dve.wait_ge(rtT_ps, g + 1)
                nc.vector.tensor_copy(LG[:, TG * g:TG * (g + 1), :].rearrange("p b e -> p (b e)"),
                                      RT_BANKS[g][1][:, 0:TG * NE]).then_inc(rtT_sb, 1)

            def step(i, par):
                a, f, t, w = i + 2, i + 1, i - 1, i - 2
                A, Fr, Tl, Wl = [live(n) for n in (a, f, t, w)]
                start, final = i_is(i, -2) or i_is(i, -1), i_is(i, B - 1)

                def row(u):
                    if Fr:
                        row_max(f, u, 1 - par)

                if i_is(i, -2):
                    project_low(0)
                    shift1(0)
                    project_low(1)
                    dve.wait_ge(trig, 1)
                    nc.vector.tensor_scalar(TRIG[:, 2], TRIG[:, 0], -1.0, None, ALU.mult).then_inc(neg_sin, 1)
                    dve.wait_ge(neg_sin, 1)
                if start:
                    hT_low(a)
                if A:
                    rope(a, TBANK[:, 0:D], kv_ps, KA, KB, k_rot, k_terms)
                if start:
                    high16(a, KR, KS, 2 * HD, k_rot, k_hi, kT_ps, 1, 1)
                if Tl:
                    divide(t)
                if final:
                    logits_evac(0)
                if A and not start:
                    hT_low(a)
                row(0)
                if i_is(i, 0):
                    add_lora(5)
                if i_is(i, 1):
                    shift1(1)
                row(1)
                if Wl:
                    norm2(w)
                if A:
                    if not start:
                        high16(a, KR, KS, 2 * HD, k_rot, k_hi, kT_ps, 1, 1)
                    rope(a, HBANK[:, D:2 * D], q_ps, QA, QB, q_rot, q_terms)
                row(2)
                if final:
                    logits_place(0)
                if Tl:
                    a_low(t)
                if final:
                    logits_evac(1)
                    logits_place(1)
                row(3)
                if A:
                    high16(a, QR, QS[:, par], HD, q_rot, q_hi, qmT_ps, 2, 2)
                row(4)
                if Tl:
                    residual(t)
                row(5)
                if Tl:
                    stats2(t)
                row(6)
                if Tl:
                    variance2(t)
                if final:
                    logits_evac(2)
                if Wl:
                    h2_low(w)
                row(7)
                if Tl:
                    add_eps2(t)
                if final:
                    logits_place(2)
                if Tl:
                    halves2(t)
                    guess2(t)
                if i_is(i, -2):
                    for n in range(PARTS[1].start, 3 * B // 4):
                        stats1_of(n)
                    add_lora(0)
                    add_lora(1)
                if i_is(i, -1):
                    add_lora(2)
                    add_lora(3)
                    add_lora(4)
                    for n in range(3 * B // 4, B):
                        stats1_of(n)
                    guess1_of(1)
                    dve.wait_ge(d_gate, 48)
                    nc.vector.reciprocal(HIT[:, 0:1], TEMP[:]).then_inc(inv_temp, 1)
                    dve.wait_ge(inv_temp, 1)
                    nc.vector.tensor_scalar(HIT[:, 1:2], HIT[:, 0:1], 0.5, None, ALU.mult).then_inc(inv_temp, 1)

            def router_ranks(lo, hi, rp):
                s = slice(lo, hi)
                dve.wait_ge(r_pool, rp + 10)
                nc.vector.tensor_reduce(RT[:, 4, s, :], RC[:, 0, s], AX_X, ALU.add).then_inc(r_dve, 1)

            def router_sums(lo, hi, rp, rd):
                s = slice(lo, hi)
                e3, w, wsum, fsum, raw = RT[:, 6, s, :], RT[:, 7, s, :], RV[:, 0, s], RV[:, 3, s], RV[:, 4, s]
                dve.wait_ge(r_pool, rp + 13)
                nc.vector.tensor_reduce(wsum, w, AX_X, ALU.add).then_inc(r_dve, 1)
                nc.vector.tensor_reduce(raw, e3, AX_X, ALU.add).then_inc(r_dve, 1)
                dve.wait_ge(r_dve, rd + 3)
                nc.vector.tensor_scalar(raw, raw, 1e-8, None, ALU.max).then_inc(r_dve, 1)
                dve.wait_ge(r_dve, rd + 4)
                nc.vector.reciprocal(fsum, raw).then_inc(r_dve, 1)

            def router_total(lo, hi, rp, rd):
                s = slice(lo, hi)
                w, wsum, raw = RT[:, 7, s, :], RV[:, 0, s], RV[:, 4, s]
                dve.wait_ge(r_pool, rp + 19)
                dve.wait_ge(r_dve, rd + 5)
                nc.vector.tensor_reduce(raw, w, AX_X, ALU.add).then_inc(r_dve, 1)
                dve.wait_ge(r_dve, rd + 6)
                nc.vector.tensor_scalar(raw, raw, 1e-8, None, ALU.max).then_inc(r_dve, 1)
                dve.wait_ge(r_dve, rd + 7)
                nc.vector.reciprocal(wsum, raw).then_inc(r_dve, 1)

            pipeline(dve, step)

            def mid_product(n, c):
                dve.wait_ge(silu_done, FK * n + c + 1)
                dve.wait_ge(u_ps, FK * n + c + 1)
                if has(n, 1):
                    dve.wait_ge(mh_done, FK * (n - 1) + c + 1)
                    dve.wait_ge(ml_done, FK * (n - 1) + c + 1)
                nc.vector.tensor_tensor(MID[:, c, :], SIL[:, c, :], PS[:, 2 + c, :], ALU.mult).then_inc(m_done, 1)

            def mid_low(n, c, par):
                dve.wait_ge(mh_done, FK * n + c + 1)
                if has(n, 2):
                    dve.wait_ge(d_ps, HALVES * (n - 1))
                nc.vector.tensor_tensor(ML[:, par, c, :], MID[:, c, :], MH[:, par, c, :].bitcast(F32),
                                        ALU.subtract).then_inc(ml_done, 1)

            def mid(n, par):
                for c in range(FK):
                    mid_product(n, c)
                for c in range(FK):
                    mid_low(n, c, par)

            def accumulate(n, e, g, par):
                if has(n, NG):
                    dve.wait_ge(acc_done, CREDIT + TG * (n - NG + 1))
                else:
                    dve.wait_ge(r_pool, 42 if g == NG - 1 else 21)
                for k in range(TG):
                    if k % 2 == 0:
                        dve.wait_ge(d_ps, HALVES * n + k // 2 + 1)
                    tile = TG * g + k
                    o = PS[:, OUT_BANK[par]:OUT_BANK[par] + 2, :].rearrange("p a (c d) -> p (a c) d", c=2)[:, k, :]
                    nc.vector.scalar_tensor_tensor(X[:, tile, :], o, WT[:, tile, bass.ds(e, 1)], X[:, tile, :],
                                                   ALU.mult, ALU.add).then_inc(acc_done, 1)

            divide(B - 1)
            norm2(B - 2)
            a_low(B - 1)
            residual(B - 1)
            stats2(B - 1)
            variance2(B - 1)
            add_eps2(B - 1)
            halves2(B - 1)
            guess2(B - 1)
            mid_product(0, 0)
            h2_low(B - 2)
            mid_product(0, 1)
            mid_low(0, 0, 0)
            norm2(B - 1)
            mid_low(0, 1, 0)
            h2_low(B - 1)
            mid_product(1, 0)
            mid_product(1, 1)
            logits_evac(NG - 1)
            logits_place(NG - 1)
            router_ranks(0, B - TG, 0)
            mid_low(1, 0, 1)
            mid_low(1, 1, 1)
            router_sums(0, B - TG, 0, 0)
            router_total(0, B - TG, 0, 0)
            accumulate(0, 0, 0, 0)
            mid(2, 0)
            accumulate(1, 0, 1, 1)
            mid(3, 1)
            accumulate(2, 0, 2, 0)
            router_ranks(B - TG, B, 21)
            mid(4, 0)
            router_sums(B - TG, B, 21, 8)
            router_total(B - TG, B, 21, 8)
            accumulate(3, 0, 3, 1)
            with dve.Fori(1, NE - 1, 1) as e:
                e = dve.snap(e)
                for g in range(NG):
                    mid(e * NG + (g + 1), (g + 1) % 2)
                    accumulate(e * NG + g, e, g, g % 2)
            for g in range(NG):
                n = NG * (NE - 1) + g
                if g < NG - 1:
                    mid(n + 1, (g + 1) % 2)
                accumulate(n, NE - 1, g, g % 2)

        @block.tensor
        def _(pe):
            mm = nc.tensor.matmul

            def low_rank(k):
                e, n = divmod(k, 3)
                if k == 0:
                    pe.wait_ge(d_lora, 16 * 6)
                for j in range(DK):
                    last = mm(PS[:, LORA_BANK[k], F * j:F * (j + 1)], LORA_A[:, n, e, P * j:P * (j + 1)],
                              LORA_B[:, n, e, :], start=True, stop=True)
                last.then_inc(lora_ps, 1)

            def product(dst, pairs):
                last = None
                ops = []
                for (sh, sl), (mh, ml) in pairs:
                    ops += [(sh, mh), (sh, ml), (sl, mh)]
                for n, (s, m) in enumerate(ops):
                    last = mm(dst, s, m, start=n == 0, stop=n == len(ops) - 1)
                return last

            def transpose_h(b):
                pe.wait_ge(h_ready, b + 1)
                if has(b, 1):
                    pe.wait_ge(qT_sb, b)
                else:
                    pe.wait_ge(d_const, 16 * 2)
                for k in range(DK):
                    last = nc.tensor.transpose(HBANK[:, P * k:P * (k + 1)], H[:, P * k:P * (k + 1)], ID[:])
                last.then_inc(hT_ps, 1)

            def project_kv(b):
                pe.wait_ge(c_lo, b + 1)
                if has(b, 2):
                    pe.wait_ge(qmT_sb, 2 * (b - 2) + 1)
                elif has(b, 1):
                    pe.wait_ge(kT_sb, b)
                else:
                    pe.wait_ge(pw_lo, 1)
                product(TBANK, [((CH[:], CL[:]), (PWH[:, 1, :], PWL[:, 1, :]))]).then_inc(kv_ps, 1)

            def project_q(b):
                pe.wait_ge(hT_lo, b + 1)
                if not has(b, 1):
                    pe.wait_ge(pw_lo, 2)
                product(HBANK[:, D:2 * D],
                        [((HTH[:, P * k:P * (k + 1)], HTL[:, P * k:P * (k + 1)]),
                          (PWH[:, 0, D * k:D * (k + 1)], PWL[:, 0, D * k:D * (k + 1)]))
                         for k in range(DK)]).then_inc(q_ps, 1)

            def transpose16(S, lo, hi, done, bank=TB16):
                for g in range(lo, hi):
                    last = nc.tensor.transpose(bank[:, P * g:P * (g + 1)],
                                               S[:, QUAD * g:QUAD * (g + 1), :].rearrange("p h r -> p (h r)"), ID16[:])
                last.then_inc(done, 1)

            def transpose_k(b):
                pe.wait_ge(k_lo, b + 1)
                pe.wait_ge(v_raw, b + 1)
                transpose16(KS, 0, GROUPS, kT_ps)

            def transpose_q(b, par):
                pe.wait_ge(q_lo, b + 1)
                pe.wait_ge(m_zero, b + 1)
                pe.wait_ge(q_terms, 3 * (b + 1))
                transpose16(QS[:, par], 0, GROUPS, qT_ps, HB16)

            def logits(b, u, par):
                if u == 0:
                    pe.wait_ge(kp_dma, 16 * QUAD * (b + 1))
                    pe.wait_ge(qT_sb, b + 1)
                if has(b, 1) or u >= 2:
                    pe.wait_ge(max_done, UNITS * b + u - 1)
                elif u == 0:
                    pe.wait_ge(lora_added, 2)
                mm(LM[u % 2].rearrange("p (a n) -> p a n", a=QUAD), QTA[par][:, u, :], KP[:, par, :, u, :],
                   start=True, stop=True).then_inc(p1_ps, 1)

            def transpose_qm(b, half, par):
                pe.wait_ge(max_done, UNITS * b + 4 * (half + 1))
                if half:
                    if has(b, 1):
                        pe.wait_ge(o_sb, b)
                    else:
                        pe.wait_ge(lora_added, 3)
                else:
                    if live(b + 1):
                        pe.wait_ge(kT_sb, b + 2)
                transpose16(QS[:, par], GROUPS // 2 * half, GROUPS // 2 * (half + 1), qmT_ps, [TB16, OB16][half])

            def logits_t(b, u, par):
                if u % 4 == 0:
                    pe.wait_ge(qmT_sb, 2 * b + u // 4 + 1)
                if has(b, 1) or u >= 2:
                    pe.wait_ge(exp_done, UNITS * b + u - 1)
                elif u == 0:
                    pe.wait_ge(lora_added, 5)
                for j in range(QUAD):
                    last = mm(LT[u % 2][:, P * j:P * (j + 1)], KP[:, par, j, u, :], QTB[:, u, :],
                              start=True, stop=True)
                last.then_inc(p2_ps, 1)

            def attend(b, u, par):
                pe.wait_ge(exp_done, UNITS * b + 2 * (u + 1))
                if u == 0:
                    pe.wait_ge(v_done, b + 1)
                    pe.wait_ge(qmT_sb, 2 * (b + 1))
                for s in range(2):
                    for c in range(4):
                        pair = 4 * u + c
                        last = mm(OBANK[32 * c:32 * (c + 1), P * u:P * (u + 1)],
                                  VA[:, par, pair, 32 * s:32 * (s + 1)],
                                  E[:, 2 * (u % 2) + c // 2, P * (2 * (c % 2) + s):P * (2 * (c % 2) + s + 1)],
                                  start=s == 0, stop=s == 1)
                last.then_inc(av_ps, 1)

            def transpose_o(b):
                pe.wait_ge(o_sb, b + 1)
                if has(b, 2):
                    pe.wait_ge(h2_lo, b - 1)
                elif not has(b, 1):
                    pe.wait_ge(lora_added, 6)
                for r in range(4):
                    last = nc.tensor.transpose(YBANK[:, P * r:P * (r + 1)], OS[:, P * r:P * (r + 1)], ID[:])
                last.then_inc(oT_ps, 1)

            def transpose_a(b):
                pe.wait_ge(attn, b + 1)
                for k in range(DK):
                    last = nc.tensor.transpose(YBANK[:, P * k:P * (k + 1)], AT[:, P * k:P * (k + 1)], ID[:])
                last.then_inc(aT_ps, 1)

            def project_o(b):
                pe.wait_ge(a_lo, b + 1)
                if not has(b, 1):
                    pe.wait_ge(out_lo, 1)
                product(YBANK[:, 0:D],
                        [((ATH[:, P * k:P * (k + 1)], ATL[:, P * k:P * (k + 1)]),
                          (PWH[:, 2, D * k:D * (k + 1)], PWL[:, 2, D * k:D * (k + 1)]))
                         for k in range(DK)]).then_inc(proj_ps, 1)

            def transpose_h2(b):
                pe.wait_ge(h2_ready, b + 1)
                if live(b + 1):
                    pe.wait_ge(x1_done, b + 2)
                for k in range(DK):
                    last = nc.tensor.transpose(YBANK[:, P * k:P * (k + 1)], H2[:, P * k:P * (k + 1)], ID[:])
                last.then_inc(h2T_ps, 1)

            def router_logits(g):
                pe.wait_ge(h2_lo, TG * (g + 1))
                if g:
                    pe.wait_ge(rt_sb, g)
                else:
                    pe.wait_ge(max_done, UNITS * B)
                    pe.wait_ge(out_lo, 2)
                s = slice(GT * g, GT * (g + 1))
                product(RT_BANKS[g][0][0:NE, :], [((RWH[:, k, :], RWL[:, k, :]), (H2H[:, k, s], H2L[:, k, s]))
                                                  for k in range(DK)]).then_inc(rt_ps, 1)

            def router_transpose(g):
                pe.wait_ge(rt_sb, g + 1)
                if g == NG - 1:
                    pe.wait_ge(qmT_sb, 2 * B)
                elif g:
                    pe.wait_ge(rtT_sb, g)
                for k in range(TG):
                    last = nc.tensor.transpose(RT_BANKS[g][1][:, NE * k:NE * (k + 1)], RTS[:, P * k:P * (k + 1)],
                                               ID[0:NE, 0:NE])
                last.then_inc(rtT_ps, 1)

            def step(i, par):
                a, f, b, t, w = i + 2, i + 1, i, i - 1, i - 2
                A, Fr, Bk, Tl, Wl = [live(n) for n in (a, f, b, t, w)]
                start, final = i_is(i, -2) or i_is(i, -1), i_is(i, B - 1)

                def lt(u):
                    if Bk:
                        logits_t(b, u, par)

                def lm(u):
                    if Fr:
                        logits(f, u, 1 - par)

                def av(u):
                    if Bk:
                        attend(b, u, par)

                lt(0)
                if start:
                    transpose_h(a)
                if A:
                    project_kv(a)
                if Tl:
                    transpose_o(t)
                if Bk:
                    transpose_qm(b, 1, par)
                lt(1)
                if i_is(i, -1):
                    project_q(a)
                lm(0)
                if A and not start:
                    transpose_h(a)
                if final:
                    router_logits(0)
                lm(1)
                lt(2)
                if i_is(i, -1):
                    low_rank(2)
                lt(3)
                if A and not i_is(i, -1):
                    project_q(a)
                av(0)
                lm(2)
                if final:
                    router_transpose(0)
                if Tl:
                    transpose_a(t)
                lt(4)
                if final:
                    router_logits(1)
                lt(5)
                av(1)
                lm(3)
                lt(6)
                if A:
                    transpose_k(a)
                if i_is(i, -2):
                    low_rank(0)
                    low_rank(1)
                lt(7)
                if i_is(i, -1):
                    low_rank(3)
                if final:
                    router_transpose(1)
                lm(4)
                if Tl:
                    project_o(t)
                lm(5)
                if i_is(i, -1):
                    low_rank(4)
                av(2)
                if final:
                    router_logits(2)
                if Fr:
                    transpose_qm(f, 0, 1 - par)
                lm(6)
                if Wl:
                    transpose_h2(w)
                av(3)
                lm(7)
                if i_is(i, -1):
                    low_rank(5)
                if A:
                    transpose_q(a, par)
                if final:
                    router_transpose(2)

            pipeline(pe, step)

            def gate_up_columns(n, g, slot, c):
                for part, base, done in ((0, 0, g_ps), (1, 2, u_ps)):
                    if has(n, 1):
                        if part == 0:
                            pe.wait_ge(silu_done, FK * (n - 1) + c + 1)
                        else:
                            pe.wait_ge(m_done, FK * (n - 1) + c + 1)
                    cols = [slice(512 * part + F * k + P * c, 512 * part + F * k + P * (c + 1)) for k in range(DK)]
                    product(PS[:, base + c, :],
                            [((WH[:, slot, cols[k]], WL[:, slot, cols[k]]),
                              (H2H[:, k, GT * g:GT * (g + 1)], H2L[:, k, GT * g:GT * (g + 1)]))
                             for k in range(DK)]).then_inc(done, 1)

            def gate_up(n, g, slot):
                for c in range(FK):
                    gate_up_columns(n, g, slot, c)

            def down(n, slot, par):
                pe.wait_ge(ml_done, FK * (n + 1))
                for k in range(TG):
                    if k % 2 == 0:
                        pe.wait_ge(acc_done, TG * n + k + 2)
                    bank = PS[:, OUT_BANK[par] + k // 2, D * (k % 2):D * (k % 2 + 1)]
                    t = slice(P * k, P * (k + 1))
                    last = product(bank, [((MH[:, par, c, t], ML[:, par, c, t]),
                                           (WH[:, slot, 1024 + D * c:1024 + D * (c + 1)],
                                            WL[:, slot, 1024 + D * c:1024 + D * (c + 1)])) for c in range(FK)])
                    if k % 2:
                        last.then_inc(d_ps, 1)

            def weights(e):
                pe.wait_ge(wl_done, 3 * (e + 1))

            def expert_group(e, s, g, final=False):
                n = NG * (e + s) + g
                nxt = NG * s + g + 1
                if not (final and nxt == 2 * NG):
                    if nxt % NG == 0:
                        weights(e + s + 1)
                    gate_up(n + 1, nxt % NG, (nxt // NG) % 2)
                down(n, s, g % 2)

            def pair_of_experts(e, final=False):
                for s in range(2):
                    for g in range(NG):
                        expert_group(e, s, g, final)

            pe.sem_inc(acc_done, CREDIT)
            transpose_o(B - 1)
            pe.wait_ge(exp_done, UNITS * B)
            pe.wait_ge(rtT_sb, NG - 1)
            weights(0)
            gate_up_columns(0, 0, 0, 0)
            transpose_a(B - 1)
            gate_up_columns(0, 0, 0, 1)
            project_o(B - 1)
            transpose_h2(B - 2)
            gate_up_columns(1, 1, 0, 0)
            transpose_h2(B - 1)
            gate_up_columns(1, 1, 0, 1)
            pe.wait_ge(o_sb, B)
            down(0, 0, 0)
            router_logits(NG - 1)
            router_transpose(NG - 1)
            gate_up(2, 2, 0)
            pe.wait_ge(rtT_sb, NG)
            down(1, 0, 1)
            for n in range(2, 2 * NG):
                expert_group(0, n // NG, n % NG)
            with pe.Fori(2, NE - 2, 2) as e:
                e = pe.snap(e)
                pair_of_experts(e)
            pair_of_experts(NE - 2, final=True)


def kernel(x, ctx_1024, fside_BxSx2_0, g_xattn, g_ffn, L0_xattn_Wq, L0_xattn_Wkv, L0_xattn_Wout, L0_xattn_bout,
           L0_ffn_Wg, L0_ffn_Wu, L0_ffn_Wd, L0_ffn_Ga, L0_ffn_Gb, L0_ffn_Ua, L0_ffn_Ub, L0_ffn_Da, L0_ffn_Db,
           L0_ffn_Wr, L0_ffn_temperature):
    import numpy as np
    import concourse.bacc as bacc
    from concourse import mybir as _mybir
    from concourse.bass_utils import run_bass_kernel_spmd

    def rows(w):
        w = np.asarray(w)
        e, r, n = w.shape
        return w.reshape(e, r // 128, 128, n).transpose(0, 2, 1, 3).reshape(e, 128, -1)

    arrays = {
        "x": np.asarray(x),
        "ctxT": np.asarray(ctx_1024).transpose(2, 0, 1).reshape(ctx_1024.shape[2], -1),
        "pos": np.asarray(fside_BxSx2_0),
        "g_xattn": np.asarray(g_xattn), "g_ffn": np.asarray(g_ffn),
        "Wq": np.asarray(L0_xattn_Wq), "Wkv": np.asarray(L0_xattn_Wkv),
        "Wout": np.asarray(L0_xattn_Wout), "bout": np.asarray(L0_xattn_bout),
        "Wexp": np.concatenate([rows(L0_ffn_Wg), rows(L0_ffn_Wu), rows(L0_ffn_Wd)], axis=2),
        "GaT": np.asarray(L0_ffn_Ga).transpose(0, 2, 1), "Gb": np.asarray(L0_ffn_Gb),
        "UaT": np.asarray(L0_ffn_Ua).transpose(0, 2, 1), "Ub": np.asarray(L0_ffn_Ub),
        "DaT": np.asarray(L0_ffn_Da).transpose(0, 2, 1), "Db": np.asarray(L0_ffn_Db),
        "Wr": np.asarray(L0_ffn_Wr), "temperature": np.asarray(L0_ffn_temperature),
        "ident": np.eye(128, dtype=np.float32),
        "ident16": np.eye(128, dtype=np.float16),
        "lower_tri": np.broadcast_to(np.tril(np.ones((8, 8), np.float32), -1), (128, 8, 8)),
    }
    nc = bacc.Bacc("TRN2", target_bir_lowering=False, num_devices=1)
    arrays = {f"in_{k}": np.ascontiguousarray(a) for k, a in arrays.items()}
    args = [nc.dram_tensor(k, a.shape, _mybir.dt.from_np(a.dtype), kind="ExternalInput").ap()
            for k, a in arrays.items()]
    out = nc.dram_tensor("out", x.shape, _mybir.dt.from_np(np.dtype("float32")), kind="ExternalOutput").ap()
    flamingo_kernel(nc, *args, out)
    r = run_bass_kernel_spmd(nc, [arrays], core_ids=[0])
    return r.results[0]["out"]
```
